# Optimizing a Trainium2 kernel written in Bass

```python
import numpy as np
import jax
import jax.numpy as jnp

def _softmax(x, axis=-1):
    return jax.nn.softmax(x, axis=axis)

def _gelu(x):
    return jax.nn.gelu(x, approximate=True)

def _silu(x):
    return jax.nn.silu(x)

def _sigmoid(x):
    return jax.nn.sigmoid(x)

def _layernorm(x, axis=-1, eps=1e-05):
    m = jnp.mean(x, axis=axis, keepdims=True)
    v = jnp.var(x, axis=axis, keepdims=True)
    return (x - m) / jnp.sqrt(v + eps)

def _scatter_add(tgt, idx, src, axis=0):
    return tgt.at[idx].add(src)

def _segment_sum(src, seg, n):
    return jax.ops.segment_sum(src, seg, n)
kernel_name = 'mk_prb_d4_jaxref_r8_95d81e'

def setup_inputs(seed: int=0):
    np.random.seed(seed)
    _w = jnp.asarray

    def _L0_attn_setup():
        import jax, jax.numpy as jnp
        import numpy as np
        B, N, C = (2, 256, 128)
        H = 16
        D = C // H
        key = jax.random.key(seed)
        ks = jax.random.split(key, 5)
        s = 0.02
        return {'x': jax.random.normal(ks[0], (B, N, C), dtype=jnp.float32), 'qkv_w': jax.random.normal(ks[1], (C, 3 * C), dtype=jnp.float32) * s, 'qkv_b': jax.random.normal(ks[2], (3 * C,), dtype=jnp.float32) * s, 'proj_w': jax.random.normal(ks[3], (C, C), dtype=jnp.float32) * s, 'proj_b': jax.random.normal(ks[4], (C,), dtype=jnp.float32) * s}
    _L0_attn_in = _L0_attn_setup()

    def _L0_ffn_setup():
        import jax, jax.numpy as jnp
        import numpy as np
        NUM_EXPERTS = 64
        TOP_K = 8
        HIDDEN = 128
        INTER = 96
        BATCH, SEQ = (1, 128)
        CAPACITY = 32

        def _moe_forward(hidden_states, gate_w, w_gate, w_up, w_down):
            B, S, H = hidden_states.shape
            x = hidden_states.reshape(-1, H)
            T = x.shape[0]
            logits = (x @ gate_w.T).astype(jnp.float32)
            probs = jax.nn.softmax(logits, axis=-1)
            topk_p, topk_i = jax.lax.top_k(probs, TOP_K)
            topk_p = topk_p / jnp.sum(topk_p, axis=-1, keepdims=True)
            flat_e = topk_i.reshape(-1)
            onehot = jax.nn.one_hot(flat_e, NUM_EXPERTS, dtype=jnp.int32)
            pos_all = jnp.cumsum(onehot, axis=0) - 1
            pos = jnp.take_along_axis(pos_all, flat_e[:, None], axis=1)[:, 0]
            x_rep = jnp.repeat(x, TOP_K, axis=0)
            dispatch = jnp.zeros((NUM_EXPERTS, CAPACITY, H), x.dtype)
            dispatch = dispatch.at[flat_e, pos].set(x_rep, mode='drop')
            g = jax.nn.silu(jnp.einsum('ech,eih->eci', dispatch, w_gate))
            u = jnp.einsum('ech,eih->eci', dispatch, w_up)
            y = jnp.einsum('eci,ehi->ech', g * u, w_down)
            valid = pos < CAPACITY
            y_tok = y[flat_e, jnp.minimum(pos, CAPACITY - 1)]
            w = (topk_p.reshape(-1) * valid.astype(topk_p.dtype)).astype(x.dtype)
            out = (y_tok * w[:, None]).reshape(T, TOP_K, H).sum(axis=1)
            return out.reshape(B, S, H)
        key = jax.random.key(seed)
        k1, k2, k3, k4, k5 = jax.random.split(key, 5)
        scale = 0.02
        return {'hidden_states': jax.random.normal(k1, (BATCH, SEQ, HIDDEN), dtype=jnp.float32), 'gate_w': jax.random.normal(k2, (NUM_EXPERTS, HIDDEN), dtype=jnp.float32) * scale, 'w_gate': jax.random.normal(k3, (NUM_EXPERTS, INTER, HIDDEN), dtype=jnp.float32) * scale, 'w_up': jax.random.normal(k4, (NUM_EXPERTS, INTER, HIDDEN), dtype=jnp.float32) * scale, 'w_down': jax.random.normal(k5, (NUM_EXPERTS, HIDDEN, INTER), dtype=jnp.float32) * scale}
    _L0_ffn_in = _L0_ffn_setup()

    def _L1_attn_setup():
        import jax, jax.numpy as jnp
        import numpy as np
        import math
        D_MODEL = 128
        N_HEADS = 16
        HEAD_DIM = D_MODEL // N_HEADS
        R = HEAD_DIM // 2
        ROPE_BASE = 10000.0
        B, T = (4, 256)

        def _fourier_bias(alpha, beta, t):
            omega = ROPE_BASE ** (-2.0 * jnp.arange(R, dtype=jnp.float32) / HEAD_DIM)
            disp = jnp.arange(-(t - 1), t, dtype=jnp.float32)
            angles = omega[:, None] * disp[None, :]
            vec = jnp.einsum('hr,rk->hk', alpha, jnp.cos(angles)) + jnp.einsum('hr,rk->hk', beta, jnp.sin(angles))
            i = jnp.arange(t)
            idx = i[:, None] - i[None, :] + (t - 1)
            return vec[:, idx]
        key = jax.random.key(seed)
        k1, k2, k3, k4, k5 = jax.random.split(key, 5)
        x = jax.random.normal(k1, (B, T, D_MODEL), dtype=jnp.float32)
        Wqkv = jax.random.normal(k2, (3 * D_MODEL, D_MODEL), dtype=jnp.float32) * (1.0 / math.sqrt(D_MODEL))
        Wout = jax.random.normal(k3, (D_MODEL, D_MODEL), dtype=jnp.float32) * (1.0 / math.sqrt(D_MODEL))
        alpha = jax.random.normal(k4, (N_HEADS, R), dtype=jnp.float32) * 0.01
        beta = jax.random.normal(k5, (N_HEADS, R), dtype=jnp.float32) * 0.01
        return {'x': x, 'Wqkv': Wqkv, 'Wout': Wout, 'alpha': alpha, 'beta': beta}
    _L1_attn_in = _L1_attn_setup()

    def _L1_ffn_setup():
        import jax, jax.numpy as jnp
        import numpy as np
        NUM_EXPERTS = 8
        TOP_K = 2
        D_MODEL = 128
        D_HID = 512
        BATCH, SEQ = (2, 256)
        key = jax.random.key(seed)
        ks = jax.random.split(key, 5)
        s = 0.02
        return {'x': jax.random.normal(ks[0], (BATCH, SEQ, D_MODEL), dtype=jnp.float32), 'Wg': jax.random.normal(ks[1], (D_MODEL, NUM_EXPERTS), dtype=jnp.float32) * s, 'bg': jnp.zeros((NUM_EXPERTS,), dtype=jnp.float32), 'W0': jax.random.normal(ks[2], (NUM_EXPERTS, D_MODEL, D_HID), dtype=jnp.float32) * s, 'b0': jnp.zeros((NUM_EXPERTS, D_HID), dtype=jnp.float32), 'W1': jax.random.normal(ks[3], (NUM_EXPERTS, D_MODEL, D_HID), dtype=jnp.float32) * s, 'b1': jnp.zeros((NUM_EXPERTS, D_HID), dtype=jnp.float32), 'W2': jax.random.normal(ks[4], (NUM_EXPERTS, D_HID, D_MODEL), dtype=jnp.float32) * s, 'b2': jnp.zeros((NUM_EXPERTS, D_MODEL), dtype=jnp.float32)}
    _L1_ffn_in = _L1_ffn_setup()

    def _L2_attn_setup():
        import jax, jax.numpy as jnp
        import numpy as np
        B_SZ, SEQ, D_MODEL, D_STATE = (8, 512, 128, 16)
        key = jax.random.key(seed)
        ks = jax.random.split(key, 4)
        x = jax.random.normal(ks[0], (B_SZ, SEQ, D_MODEL), jnp.float32)

        def lin_w(k, out_f, in_f):
            return jax.random.normal(k, (out_f, in_f), jnp.float32) / np.float32(np.sqrt(in_f))
        in_proj_w = lin_w(ks[1], 2 * D_MODEL, D_MODEL)
        in_proj_b = jnp.zeros((2 * D_MODEL,), jnp.float32)
        x_proj_w = lin_w(ks[2], D_STATE + 2 * D_MODEL, D_MODEL)
        x_proj_b = jnp.zeros((D_STATE + 2 * D_MODEL,), jnp.float32)
        dt_proj_w = jnp.full((D_MODEL, D_STATE), 0.001, jnp.float32)
        dt_proj_b = jnp.full((D_MODEL,), 0.1, jnp.float32)
        A_log = jnp.log(jnp.tile(jnp.linspace(0.5, 2.0, D_STATE, dtype=jnp.float32)[None, :], (D_MODEL, 1)))
        D_param = jnp.full((D_MODEL,), 0.01, jnp.float32)
        out_proj_w = lin_w(ks[3], D_MODEL, D_MODEL)
        out_proj_b = jnp.zeros((D_MODEL,), jnp.float32)
        return {'x': x, 'in_proj_w': in_proj_w, 'in_proj_b': in_proj_b, 'x_proj_w': x_proj_w, 'x_proj_b': x_proj_b, 'dt_proj_w': dt_proj_w, 'dt_proj_b': dt_proj_b, 'A_log': A_log, 'D_param': D_param, 'out_proj_w': out_proj_w, 'out_proj_b': out_proj_b}
    _L2_attn_in = _L2_attn_setup()

    def _L2_ffn_setup():
        import math
        import jax, jax.numpy as jnp
        import numpy as np
        D_MODEL = 128
        D_HIDDEN = 256
        N_EXPERTS = 8
        TOP_K = 2
        CAPACITY_FACTOR = 1.25

        def _moe_forward(x, w_router, w_gate, w_down):
            B, T, D = x.shape
            N = B * T
            xf = x.reshape(N, D)
            logits = xf.astype(jnp.float32) @ w_router.T
            gates = jax.nn.softmax(logits, axis=-1)
            topk_gates, topk_idx = jax.lax.top_k(gates, TOP_K)
            expert_mask = jax.nn.one_hot(topk_idx, N_EXPERTS, dtype=jnp.int32).sum(axis=1)
            capacity = math.ceil(N / N_EXPERTS * CAPACITY_FACTOR)
            position_in_expert = jnp.cumsum(expert_mask, axis=0) - 1
            expert_mask = expert_mask * (position_in_expert < capacity)
            keep = jnp.take_along_axis(expert_mask, topk_idx, axis=1) > 0
            topk_gates = topk_gates * keep
            topk_gates = topk_gates / (topk_gates.sum(axis=-1, keepdims=True) + 1e-06)
            hidden = jax.nn.silu(xf @ w_gate.T)
            combine = (topk_gates[:, :, None] * jax.nn.one_hot(topk_idx, N_EXPERTS, dtype=topk_gates.dtype)).sum(axis=1)
            y = jnp.zeros((N, D), dtype=x.dtype)
            for e in range(N_EXPERTS):
                y = y + combine[:, e:e + 1] * (hidden @ w_down[e].T)
            return y.reshape(B, T, D)
        key = jax.random.key(seed)
        k0, k1, k2, k3 = jax.random.split(key, 4)
        B, T = (2, 256)
        x = jax.random.normal(k0, (B, T, D_MODEL), dtype=jnp.float32)
        w_router = jax.random.normal(k1, (N_EXPERTS, D_MODEL), dtype=jnp.float32) * 0.02
        w_gate = jax.random.normal(k2, (D_HIDDEN, D_MODEL), dtype=jnp.float32) * 0.02
        w_down = jax.random.normal(k3, (N_EXPERTS, D_MODEL, D_HIDDEN), dtype=jnp.float32) * 0.02
        return {'x': x, 'w_router': w_router, 'w_gate': w_gate, 'w_down': w_down}
    _L2_ffn_in = _L2_ffn_setup()

    def _L3_attn_setup():
        import jax, jax.numpy as jnp
        import numpy as np
        import math
        B, T, E, H, DQ, NB, MAXLEN = (4, 128, 128, 16, 64, 10, 128)
        NEG = -1000000000.0

        def _attn_forward(X, Wq, bq, Wk, Wv, Wproj, bproj, Wr, br, b_nd):
            b, t, e = X.shape
            maxlen = b_nd.shape[1]
            nb = b_nd.shape[0]
            h = H
            dq = Wq.shape[1] // h
            Q = (X @ Wq + bq).reshape(b, t, h, dq).transpose(0, 2, 1, 3)
            K = (X @ Wk).reshape(b, t, h, dq).transpose(0, 2, 1, 3)
            V = (X @ Wv).reshape(b, t, h, dq).transpose(0, 2, 1, 3)
            R = (X @ Wr + br).reshape(b, t, h, nb).transpose(0, 2, 1, 3)
            d = jnp.arange(t)[:, None] - jnp.arange(t)[None, :]
            valid = (d >= 0) & (d < maxlen)
            bias = jnp.where(valid, 0.0, NEG).astype(jnp.float32)
            D_ntT = jnp.where(valid[None, :, :], b_nd[:, jnp.clip(d, 0, maxlen - 1)], 0.0)
            extra = jnp.einsum('bhtn,ntp->bhtp', R, D_ntT)
            logits = jnp.einsum('bhtd,bhpd->bhtp', Q, K) / math.sqrt(dq) + bias + extra
            W = jax.nn.softmax(logits, axis=-1)
            A = jnp.einsum('bhtp,bhpd->bhtd', W, V)
            A = A.transpose(0, 2, 1, 3).reshape(b, t, h * dq)
            return A @ Wproj + bproj
        key = jax.random.key(seed)
        k = jax.random.split(key, 10)
        X = jax.random.normal(k[0], (B, T, E), jnp.float32)
        Wq = jax.random.normal(k[1], (E, H * DQ), jnp.float32) * (0.1 / math.sqrt(E))
        bq = jnp.zeros((H * DQ,), jnp.float32)
        Wk = jax.random.normal(k[2], (E, H * DQ), jnp.float32) * (0.2 / math.sqrt(E))
        Wv = jax.random.normal(k[3], (E, H * DQ), jnp.float32) * (1.0 / math.sqrt(E))
        Wproj = jax.random.normal(k[4], (H * DQ, E), jnp.float32) * (1.0 / math.sqrt(H * DQ))
        bproj = jnp.zeros((E,), jnp.float32)
        Wr = jax.random.normal(k[5], (E, H * NB), jnp.float32) * (0.1 / math.sqrt(E))
        br = jnp.zeros((H * NB,), jnp.float32)
        b_nd = jax.random.normal(k[6], (NB, MAXLEN), jnp.float32) * 0.2
        return dict(X=X, Wq=Wq, bq=bq, Wk=Wk, Wv=Wv, Wproj=Wproj, bproj=bproj, Wr=Wr, br=br, b_nd=b_nd)
    _L3_attn_in = _L3_attn_setup()

    def _L3_ffn_setup():
        import jax, jax.numpy as jnp
        import numpy as np
        B, S, D = (2, 256, 128)
        H, E, P, K = (8, 8, 128, 2)
        SCALE = 1.0 / np.sqrt(P)

        def _get_sel_gate(x, w, route_scale):
            logits = jnp.einsum('bsd,ed->bse', x, w).astype(jnp.float32)
            raw = logits.reshape(x.shape[0], x.shape[1], H, E)
            probs = jax.nn.sigmoid(raw)
            vals, idx = jax.lax.top_k(probs, K)
            vals = vals / jnp.clip(vals.sum(-1, keepdims=True), 1e-09)
            vals = vals * route_scale
            gate = (jax.nn.one_hot(idx, E, dtype=vals.dtype) * vals[..., None]).sum(-2)
            return gate
        key = jax.random.key(seed)
        ks = jax.random.split(key, 8)
        std = 1.0 / np.sqrt(D)
        return {'x': jax.random.normal(ks[0], (B, S, D), jnp.float32), 'q_w': jax.random.normal(ks[1], (H * P, D), jnp.float32) * std, 'k_w': jax.random.normal(ks[2], (H * P, D), jnp.float32) * std, 'v_w': jax.random.normal(ks[3], (H * E, D, P), jnp.float32) * std, 'o_w': jax.random.normal(ks[4], (H * E, P, D), jnp.float32) * (1.0 / np.sqrt(H * P)), 'sel_v_w': jax.random.normal(ks[5], (H * E, D), jnp.float32) * std, 'sel_o_w': jax.random.normal(ks[6], (H * E, D), jnp.float32) * std, 'route_scale': jnp.ones((1,), jnp.float32)}
    _L3_ffn_in = _L3_ffn_setup()
    _d = {'L0_attn_x': _L0_attn_in['x'], 'L0_attn_qkv_w': _L0_attn_in['qkv_w'], 'L0_attn_qkv_b': _L0_attn_in['qkv_b'], 'L0_attn_proj_w': _L0_attn_in['proj_w'], 'L0_attn_proj_b': _L0_attn_in['proj_b'], 'L0_ffn_gate_w': _L0_ffn_in['gate_w'], 'L0_ffn_w_gate': _L0_ffn_in['w_gate'], 'L0_ffn_w_up': _L0_ffn_in['w_up'], 'L0_ffn_w_down': _L0_ffn_in['w_down'], 'L1_attn_Wqkv': _L1_attn_in['Wqkv'], 'L1_attn_Wout': _L1_attn_in['Wout'], 'L1_attn_alpha': _L1_attn_in['alpha'], 'L1_attn_beta': _L1_attn_in['beta'], 'L1_ffn_Wg': _L1_ffn_in['Wg'], 'L1_ffn_bg': _L1_ffn_in['bg'], 'L1_ffn_W0': _L1_ffn_in['W0'], 'L1_ffn_b0': _L1_ffn_in['b0'], 'L1_ffn_W1': _L1_ffn_in['W1'], 'L1_ffn_b1': _L1_ffn_in['b1'], 'L1_ffn_W2': _L1_ffn_in['W2'], 'L1_ffn_b2': _L1_ffn_in['b2'], 'L2_attn_in_proj_w': _L2_attn_in['in_proj_w'], 'L2_attn_in_proj_b': _L2_attn_in['in_proj_b'], 'L2_attn_x_proj_w': _L2_attn_in['x_proj_w'], 'L2_attn_x_proj_b': _L2_attn_in['x_proj_b'], 'L2_attn_dt_proj_w': _L2_attn_in['dt_proj_w'], 'L2_attn_dt_proj_b': _L2_attn_in['dt_proj_b'], 'L2_attn_A_log': _L2_attn_in['A_log'], 'L2_attn_D_param': _L2_attn_in['D_param'], 'L2_attn_out_proj_w': _L2_attn_in['out_proj_w'], 'L2_attn_out_proj_b': _L2_attn_in['out_proj_b'], 'L2_ffn_w_router': _L2_ffn_in['w_router'], 'L2_ffn_w_gate': _L2_ffn_in['w_gate'], 'L2_ffn_w_down': _L2_ffn_in['w_down'], 'L3_attn_Wq': _L3_attn_in['Wq'], 'L3_attn_bq': _L3_attn_in['bq'], 'L3_attn_Wk': _L3_attn_in['Wk'], 'L3_attn_Wv': _L3_attn_in['Wv'], 'L3_attn_Wproj': _L3_attn_in['Wproj'], 'L3_attn_bproj': _L3_attn_in['bproj'], 'L3_attn_Wr': _L3_attn_in['Wr'], 'L3_attn_br': _L3_attn_in['br'], 'L3_attn_b_nd': _L3_attn_in['b_nd'], 'L3_ffn_q_w': _L3_ffn_in['q_w'], 'L3_ffn_k_w': _L3_ffn_in['k_w'], 'L3_ffn_v_w': _L3_ffn_in['v_w'], 'L3_ffn_o_w': _L3_ffn_in['o_w'], 'L3_ffn_sel_v_w': _L3_ffn_in['sel_v_w'], 'L3_ffn_sel_o_w': _L3_ffn_in['sel_o_w'], 'L3_ffn_route_scale': _L3_ffn_in['route_scale']}
    _x0 = _d['L0_attn_x']
    _d['L0_attn_x'] = jax.random.normal(jax.random.fold_in(jax.random.key(seed), 1), (4, 512, 128), dtype=_x0.dtype)
    del _x0
    return _d

def reference(L0_attn_x, L0_attn_qkv_w, L0_attn_qkv_b, L0_attn_proj_w, L0_attn_proj_b, L0_ffn_gate_w, L0_ffn_w_gate, L0_ffn_w_up, L0_ffn_w_down, L1_attn_Wqkv, L1_attn_Wout, L1_attn_alpha, L1_attn_beta, L1_ffn_Wg, L1_ffn_bg, L1_ffn_W0, L1_ffn_b0, L1_ffn_W1, L1_ffn_b1, L1_ffn_W2, L1_ffn_b2, L2_attn_in_proj_w, L2_attn_in_proj_b, L2_attn_x_proj_w, L2_attn_x_proj_b, L2_attn_dt_proj_w, L2_attn_dt_proj_b, L2_attn_A_log, L2_attn_D_param, L2_attn_out_proj_w, L2_attn_out_proj_b, L2_ffn_w_router, L2_ffn_w_gate, L2_ffn_w_down, L3_attn_Wq, L3_attn_bq, L3_attn_Wk, L3_attn_Wv, L3_attn_Wproj, L3_attn_bproj, L3_attn_Wr, L3_attn_br, L3_attn_b_nd, L3_ffn_q_w, L3_ffn_k_w, L3_ffn_v_w, L3_ffn_o_w, L3_ffn_sel_v_w, L3_ffn_sel_o_w, L3_ffn_route_scale):

    def _L0_attn_ref(x, qkv_w, qkv_b, proj_w, proj_b):
        import jax, jax.numpy as jnp
        import numpy as np
        B, N, C = (2, 256, 128)
        H = 16
        D = C // H
        b, n, c = x.shape
        scale = (c // H) ** (-0.5)
        qkv = x @ qkv_w + qkv_b
        qkv = qkv.reshape(b, n, 3, H, D)
        q, k, v = jnp.moveaxis(qkv, 2, 0)
        attn = jnp.einsum('bnhd,bmhd->bhnm', q, k) * scale
        attn = jax.nn.softmax(attn, axis=-1)
        out = jnp.einsum('bhnm,bmhd->bnhd', attn, v).reshape(b, n, c)
        out = out @ proj_w + proj_b
        return out

    def _L0_ffn_ref(hidden_states, gate_w, w_gate, w_up, w_down):
        import jax, jax.numpy as jnp
        import numpy as np
        NUM_EXPERTS = 64
        TOP_K = 8
        HIDDEN = 128
        INTER = 96
        BATCH, SEQ = (1, 128)
        CAPACITY = 32

        def _moe_forward(hidden_states, gate_w, w_gate, w_up, w_down):
            B, S, H = hidden_states.shape
            x = hidden_states.reshape(-1, H)
            T = x.shape[0]
            logits = (x @ gate_w.T).astype(jnp.float32)
            probs = jax.nn.softmax(logits, axis=-1)
            topk_p, topk_i = jax.lax.top_k(probs, TOP_K)
            topk_p = topk_p / jnp.sum(topk_p, axis=-1, keepdims=True)
            flat_e = topk_i.reshape(-1)
            onehot = jax.nn.one_hot(flat_e, NUM_EXPERTS, dtype=jnp.int32)
            pos_all = jnp.cumsum(onehot, axis=0) - 1
            pos = jnp.take_along_axis(pos_all, flat_e[:, None], axis=1)[:, 0]
            x_rep = jnp.repeat(x, TOP_K, axis=0)
            dispatch = jnp.zeros((NUM_EXPERTS, CAPACITY, H), x.dtype)
            dispatch = dispatch.at[flat_e, pos].set(x_rep, mode='drop')
            g = jax.nn.silu(jnp.einsum('ech,eih->eci', dispatch, w_gate))
            u = jnp.einsum('ech,eih->eci', dispatch, w_up)
            y = jnp.einsum('eci,ehi->ech', g * u, w_down)
            valid = pos < CAPACITY
            y_tok = y[flat_e, jnp.minimum(pos, CAPACITY - 1)]
            w = (topk_p.reshape(-1) * valid.astype(topk_p.dtype)).astype(x.dtype)
            out = (y_tok * w[:, None]).reshape(T, TOP_K, H).sum(axis=1)
            return out.reshape(B, S, H)
        return _moe_forward(hidden_states, gate_w, w_gate, w_up, w_down)

    def _L1_attn_ref(x, Wqkv, Wout, alpha, beta):
        import jax, jax.numpy as jnp
        import numpy as np
        import math
        D_MODEL = 128
        N_HEADS = 16
        HEAD_DIM = D_MODEL // N_HEADS
        R = HEAD_DIM // 2
        ROPE_BASE = 10000.0
        B, T = (4, 256)

        def _fourier_bias(alpha, beta, t):
            omega = ROPE_BASE ** (-2.0 * jnp.arange(R, dtype=jnp.float32) / HEAD_DIM)
            disp = jnp.arange(-(t - 1), t, dtype=jnp.float32)
            angles = omega[:, None] * disp[None, :]
            vec = jnp.einsum('hr,rk->hk', alpha, jnp.cos(angles)) + jnp.einsum('hr,rk->hk', beta, jnp.sin(angles))
            i = jnp.arange(t)
            idx = i[:, None] - i[None, :] + (t - 1)
            return vec[:, idx]
        b, t, d = x.shape
        qkv = x @ Wqkv.T
        q, k, v = jnp.split(qkv, 3, axis=-1)

        def heads(a):
            return a.reshape(b, t, N_HEADS, HEAD_DIM).transpose(0, 2, 1, 3)
        q, k, v = (heads(q), heads(k), heads(v))
        scale = 1.0 / math.sqrt(HEAD_DIM)
        logits = jnp.einsum('bhqd,bhkd->bhqk', q, k) * scale
        logits = logits + _fourier_bias(alpha, beta, t)[None]
        causal = jnp.tril(jnp.ones((t, t), dtype=bool))
        logits = jnp.where(causal[None, None], logits, -jnp.inf)
        attn = jax.nn.softmax(logits, axis=-1)
        out = jnp.einsum('bhqk,bhkd->bhqd', attn, v)
        out = out.transpose(0, 2, 1, 3).reshape(b, t, d)
        return out @ Wout.T

    def _L1_ffn_ref(x, Wg, bg, W0, b0, W1, b1, W2, b2):
        import jax, jax.numpy as jnp
        import numpy as np
        NUM_EXPERTS = 8
        TOP_K = 2
        D_MODEL = 128
        D_HID = 512
        BATCH, SEQ = (2, 256)
        n, s, d = x.shape
        gate_logits = x @ Wg + bg
        top_vals, top_idx = jax.lax.top_k(gate_logits, TOP_K)
        w = jax.nn.softmax(top_vals, axis=-1)
        combine = jnp.sum(jax.nn.one_hot(top_idx, NUM_EXPERTS, dtype=x.dtype) * w[..., None], axis=-2)
        xf = x.reshape(n * s, d)
        h = jnp.einsum('td,edh->eth', xf, W0) + b0[:, None, :]
        g = jax.nn.silu(jnp.einsum('td,edh->eth', xf, W1) + b1[:, None, :])
        y = jnp.einsum('eth,ehd->etd', h * g, W2) + b2[:, None, :]
        out = jnp.einsum('te,etd->td', combine.reshape(n * s, NUM_EXPERTS), y)
        return out.reshape(n, s, d)

    def _L2_attn_ref(x, in_proj_w, in_proj_b, x_proj_w, x_proj_b, dt_proj_w, dt_proj_b, A_log, D_param, out_proj_w, out_proj_b):
        import jax, jax.numpy as jnp
        import numpy as np
        B_SZ, SEQ, D_MODEL, D_STATE = (8, 512, 128, 16)
        batch, seq, d_model = x.shape
        d_state = A_log.shape[1]
        x_and_res = x @ in_proj_w.T + in_proj_b
        x_in = jax.nn.silu(x_and_res[..., :d_model])
        res = x_and_res[..., d_model:]
        ssm = x_in @ x_proj_w.T + x_proj_b
        dlt_raw = ssm[..., :d_state]
        Bm = ssm[..., d_state:d_state + d_model]
        Cm = ssm[..., d_state + d_model:]
        delta = jnp.clip(jax.nn.softplus(dlt_raw @ dt_proj_w.T + dt_proj_b), 1e-05, 0.1)
        A = jnp.clip(-jnp.exp(A_log), -5.0, -0.01)

        def step(h, inp):
            dt, Bt, Ct, xt = inp
            dA = jnp.clip(jnp.exp(A * dt[..., None]), 1e-06, 1.0)
            h = jnp.clip(h * dA + (Bt * dt * xt)[..., None], -100.0, 100.0)
            y = jnp.sum(h, axis=-1) * Ct + D_param * xt
            return (h, y)
        tm = lambda a: jnp.swapaxes(a, 0, 1)
        h0 = jnp.zeros((batch, d_model, d_state), x.dtype)
        _, ys = jax.lax.scan(step, h0, (tm(delta), tm(Bm), tm(Cm), tm(x_in)))
        y = jnp.swapaxes(ys, 0, 1)
        return y * jax.nn.silu(res) @ out_proj_w.T + out_proj_b

    def _L2_ffn_ref(x, w_router, w_gate, w_down):
        import math
        import jax, jax.numpy as jnp
        import numpy as np
        D_MODEL = 128
        D_HIDDEN = 256
        N_EXPERTS = 8
        TOP_K = 2
        CAPACITY_FACTOR = 1.25

        def _moe_forward(x, w_router, w_gate, w_down):
            B, T, D = x.shape
            N = B * T
            xf = x.reshape(N, D)
            logits = xf.astype(jnp.float32) @ w_router.T
            gates = jax.nn.softmax(logits, axis=-1)
            topk_gates, topk_idx = jax.lax.top_k(gates, TOP_K)
            expert_mask = jax.nn.one_hot(topk_idx, N_EXPERTS, dtype=jnp.int32).sum(axis=1)
            capacity = math.ceil(N / N_EXPERTS * CAPACITY_FACTOR)
            position_in_expert = jnp.cumsum(expert_mask, axis=0) - 1
            expert_mask = expert_mask * (position_in_expert < capacity)
            keep = jnp.take_along_axis(expert_mask, topk_idx, axis=1) > 0
            topk_gates = topk_gates * keep
            topk_gates = topk_gates / (topk_gates.sum(axis=-1, keepdims=True) + 1e-06)
            hidden = jax.nn.silu(xf @ w_gate.T)
            combine = (topk_gates[:, :, None] * jax.nn.one_hot(topk_idx, N_EXPERTS, dtype=topk_gates.dtype)).sum(axis=1)
            y = jnp.zeros((N, D), dtype=x.dtype)
            for e in range(N_EXPERTS):
                y = y + combine[:, e:e + 1] * (hidden @ w_down[e].T)
            return y.reshape(B, T, D)
        return _moe_forward(x, w_router, w_gate, w_down)

    def _L3_attn_ref(X, Wq, bq, Wk, Wv, Wproj, bproj, Wr, br, b_nd):
        import jax, jax.numpy as jnp
        import numpy as np
        import math
        B, T, E, H, DQ, NB, MAXLEN = (4, 128, 128, 16, 64, 10, 128)
        NEG = -1000000000.0

        def _attn_forward(X, Wq, bq, Wk, Wv, Wproj, bproj, Wr, br, b_nd):
            b, t, e = X.shape
            maxlen = b_nd.shape[1]
            nb = b_nd.shape[0]
            h = H
            dq = Wq.shape[1] // h
            Q = (X @ Wq + bq).reshape(b, t, h, dq).transpose(0, 2, 1, 3)
            K = (X @ Wk).reshape(b, t, h, dq).transpose(0, 2, 1, 3)
            V = (X @ Wv).reshape(b, t, h, dq).transpose(0, 2, 1, 3)
            R = (X @ Wr + br).reshape(b, t, h, nb).transpose(0, 2, 1, 3)
            d = jnp.arange(t)[:, None] - jnp.arange(t)[None, :]
            valid = (d >= 0) & (d < maxlen)
            bias = jnp.where(valid, 0.0, NEG).astype(jnp.float32)
            D_ntT = jnp.where(valid[None, :, :], b_nd[:, jnp.clip(d, 0, maxlen - 1)], 0.0)
            extra = jnp.einsum('bhtn,ntp->bhtp', R, D_ntT)
            logits = jnp.einsum('bhtd,bhpd->bhtp', Q, K) / math.sqrt(dq) + bias + extra
            W = jax.nn.softmax(logits, axis=-1)
            A = jnp.einsum('bhtp,bhpd->bhtd', W, V)
            A = A.transpose(0, 2, 1, 3).reshape(b, t, h * dq)
            return A @ Wproj + bproj
        return _attn_forward(X, Wq, bq, Wk, Wv, Wproj, bproj, Wr, br, b_nd)

    def _L3_ffn_ref(x, q_w, k_w, v_w, o_w, sel_v_w, sel_o_w, route_scale):
        import jax, jax.numpy as jnp
        import numpy as np
        B, S, D = (2, 256, 128)
        H, E, P, K = (8, 8, 128, 2)
        SCALE = 1.0 / np.sqrt(P)

        def _get_sel_gate(x, w, route_scale):
            logits = jnp.einsum('bsd,ed->bse', x, w).astype(jnp.float32)
            raw = logits.reshape(x.shape[0], x.shape[1], H, E)
            probs = jax.nn.sigmoid(raw)
            vals, idx = jax.lax.top_k(probs, K)
            vals = vals / jnp.clip(vals.sum(-1, keepdims=True), 1e-09)
            vals = vals * route_scale
            gate = (jax.nn.one_hot(idx, E, dtype=vals.dtype) * vals[..., None]).sum(-2)
            return gate
        rs = route_scale[0]
        gate_v = _get_sel_gate(x, sel_v_w, rs)
        gate_o = _get_sel_gate(x, sel_o_w, rs)
        q = jnp.einsum('bsd,hpd->bhsp', x, q_w.reshape(H, P, D))
        k = jnp.einsum('bsd,hpd->bhsp', x, k_w.reshape(H, P, D))
        xv = jnp.einsum('bsd,hedp->bshep', x, v_w.reshape(H, E, D, P))
        v = jnp.einsum('bshep,bshe->bhsp', xv, gate_v)
        att = jax.nn.softmax(jnp.einsum('bhqp,bhkp->bhqk', q, k) * SCALE, axis=-1)
        ctx = jnp.einsum('bhqk,bhkp->bqhp', att, v)
        weighted = ctx[:, :, :, None, :] * gate_o[..., None]
        out = jnp.einsum('bshep,hepd->bsd', weighted, o_w.reshape(H, E, P, D))
        return out
    x = L0_attn_x
    xn = _layernorm(x, axis=-1)
    x = x + _L0_attn_ref(xn, L0_attn_qkv_w, L0_attn_qkv_b, L0_attn_proj_w, L0_attn_proj_b) + _L0_ffn_ref(xn, L0_ffn_gate_w, L0_ffn_w_gate, L0_ffn_w_up, L0_ffn_w_down)
    xn = _layernorm(x, axis=-1)
    x = x + _L1_attn_ref(xn, L1_attn_Wqkv, L1_attn_Wout, L1_attn_alpha, L1_attn_beta) + _L1_ffn_ref(xn, L1_ffn_Wg, L1_ffn_bg, L1_ffn_W0, L1_ffn_b0, L1_ffn_W1, L1_ffn_b1, L1_ffn_W2, L1_ffn_b2)
    xn = _layernorm(x, axis=-1)
    x = x + _L2_attn_ref(xn, L2_attn_in_proj_w, L2_attn_in_proj_b, L2_attn_x_proj_w, L2_attn_x_proj_b, L2_attn_dt_proj_w, L2_attn_dt_proj_b, L2_attn_A_log, L2_attn_D_param, L2_attn_out_proj_w, L2_attn_out_proj_b) + _L2_ffn_ref(xn, L2_ffn_w_router, L2_ffn_w_gate, L2_ffn_w_down)
    xn = _layernorm(x, axis=-1)
    x = x + _L3_attn_ref(xn, L3_attn_Wq, L3_attn_bq, L3_attn_Wk, L3_attn_Wv, L3_attn_Wproj, L3_attn_bproj, L3_attn_Wr, L3_attn_br, L3_attn_b_nd) + _L3_ffn_ref(xn, L3_ffn_q_w, L3_ffn_k_w, L3_ffn_v_w, L3_ffn_o_w, L3_ffn_sel_v_w, L3_ffn_sel_o_w, L3_ffn_route_scale)
    return x

_drawn_inputs = setup_inputs


def setup_inputs(seed=0):
    import zlib

    import numpy as np

    out = dict(_drawn_inputs(seed))
    spreads = {'L1_ffn_bg': (0.0, 0.1),
     'L1_ffn_b0': (0.0, 0.8),
     'L1_ffn_b1': (0.0, 0.8),
     'L1_ffn_b2': (0.0, 0.1),
     'L2_attn_in_proj_b': (0.0, 0.1),
     'L2_attn_x_proj_b': (0.0, 0.1),
     'L2_attn_dt_proj_w': (0.0010000000474974513, 0.2),
     'L2_attn_dt_proj_b': (0.10000000149011612, 0.2),
     'L2_attn_D_param': (0.009999999776482582, 0.6),
     'L2_attn_out_proj_b': (0.0, 0.1),
     'L3_attn_bq': (0.0, 0.8),
     'L3_attn_bproj': (0.0, 0.338),
     'L3_attn_br': (0.0, 0.8)}
    factors = {'L0_attn_qkv_w': 7.908,
     'L0_attn_qkv_b': 4.964,
     'L0_attn_proj_w': 4.061,
     'L0_ffn_gate_w': 8.0,
     'L0_ffn_w_gate': 8.0,
     'L0_ffn_w_up': 8.0,
     'L0_ffn_w_down': 8.0,
     'L1_attn_alpha': 28.006,
     'L1_attn_beta': 30.9,
     'L1_ffn_W0': 4.68,
     'L1_ffn_W1': 4.791,
     'L1_ffn_W2': 4.393,
     'L2_attn_A_log': 200.0,
     'L2_ffn_w_router': 4.003,
     'L2_ffn_w_gate': 3.704,
     'L2_ffn_w_down': 3.65,
     'L3_attn_Wq': 8.0,
     'L3_attn_Wk': 8.0,
     'L3_attn_Wr': 8.0,
     'L3_attn_b_nd': 8.0,
     'L3_ffn_q_w': 4.362,
     'L3_ffn_k_w': 4.374,
     'L3_ffn_sel_v_w': 3.424,
     'L3_ffn_sel_o_w': 2.694}
    for name, (base, spread) in spreads.items():
        noise = np.random.default_rng([zlib.crc32(name.encode()), seed]).standard_normal(out[name].shape)
        drawn = base * np.exp(spread * noise) if base else spread * noise
        out[name] = jnp.asarray(drawn.astype(out[name].dtype))
    for name, factor in factors.items():
        out[name] = (out[name] * factor).astype(out[name].dtype)
    return out
```

```python
from contextlib import ExitStack

import numpy as np

import concourse.bass as bass
from concourse import mybir

F32 = mybir.dt.float32
BF16 = mybir.dt.bfloat16
I32 = mybir.dt.int32
ALU = mybir.AluOpType
ACT = mybir.ActivationFunctionType
AX = mybir.AxisListType

P = 128
B, T = 4, 512
N = B * T
NT = N // P
QT = T // P
EPS = 1e-5
BIG = 1.0e30


def bc(ap, shape):
    return ap.broadcast_to(shape)


class Phase:

    counted = []

    def __init__(self, nc, ctx, tag):
        self.nc, self.ctx, self.tag = nc, ctx, tag

    def sem(self, name):
        s = self.nc.alloc_semaphore(f"{self.tag}_{name}")
        self.counted.append(s)
        return s

    @classmethod
    def retire(cls, nc):
        nc.clear_and_free_semaphores(cls.counted)
        cls.counted = []
        nc.all_engine_barrier()

    def sb(self, name, shape, dtype=F32):
        return self.ctx.enter_context(self.nc.sbuf_tensor(f"{self.tag}_{name}", shape, dtype))

    def banks(self, name, n):
        return [self.ctx.enter_context(self.nc.psum_tensor(f"{self.tag}_{name}{i}", [P, 512], F32)) for i in range(n)]


def layer_norm(nc, k, tag):
    with ExitStack() as ctx:
        ph = Phase(nc, ctx, tag)
        stats = ph.sb("stats", [P, NT, 6])
        mv = ph.sb("mv", [P, NT, 2])
        ve = ph.sb("ve", [P, NT])
        std = ph.sb("std", [P, NT])
        y = ph.sb("y", [P, NT])
        t = ph.sb("t", [P, NT])
        tps = ph.banks("tps", 4)
        chain, var_ready, std_ready, xn_ready, turned = (ph.sem(s) for s in (
            "chain", "var_ready", "std_ready", "xn_ready", "turned"))
        copied = ph.sem("copied")
        block = ctx.enter_context(nc.Block())

        @block.vector
        def _(v):
            done = [0]

            def link(ins):
                done[0] += 1
                ins.then_inc(chain, 1)

            def settle():
                v.wait_ge(chain, done[0])

            for i in range(NT):
                link(v.bn_stats(stats[:, i, :], k.x[:, i, :]))
            settle()
            for i in range(NT):
                link(v.bn_aggr(mv[:, i, :], stats[:, i, :]))
            settle()
            v.tensor_scalar(ve[:, :], mv[:, :, 1], EPS, None, ALU.add).then_inc(var_ready, 1)
            v.wait_ge(std_ready, 1)
            link(v.reciprocal(y[:, :], std[:, :]))
            settle()
            for _ in range(2):
                link(v.tensor_tensor(t[:, :], y[:, :], y[:, :], ALU.mult))
                settle()
                link(v.tensor_tensor(t[:, :], t[:, :], ve[:, :], ALU.mult))
                settle()
                link(v.tensor_scalar(t[:, :], t[:, :], -0.5, 1.5, ALU.mult, ALU.add))
                settle()
                link(v.tensor_tensor(y[:, :], y[:, :], t[:, :], ALU.mult))
                settle()
            for i in range(NT):
                v.tensor_scalar(k.xn[:, i, :], k.x[:, i, :], mv[:, i, 0:1], y[:, i:i + 1],
                                ALU.subtract, ALU.mult).then_inc(xn_ready, 1)

        @block.tensor
        def _(pe):
            for i in range(NT):
                pe.wait_ge(xn_ready, i + 1)
                pe.transpose(tps[i // 4][:, (i % 4) * P:(i % 4 + 1) * P], k.xn[:, i, :],
                             k.ident[:, :]).then_inc(turned, 1)

        @block.scalar
        def _(act):
            act.wait_ge(var_ready, 1)
            act.activation(std[:, :], ve[:, :], ACT.Sqrt).then_inc(std_ready, 1)
            for j in range(4):
                act.wait_ge(turned, 4 * j + 4)
                act.copy(k.xnT[:, j * 512:(j + 1) * 512], tps[j][:, :]).then_inc(copied, 1)
            act.wait_ge(copied, 4)


def small_heads(nc, k, tag, w_q, w_k, w_v, w_out, q_bias, k_bias, row_scale, v_bias, out_bias,
                fourier, mask):
    H, G, DH = 16, 4, 8
    UNITS = H * QT
    K_ROWS = 16 if fourier else 8
    with ExitStack() as ctx:
        ph = Phase(nc, ctx, tag)
        wq = ph.sb("wq", [P, G, P])
        wk = ph.sb("wk", [P, G, P])
        wv = ph.sb("wv", [P, P])
        wo = ph.sb("wo", [P, P])
        qb = ph.sb("qb", [P, G])
        kb = ph.sb("kb", [P, G])
        rs = ph.sb("rs", [P, 1])
        vb = ph.sb("vb", [1, P])
        ob = ph.sb("ob", [1, P])
        xb = ph.sb("xb", [P, T])
        qt_ = ph.sb("qT", [P, G, T])
        kt_ = ph.sb("kT", [P, G, T])
        vp = ph.sb("vpad", [P, QT, H, 32])
        nmax = ph.sb("nmax", [P, 4])
        prob = ph.sb("prob", [P, 2, T])
        pt = ph.sb("pT", [P, 2, 4, QT, T])
        rsum = ph.sb("rsum", [P, QT, H])
        rinv = ph.sb("rinv", [P, QT, H])
        og = ph.sb("og", [P, T])
        o = ph.sb("o", [P, QT, P])
        oT = ph.sb("oT", [P, T])
        if fourier:
            fa = ph.sb("fa", [12, G, P])
            fk = ph.sb("fk", [12, G, P])
            trig = ph.sb("trig", [12, T])
        s_ps, t_ps, o_ps, m_ps = (ph.banks(s, 2) for s in ("s", "t", "o", "m"))
        loaded, xb_ready, v_set, m_full0, m_full1, m_free0, m_free1 = (ph.sem(s) for s in (
            "loaded", "xb_ready", "v_set", "m_full0", "m_full1", "m_free0", "m_free1"))
        s_done, max_done, exp_done, t_done, pt_copied, pv_done, og_free, rinv_ready = (ph.sem(s) for s in (
            "s_done", "max_done", "exp_done", "t_done", "pt_copied", "pv_done", "og_free", "rinv_ready"))
        x_added = ph.sem("x_added")
        m_full, m_free = (m_full0, m_full1), (m_free0, m_free1)
        M_Q, M_K, M_V, M_O, M_OT, M_Y = 0, 1, 8, 9, 13, 14
        PER = (8, 7)
        block = ctx.enter_context(nc.Block())
        n_loads = 9 + (3 if fourier else 0)

        def nk(qt):
            return (qt + 1) * P if mask is not None else T

        @block.sync
        def _(sp):
            pairs = [(wq[:, :, :], w_q), (wk[:, :, :], w_k), (wv[:, :], w_v), (wo[:, :], w_out),
                     (qb[:, :], q_bias), (kb[:, :], k_bias), (rs[:, :], row_scale), (vb[:, :], v_bias),
                     (ob[:, :], out_bias)]
            if fourier:
                pairs += [(fa[:, :, :], fourier[0]), (fk[:, :, :], fourier[1]), (trig[:, :], fourier[2])]
            for dst, src in pairs:
                sp.dma_start(dst, src).then_inc(loaded, 16)

        @block.tensor
        def _(pe):
            pe.wait_ge(loaded, 16 * n_loads)
            with pe.Fori(0, B) as b:
                def m_open(m):
                    pe.wait_ge(m_free[m % 2], b * PER[m % 2] + m // 2 + 1)
                    return m_ps[m % 2]

                pe.wait_ge(xb_ready, b + 1)
                for g in range(G):
                    for m, w, f in ((M_Q + 2 * g, wq, 0), (M_K + 2 * g, wk, 1)):
                        ps = m_open(m)
                        last = pe.matmul(ps[:, :], w[:, g, :], xb[:, :], start=True, stop=not fourier)
                        if fourier:
                            last = pe.matmul(ps[:, :], (fa, fk)[f][:, g, :], trig[:, :], start=False, stop=True)
                        last.then_inc(m_full[m % 2], 1)
                ps = m_open(M_V)
                for i in range(QT):
                    pe.matmul(ps[:, i * P:(i + 1) * P], xb[:, i * P:(i + 1) * P], wv[:, :], start=True, stop=False)
                    last = pe.matmul(ps[:, i * P:(i + 1) * P], k.ones[0:1, :], vb[:, :], start=False, stop=True)
                last.then_inc(m_full[M_V % 2], 1)
                pe.wait_ge(m_free[M_V % 2], b * PER[M_V % 2] + M_V // 2 + 2)
                pe.wait_ge(m_free[1], b * PER[1] + 4 + 1)

                def scores(u):
                    g, j, qt = u // 16, u // 4 % 4, u % 4
                    pe.wait_ge(exp_done, b * UNITS + u + 1)
                    r = slice(32 * j, 32 * j + K_ROWS)
                    n = nk(qt)
                    last = pe.matmul(s_ps[u % 2][:, 0:n], qt_[r, g, qt * P:(qt + 1) * P], kt_[r, g, 0:n],
                                     start=True, stop=mask is None)
                    if mask is not None:
                        last = pe.matmul(s_ps[u % 2][:, n - P:n], k.ident_bf[:, :], mask[:, :],
                                         start=False, stop=True)
                    last.then_inc(s_done, 1)

                def turn(u):
                    qt = u % 4
                    pe.wait_ge(exp_done, b * UNITS + u + 3)
                    pe.wait_ge(pt_copied, b * UNITS + u + 1)
                    for kt in range(nk(qt) // P):
                        last = pe.transpose(t_ps[u % 2][:, kt * P:(kt + 1) * P],
                                            prob[:, u % 2, kt * P:(kt + 1) * P], k.ident[:, :])
                    last.then_inc(t_done, 1)

                def values(g):
                    pe.wait_ge(pt_copied, b * UNITS + 16 * (g + 1) + 2)
                    pe.wait_ge(og_free, b * G + g + 1)
                    for kt in range(QT):
                        q0 = kt * P if mask is not None else 0
                        for j in range(4):
                            last = pe.matmul(o_ps[g % 2][32 * j:32 * j + 32, q0:T], vp[:, kt, 4 * g + j, :],
                                             pt[:, g % 2, j, kt, q0:T], start=(kt == 0), stop=(kt == QT - 1))
                    last.then_inc(pv_done, 1)

                def turn_o(g):
                    pe.wait_ge(og_free, b * G + g + 3)
                    ps = m_open(M_O + g)
                    for qt in range(QT):
                        last = pe.transpose(ps[:, qt * P:(qt + 1) * P], og[:, qt * P:(qt + 1) * P], k.ident[:, :])
                    last.then_inc(m_full[(M_O + g) % 2], 1)

                for u in range(UNITS + 2):
                    if u < UNITS:
                        scores(u)
                    if u >= 1 and u - 1 < UNITS:
                        turn(u - 1)
                    if u >= 18 and u % 16 == 2:
                        values(u // 16 - 1)
                    if u >= 24 and u % 16 == 8:
                        turn_o(u // 16 - 1)
                values(G - 1) if (UNITS + 1) % 16 < 2 else None
                turn_o(G - 1)
                pe.wait_ge(m_free[(M_O + 3) % 2], b * PER[(M_O + 3) % 2] + (M_O + 3) // 2 + 2)
                ps = m_open(M_OT)
                for qt in range(QT):
                    last = pe.transpose(ps[:, qt * P:(qt + 1) * P], o[:, qt, :], k.ident[:, :])
                last.then_inc(m_full[M_OT % 2], 1)
                pe.wait_ge(m_free[M_OT % 2], b * PER[M_OT % 2] + M_OT // 2 + 2)
                ps = m_open(M_Y)
                for qt in range(QT):
                    pe.matmul(ps[:, qt * P:(qt + 1) * P], oT[:, qt * P:(qt + 1) * P], wo[:, :], start=True, stop=False)
                    last = pe.matmul(ps[:, qt * P:(qt + 1) * P], k.ones[0:1, :], ob[:, :], start=False, stop=True)
                last.then_inc(m_full[M_Y % 2], 1)

        @block.scalar
        def _(act):
            act.sem_inc(exp_done, 2)
            with act.Fori(0, B) as b:
                for u in range(UNITS):
                    g, j, qt = u // 16, u // 4 % 4, u % 4
                    n = nk(qt)
                    act.wait_ge(max_done, b * UNITS + u + 1)
                    act.wait_ge(t_done, b * UNITS + u + 1)
                    act.activation(prob[:, u % 2, 0:n], s_ps[u % 2][:, 0:n], ACT.Exp, bias=nmax[:, u % 4:u % 4 + 1],
                                   accum_out=rsum[:, qt, 4 * g + j:4 * g + j + 1]).then_inc(exp_done, 1)

        @block.vector
        def _(v):
            v.sem_inc(t_done, 2)
            v.sem_inc(pt_copied, 2)
            v.sem_inc(pv_done, 2)
            v.sem_inc(og_free, 2)
            v.sem_inc(m_free0, 1)
            v.sem_inc(m_free1, 1)
            v.memset(vp[:, :, :, :], 0.0).then_inc(v_set, 1)
            v.wait_ge(v_set, 1)
            v.memset(vp[:, :, :, DH:DH + 1], 1.0).then_inc(v_set, 1)
            v.wait_ge(v_set, 2)
            v.wait_ge(loaded, 16 * n_loads)
            with v.Fori(0, B) as b:
                def m_wait(m):
                    v.wait_ge(m_full[m % 2], b * PER[m % 2] + m // 2 + 1)
                    return m_ps[m % 2]

                v.tensor_copy(xb[:, :], k.xnT[:, bass.ds(b * T, T)]).then_inc(xb_ready, 1)
                for g in range(G):
                    ps = m_wait(M_Q + 2 * g)
                    v.tensor_scalar(qt_[:, g, :], ps[:, :], qb[:, g:g + 1], rs[:, 0:1],
                                    ALU.add, ALU.mult).then_inc(m_free[0], 1)
                    ps = m_wait(M_K + 2 * g)
                    v.tensor_scalar(kt_[:, g, :], ps[:, :], kb[:, g:g + 1], None, ALU.add).then_inc(m_free[1], 1)
                ps = m_wait(M_V)
                v.tensor_copy(vp[:, :, :, 0:DH], ps[:, :].rearrange("p (t h d) -> p t h d", t=QT, h=H))\
                    .then_inc(m_free[M_V % 2], 1)

                def row_max(u):
                    n = nk(u % 4)
                    v.wait_ge(s_done, b * UNITS + u + 1)
                    v.tensor_reduce(nmax[:, u % 4:u % 4 + 1], s_ps[u % 2][:, 0:n], AX.X, ALU.max,
                                    negate=True).then_inc(max_done, 1)

                def copy_t(u):
                    g, j, qt = u // 16, u // 4 % 4, u % 4
                    n = nk(qt)
                    v.wait_ge(t_done, b * UNITS + u + 3)
                    if u % 16 == 0:
                        v.wait_ge(pv_done, b * G + g + 1)
                    v.tensor_copy(pt[:, g % 2, j, 0:n // P, qt * P:(qt + 1) * P],
                                  t_ps[u % 2][:, 0:n].rearrange("p (a q) -> p a q", q=P)).then_inc(pt_copied, 1)

                def take_og(g):
                    v.wait_ge(pv_done, b * G + g + 3)
                    if g == 0:
                        pass
                    v.tensor_copy(og[:, :], o_ps[g % 2][:, :]).then_inc(og_free, 1)

                def norm(g):
                    ps = m_wait(M_O + g)
                    v.wait_ge(exp_done, b * UNITS + 16 * (g + 1) + 2)
                    v.reciprocal(rinv[:, :, 4 * g:4 * g + 4], rsum[:, :, 4 * g:4 * g + 4]).then_inc(rinv_ready, 1)
                    v.wait_ge(rinv_ready, b * G + g + 1)
                    v4 = ps[:, :].rearrange("p (t h d) -> p t h d", t=QT, h=4)
                    for qt in range(QT):
                        ins = v.tensor_tensor(
                            o[:, qt, 32 * g:32 * g + 32].rearrange("p (h d) -> p h d", h=4), v4[:, qt, :, 0:DH],
                            bc(rinv[:, qt, 4 * g:4 * g + 4].unsqueeze(2), [P, 4, DH]), ALU.mult)
                    ins.then_inc(m_free[(M_O + g) % 2], 1)

                for u in range(UNITS + 3):
                    if u < UNITS:
                        row_max(u)
                    if 2 <= u < UNITS + 2:
                        copy_t(u - 2)
                    if u >= 20 and u % 16 == 4:
                        take_og(u // 16 - 1)
                    if u >= 26 and u % 16 == 10:
                        norm(u // 16 - 1)
                take_og(G - 1)
                norm(G - 1)
                ps = m_wait(M_OT)
                v.tensor_copy(oT[:, :], ps[:, :]).then_inc(m_free[M_OT % 2], 1)
                ps = m_wait(M_Y)
                xs = k.x[:, bass.ds(b * QT, QT), :]
                v.tensor_tensor(xs, ps[:, :].rearrange("p (t d) -> p t d", t=QT), xs, ALU.add)\
                    .then_inc(m_free[M_Y % 2], 1)


def token_logits(nc, k, tag, w_dram, width, bias_dram=None):
    per_bank = min(512 // width, NT)
    n_banks = NT // per_bank
    with ExitStack() as ctx:
        ph = Phase(nc, ctx, tag)
        w = ph.sb("w", [P, width])
        bias = ph.sb("bias", [1, width])
        ps = ph.banks("ps", n_banks)
        loaded, filled, copied = (ph.sem(s) for s in ("loaded", "filled", "copied"))
        block = ctx.enter_context(nc.Block())
        n_loads = 2 if bias_dram is not None else 1

        @block.sync
        def _(sp):
            sp.dma_start(w[:, :], w_dram).then_inc(loaded, 16)
            if bias_dram is not None:
                sp.dma_start(bias[:, :], bias_dram).then_inc(loaded, 16)

        @block.tensor
        def _(pe):
            pe.wait_ge(loaded, 16 * n_loads)
            for i in range(NT):
                c = (i % per_bank) * width
                out = ps[i // per_bank][:, c:c + width]
                last = pe.matmul(out, k.xnT[:, i * P:(i + 1) * P], w[:, :], start=True, stop=bias_dram is None)
                if bias_dram is not None:
                    last = pe.matmul(out, k.ones[0:1, :], bias[:, :], start=False, stop=True)
                if i % per_bank == per_bank - 1:
                    last.then_inc(filled, 1)

        @block.scalar
        def _(act):
            for j in range(n_banks):
                act.wait_ge(filled, j + 1)
                act.copy(k.logits[:, j * per_bank * width:(j + 1) * per_bank * width],
                         ps[j][:, 0:per_bank * width]).then_inc(copied, 1)
            act.wait_ge(copied, n_banks)


def top8_slots(nc, k, tag):
    E = 64
    M = NT * E
    with ExitStack() as ctx:
        ph = Phase(nc, ctx, tag)
        best = ph.sb("best", [P, NT, 8])
        rest = ph.sb("rest", [P, NT, E])
        chosen = ph.sb("chosen", [P, NT, E])
        chosen_bf = ph.sb("chosen_bf", [P, NT, E], BF16)
        before = ph.sb("before", [P, NT, E], BF16)
        ex = ph.sb("ex", [P, NT, E])
        tot = ph.sb("tot", [P, NT])
        rtot = ph.sb("rtot", [P, NT])
        ps = ph.banks("ps", 2)
        chain, shifted, exp_done, before_ready, counted = (ph.sem(s) for s in (
            "chain", "shifted", "exp_done", "before_ready", "counted"))
        lg = k.logits[:, 0:M].rearrange("p (t e) -> p t e", e=E)
        block = ctx.enter_context(nc.Block())

        @block.vector
        def _(v):
            done = [0]

            def link(ins):
                done[0] += 1
                ins.then_inc(chain, 1)

            def settle():
                v.wait_ge(chain, done[0])

            for i in range(NT):
                link(v.max(best[:, i, :], lg[:, i, :]))
            settle()
            v.tensor_tensor(ex[:, :, :], lg, bc(best[:, :, 0:1], [P, NT, E]), ALU.subtract).then_inc(shifted, 1)
            for i in range(NT):
                link(v.match_replace(rest[:, i, :], best[:, i, :], lg[:, i, :], -BIG))
            settle()
            link(v.tensor_tensor(chosen[:, :, :], rest[:, :, :], lg, ALU.not_equal))
            settle()
            link(v.tensor_copy(chosen_bf[:, :, :], chosen[:, :, :]))
            link(v.memset(before[:, 0, :], 0.0))
            settle()
            for i in range(1, NT):
                link(v.tensor_tensor(before[:, i, :], before[:, i - 1, :], chosen_bf[:, i - 1, :], ALU.add))
                settle()
            v.sem_inc(before_ready, 1)
            v.wait_ge(exp_done, 1)
            link(v.tensor_tensor(ex[:, :, :], ex[:, :, :], chosen[:, :, :], ALU.mult))
            settle()
            link(v.tensor_reduce(tot[:, :], ex[:, :, :], AX.X, ALU.add))
            settle()
            link(v.reciprocal(rtot[:, :], tot[:, :]))
            settle()
            link(v.tensor_tensor(k.weight[:, :, :], ex[:, :, :], bc(rtot[:, :].unsqueeze(2), [P, NT, E]), ALU.mult))
            link(v.tensor_scalar(chosen[:, :, :], chosen[:, :, :], -4096.0, 4096.0, ALU.mult, ALU.add))
            settle()
            for j in range(2):
                v.wait_ge(counted, j + 1)
                link(v.tensor_tensor(k.place[:, 8 * j:8 * j + 8, :], ps[j][:, :].rearrange("p (t e) -> p t e", e=E),
                                     chosen[:, 8 * j:8 * j + 8, :], ALU.add))
            settle()

        @block.scalar
        def _(act):
            act.wait_ge(shifted, 1)
            act.activation(ex[:, :, :], ex[:, :, :], ACT.Exp).then_inc(exp_done, 1)

        @block.tensor
        def _(pe):
            pe.wait_ge(before_ready, 1)
            for i in range(NT):
                out = ps[i // 8][:, (i % 8) * E:(i % 8 + 1) * E]
                pe.matmul(out, k.earlier[:, :], chosen_bf[:, i, :], start=True, stop=False)
                last = pe.matmul(out, k.ones_bf[:, :], before[:, i, :], start=False, stop=True)
                if i % 8 == 7:
                    last.then_inc(counted, 1)


def slot_dispatch(nc, k, tag):
    E, C = 64, 32
    with ExitStack() as ctx:
        ph = Phase(nc, ctx, tag)
        xs = ph.sb("xs", [P, 2, P])
        hot = ph.sb("hot", [P, 2, E, C])
        zeros = ph.sb("zeros", [P, 512], BF16)
        ps = ph.banks("ps", 4)
        zeroed, ready, used, copied = (ph.sem(s) for s in ("zeroed", "ready", "used", "copied"))
        filled = ph.sem("filled")
        block = ctx.enter_context(nc.Block())

        @block.vector
        def _(v):
            v.memset(zeros[:, :], 0.0).then_inc(zeroed, 1)
            v.sem_inc(used, 2)
            with v.Fori(0, NT // 2) as i:
                for s in range(2):
                    v.wait_ge(used, 2 * i + s + 1)
                    v.tensor_copy(xs[:, s, :], k.xn[:, bass.ds(2 * i + s, 1), :].rearrange("p a d -> p (a d)"))
                    v.tensor_tensor(hot[:, s, :, :],
                                    bc(k.place[:, bass.ds(2 * i + s, 1), :].rearrange("p a e -> p (a e)").unsqueeze(2), [P, E, C]),
                                    bc(k.iota[:, 0:C].unsqueeze(1), [P, E, C]), ALU.is_equal).then_inc(ready, 1)

        @block.tensor
        def _(pe):
            pe.wait_ge(zeroed, 1)
            for c in range(4):
                pe.matmul(ps[c][:, :], zeros[:, 0:P], zeros[:, :], start=True, stop=False, skip_group_check=True)
            with pe.Fori(0, NT // 2) as i:
                for s in range(2):
                    pe.wait_ge(ready, 2 * i + s + 1)
                    for c in range(4):
                        last = pe.matmul(ps[c][:, :], xs[:, s, :],
                                         hot[:, s, 16 * c:16 * c + 16, :].rearrange("p e c -> p (e c)"),
                                         start=False, stop=False, skip_group_check=True)
                    last.then_inc(used, 1)
            for c in range(4):
                pe.matmul(ps[c][:, :], zeros[:, 0:P], zeros[:, :], start=False, stop=True,
                          skip_group_check=True).then_inc(filled, 1)

        @block.scalar
        def _(act):
            for c in range(4):
                act.wait_ge(filled, c + 1)
                act.copy(k.slots_x[:, c * 512:(c + 1) * 512], ps[c][:, :]).then_inc(copied, 1)
            act.wait_ge(copied, 4)


def slot_experts(nc, k, tag, gate_up, down):
    F, GROUPS = 96, 16
    with ExitStack() as ctx:
        ph = Phase(nc, ctx, tag)
        wgu = ph.sb("wgu", [P, 2, 4, 2 * F])
        wd = ph.sb("wd", [F, 2, 4, P])
        sg = ph.sb("sg", [F, 2, P])
        h = ph.sb("h", [F, 2, P])
        yT = ph.sb("yT", [P, 2, P])
        gu_ps, y_ps, t_ps = (ph.banks(s, 2) for s in ("gu", "y", "t"))
        in_a, in_b, loaded0, loaded1, gu_done, silu_done, h_done, y_done, yT_done, turned, stored = (
            ph.sem(s) for s in ("in_a", "in_b", "loaded0", "loaded1", "gu_done", "silu_done", "h_done",
                                "y_done", "yT_done", "turned", "stored"))
        loaded = (loaded0, loaded1)
        block = ctx.enter_context(nc.Block())

        @block.sync
        def _(sp):
            for s in range(2):
                sp.dma_start(wgu[:, s, :, :], gate_up[s]).then_inc(loaded[s], 16)
                sp.dma_start(wd[:, s, :, :], down[s]).then_inc(loaded[s], 16)
            with sp.Fori(1, GROUPS // 2) as i:
                for s in range(2):
                    sp.wait_ge(y_done, 2 * i + s - 1)
                    sp.dma_start(wgu[:, s, :, :], gate_up[bass.ds(2 * i + s, 1)].rearrange("a p e f -> (a p) e f"))\
                        .then_inc(loaded[s], 16)
                    sp.dma_start(wd[:, s, :, :], down[bass.ds(2 * i + s, 1)].rearrange("a p e f -> (a p) e f"))\
                        .then_inc(loaded[s], 16)

        @block.tensor
        def _(pe):
            with pe.Fori(0, GROUPS // 2) as i:
                for s in range(2):
                    pe.wait_ge(loaded[s], 32 * i + 32)
                    pe.wait_ge(h_done, 2 * i + s + 1)
                    for f in range(2):
                        for e in range(4):
                            last = pe.matmul(gu_ps[s][0:F, f * P + 32 * e:f * P + 32 * e + 32],
                                             wgu[:, s, e, f * F:(f + 1) * F],
                                             k.slots_x[:, bass.ds((2 * i + s) * P + 32 * e, 32)], start=True, stop=True)
                    last.then_inc(gu_done, 1)
                for s in range(2):
                    pe.wait_ge(h_done, 2 * i + s + 3)
                    pe.wait_ge(yT_done, 2 * i + s + 1)
                    for e in range(4):
                        last = pe.matmul(y_ps[s][:, 32 * e:32 * e + 32], wd[:, s, e, :], h[:, s, 32 * e:32 * e + 32],
                                         start=True, stop=True)
                    last.then_inc(y_done, 1)
                for s in range(2):
                    pe.wait_ge(yT_done, 2 * i + s + 3)
                    pe.wait_ge(stored, 2 * i + s + 1)
                    pe.transpose(t_ps[s][:, 0:P], yT[:, s, :], k.ident[:, :]).then_inc(turned, 1)

        @block.scalar
        def _(act):
            act.sem_inc(stored, 2)
            with act.Fori(0, GROUPS // 2) as i:
                for s in range(2):
                    act.wait_ge(gu_done, 2 * i + s + 1)
                    act.activation(sg[:, s, :], gu_ps[s][0:F, 0:P], ACT.Silu).then_inc(silu_done, 1)
                for s in range(2):
                    act.wait_ge(turned, 2 * i + s + 1)
                    act.copy(k.slots_y[:, bass.ds(2 * i + s, 1), :].rearrange("p a d -> p (a d)"), t_ps[s][:, 0:P])\
                        .then_inc(stored, 1)

        @block.vector
        def _(v):
            v.sem_inc(h_done, 2)
            v.sem_inc(yT_done, 2)
            with v.Fori(0, GROUPS // 2) as i:
                for s in range(2):
                    v.wait_ge(silu_done, 2 * i + s + 1)
                    v.tensor_tensor(h[:, s, :], sg[:, s, :], gu_ps[s][0:F, P:2 * P], ALU.mult).then_inc(h_done, 1)
                for s in range(2):
                    v.wait_ge(y_done, 2 * i + s + 1)
                    v.tensor_copy(yT[:, s, :], y_ps[s][:, 0:P]).then_inc(yT_done, 1)


def slot_combine(nc, k, tag):
    E, C, GROUPS = 64, 32, 16
    with ExitStack() as ctx:
        ph = Phase(nc, ctx, tag)
        hot = ph.sb("hot", [P, 2, E, C])
        share = ph.sb("share", [P, 2, E, C])
        shareT = ph.sb("shareT", [P, 2, GROUPS, P])
        t_ps = ph.banks("t", 4)
        y_ps = ph.banks("y", 2)
        hot_ready, share_ready, turned, copied, summed, added = (
            ph.sem(s) for s in ("hot_ready", "share_ready", "turned", "copied", "summed", "added"))
        block = ctx.enter_context(nc.Block())

        @block.vector
        def _(v):
            v.sem_inc(turned, 8)
            v.sem_inc(summed, 2)
            v.sem_inc(added, 2)
            with v.Fori(0, NT // 2) as i:
                for s in range(2):
                    t = 2 * i + s
                    v.wait_ge(turned, 8 * i + 4 * s + 4)
                    v.tensor_tensor(hot[:, s, :, :],
                                    bc(k.place[:, bass.ds(t, 1), :].rearrange("p a e -> p (a e)").unsqueeze(2), [P, E, C]),
                                    bc(k.iota[:, 0:C].unsqueeze(1), [P, E, C]), ALU.is_equal).then_inc(hot_ready, 1)
                    v.wait_ge(hot_ready, 2 * i + s + 1)
                    v.tensor_tensor(share[:, s, :, :], hot[:, s, :, :],
                                    bc(k.weight[:, bass.ds(t, 1), :].rearrange("p a e -> p (a e)").unsqueeze(2), [P, E, C]),
                                    ALU.mult).then_inc(share_ready, 1)
                for s in range(2):
                    t = 2 * i + s
                    v.wait_ge(summed, 2 * i + s + 3)
                    xs = k.x[:, bass.ds(t, 1), :].rearrange("p a d -> p (a d)")
                    v.tensor_tensor(xs, y_ps[s][:, 0:P], xs, ALU.add).then_inc(added, 1)

        @block.tensor
        def _(pe):
            with pe.Fori(0, NT // 2) as i:
                for s in range(2):
                    pe.wait_ge(share_ready, 2 * i + s + 1)
                    sh = share[:, s, :, :].rearrange("p e c -> p (e c)")
                    for c in range(4):
                        pe.wait_ge(copied, 8 * i + 4 * s + c + 1)
                        for g in range(4):
                            last = pe.transpose(t_ps[c][:, g * P:(g + 1) * P],
                                                sh[:, (4 * c + g) * P:(4 * c + g + 1) * P], k.ident[:, :])
                        last.then_inc(turned, 1)
                    pe.wait_ge(copied, 8 * i + 4 * s + 4 + 4)
                    pe.wait_ge(added, 2 * i + s + 1)
                    for g in range(GROUPS):
                        last = pe.matmul(y_ps[s][:, 0:P], shareT[:, s, g, :], k.slots_y[:, g, :],
                                         start=(g == 0), stop=(g == GROUPS - 1))
                    last.then_inc(summed, 1)

        @block.scalar
        def _(act):
            act.sem_inc(copied, 4)
            with act.Fori(0, NT // 2) as i:
                for s in range(2):
                    act.wait_ge(summed, 2 * i + s + 1)
                    for c in range(4):
                        act.wait_ge(turned, 8 * i + 4 * s + c + 1 + 8)
                        act.copy(shareT[:, s, 4 * c:4 * c + 4, :].rearrange("p g t -> p (g t)"), t_ps[c][:, :])\
                            .then_inc(copied, 1)


def top2_gates(nc, k, tag, groups, rule, scale_dram=None, capacity=None):
    M = NT * groups
    with ExitStack() as ctx:
        ph = Phase(nc, ctx, tag)
        below = ph.sb("below", [P, M, 8])
        first = ph.sb("first", [P, M, 8])
        second = ph.sb("second", [P, M, 8])
        left = ph.sb("left", [P, M, 8])
        m = ph.sb("m", [P, 2, M])
        e = ph.sb("e", [P, 2, M])
        where = ph.sb("where", [P, M])
        tot = ph.sb("tot", [P, M])
        chain, best_ready, exp_done, scale_in, both_ready, counted = (
            ph.sem(s) for s in ("chain", "best_ready", "exp_done", "scale_in", "both_ready", "counted"))
        if rule == "capacity":
            both = ph.sb("both", [P, NT, 8], BF16)
            before = ph.sb("before", [P, NT, 8], BF16)
            ex = ph.sb("ex", [P, M, 8])
            ps = ph.banks("ps", 1)
        if rule == "sigmoid":
            rscale = ph.sb("rscale", [P, 1])
        lg = k.logits[:, 0:M * 8].rearrange("p (m e) -> p m e", e=8)
        gate = k.gate[:, 0:M * 8].rearrange("p (m e) -> p m e", e=8)
        wide = [P, M, 8]
        iota8 = bc(k.iota[:, 0:8].unsqueeze(1), wide)
        block = ctx.enter_context(nc.Block())

        @block.sync
        def _(sp):
            if rule == "sigmoid":
                sp.dma_start(rscale[:, :], scale_dram).then_inc(scale_in, 16)

        @block.vector
        def _(v):
            done = [0]

            def link(ins):
                done[0] += 1
                ins.then_inc(chain, 1)
                v.wait_ge(chain, done[0])

            def over8(ap):
                return bc(ap.unsqueeze(2), wide)

            def best(src, i, hot):
                link(v.tensor_reduce(m[:, i, :], src, AX.X, ALU.max))
                link(v.tensor_tensor(below[:, :, :], src, over8(m[:, i, :]), ALU.is_lt))
                link(v.scalar_tensor_tensor(below[:, :, :], below[:, :, :], 1024.0, iota8, ALU.mult, ALU.add))
                link(v.tensor_reduce(where[:, :], below[:, :, :], AX.X, ALU.min))
                link(v.tensor_tensor(hot[:, :, :], iota8, over8(where[:, :]), ALU.is_equal))

            best(lg, 0, first)
            link(v.scalar_tensor_tensor(left[:, :, :], first[:, :, :], -BIG, lg, ALU.mult, ALU.add))
            best(left[:, :, :], 1, second)
            if rule == "sigmoid":
                v.sem_inc(best_ready, 1)
                v.wait_ge(exp_done, 1)
                link(v.tensor_scalar(e[:, :, :], e[:, :, :], 1.0, None, ALU.add))
                link(v.reciprocal(e[:, :, :], e[:, :, :]))
                link(v.tensor_tensor(tot[:, :], e[:, 0, :], e[:, 1, :], ALU.add))
                link(v.tensor_scalar(tot[:, :], tot[:, :], 1e-9, None, ALU.max))
                link(v.reciprocal(tot[:, :], tot[:, :]))
                v.wait_ge(scale_in, 16)
                link(v.tensor_scalar(tot[:, :], tot[:, :], rscale[:, 0:1], None, ALU.mult))
                for i in range(2):
                    link(v.tensor_tensor(e[:, i, :], e[:, i, :], tot[:, :], ALU.mult))
            else:
                link(v.tensor_tensor(e[:, 1, :], m[:, 1, :], m[:, 0, :], ALU.subtract))
                if rule == "capacity":
                    link(v.tensor_tensor(ex[:, :, :], lg, over8(m[:, 0, :]), ALU.subtract))
                v.sem_inc(best_ready, 1)
                v.wait_ge(exp_done, 1)
                if rule == "softmax2":
                    link(v.tensor_scalar(tot[:, :], e[:, 1, :], 1.0, None, ALU.add))
                else:
                    link(v.tensor_reduce(tot[:, :], ex[:, :, :], AX.X, ALU.add))
                link(v.reciprocal(e[:, 0, :], tot[:, :]))
                link(v.tensor_tensor(e[:, 1, :], e[:, 1, :], e[:, 0, :], ALU.mult))
            if rule == "capacity":
                link(v.tensor_tensor(both[:, :, :], first[:, :, :], second[:, :, :], ALU.add))
                link(v.memset(before[:, 0, :], 0.0))
                for i in range(1, NT):
                    link(v.tensor_tensor(before[:, i, :], before[:, i - 1, :], both[:, i - 1, :], ALU.add))
                v.sem_inc(both_ready, 1)
            link(v.tensor_tensor(first[:, :, :], first[:, :, :], over8(e[:, 0, :]), ALU.mult))
            link(v.tensor_tensor(second[:, :, :], second[:, :, :], over8(e[:, 1, :]), ALU.mult))
            link(v.tensor_tensor(gate, first[:, :, :], second[:, :, :], ALU.add))
            if rule == "capacity":
                v.wait_ge(counted, 1)
                link(v.tensor_scalar(left[:, :, :], ps[0][:, 0:M * 8].rearrange("p (m e) -> p m e", e=8),
                                     float(capacity), None, ALU.is_lt))
                link(v.tensor_tensor(gate, gate, left[:, :, :], ALU.mult))
                link(v.tensor_reduce(tot[:, :], gate, AX.X, ALU.add))
                link(v.tensor_scalar(tot[:, :], tot[:, :], 1e-6, None, ALU.add))
                link(v.reciprocal(tot[:, :], tot[:, :]))
                link(v.tensor_tensor(gate, gate, over8(tot[:, :]), ALU.mult))

        @block.scalar
        def _(act):
            act.wait_ge(best_ready, 1)
            if rule == "sigmoid":
                act.activation(e[:, :, :], m[:, :, :], ACT.Exp, scale=-1.0).then_inc(exp_done, 1)
            elif rule == "softmax2":
                act.activation(e[:, 1, :], e[:, 1, :], ACT.Exp).then_inc(exp_done, 1)
            else:
                act.activation(ex[:, :, :], ex[:, :, :], ACT.Exp)
                act.activation(e[:, 1, :], e[:, 1, :], ACT.Exp).then_inc(exp_done, 1)

        if rule == "capacity":
            @block.tensor
            def _(pe):
                pe.wait_ge(both_ready, 1)
                for i in range(NT):
                    out = ps[0][:, i * 8:(i + 1) * 8]
                    pe.matmul(out, k.earlier[:, :], both[:, i, :], start=True, stop=False)
                    last = pe.matmul(out, k.ones_bf[:, :], before[:, i, :], start=False, stop=True)
                last.then_inc(counted, 1)


def gated_ffn(nc, k, tag, w0d, w1d, w2d, b0d, b1d, b2d):
    E, C = 8, 4
    STEPS = E * C
    with ExitStack() as ctx:
        ph = Phase(nc, ctx, tag)
        w0 = ph.sb("w0", [P, E, C, P])
        w1 = ph.sb("w1", [P, E, C, P])
        w2 = ph.sb("w2", [P, E, C, P])
        b0 = ph.sb("b0", [P, E * C])
        b1 = ph.sb("b1", [P, E * C])
        b2 = ph.sb("b2", [8, P])
        sg = ph.sb("sg", [P, 2, T])
        hg = ph.sb("hg", [P, 2, T])
        gs = ph.sb("gs", [P, QT, 8])
        gT = ph.sb("gT", [8, T])
        h_ps, g_ps, y_ps, m_ps = (ph.banks(s, 2) for s in ("h", "g", "y", "m"))
        loaded, h_full, g_full, silu_done, hg_done, hg_used, y_full, y_free, gs_ready, gT_full, gT_ready, b_full = (
            ph.sem(s) for s in ("loaded", "h_full", "g_full", "silu_done", "hg_done", "hg_used", "y_full",
                                "y_free", "gs_ready", "gT_full", "gT_ready", "b_full"))
        acc_chain = ph.sem("acc_chain")
        block = ctx.enter_context(nc.Block())

        @block.sync
        def _(sp):
            for dst, src in ((w1[:, :, :, :], w1d), (w0[:, :, :, :], w0d), (w2[:, :, :, :], w2d), (b0[:, :], b0d),
                             (b1[:, :], b1d), (b2[:, :], b2d)):
                sp.dma_start(dst, src).then_inc(loaded, 16)

        @block.tensor
        def _(pe):
            pe.wait_ge(loaded, 16 * 6)
            with pe.Fori(0, B) as t:
                xs = k.xnT[:, bass.ds(t * T, T)]

                def up(n):
                    pe.wait_ge(hg_done, t * STEPS + n + 1)
                    pe.matmul(g_ps[n % 2][:, :], w1[:, n // C, n % C, :], xs, start=True, stop=True).then_inc(g_full, 1)
                    pe.matmul(h_ps[n % 2][:, :], w0[:, n // C, n % C, :], xs, start=True, stop=True).then_inc(h_full, 1)

                def down(n):
                    e, c = n // C, n % C
                    pe.wait_ge(hg_done, t * STEPS + n + 3)
                    if c == 0:
                        pe.wait_ge(y_free, t * E + e + 1)
                    for i in range(QT):
                        last = pe.matmul(y_ps[e % 2][:, i * P:(i + 1) * P], hg[:, n % 2, i * P:(i + 1) * P],
                                         w2[:, e, c, :], start=(c == 0 and i == 0), stop=(c == C - 1),
                                         skip_group_check=True)
                    last.then_inc(hg_used, 1)

                for n in range(STEPS + 1):
                    if n < STEPS:
                        up(n)
                    if n >= 1:
                        down(n - 1)
                pe.wait_ge(gs_ready, t + 1)
                for i in range(QT):
                    last = pe.transpose(m_ps[0][0:8, i * P:(i + 1) * P], gs[:, i, :], k.ident[:, :])
                last.then_inc(gT_full, 1)
                pe.wait_ge(gT_ready, t + 1)
                for i in range(QT):
                    last = pe.matmul(m_ps[1][:, i * P:(i + 1) * P], gT[:, i * P:(i + 1) * P], b2[:, :],
                                     start=True, stop=True)
                last.then_inc(b_full, 1)

        @block.scalar
        def _(act):
            act.wait_ge(loaded, 16 * 6)
            with act.Fori(0, B) as t:
                for n in range(STEPS):
                    act.wait_ge(g_full, t * STEPS + n + 1)
                    act.wait_ge(hg_done, t * STEPS + n + 1)
                    act.activation(sg[:, n % 2, :], g_ps[n % 2][:, :], ACT.Silu, bias=b1[:, n:n + 1]).then_inc(silu_done, 1)

        @block.vector
        def _(v):
            v.sem_inc(hg_done, 2)
            v.sem_inc(hg_used, 2)
            v.sem_inc(y_free, 2)
            v.wait_ge(loaded, 16 * 6)
            with v.Fori(0, B) as t:
                v.tensor_copy(gs[:, :, :], k.gate[:, bass.ds(t * QT * 8, QT * 8)].rearrange("p (i e) -> p i e", e=8))\
                    .then_inc(gs_ready, 1)
                v.wait_ge(gs_ready, t + 1)
                xs = k.x[:, bass.ds(t * QT, QT), :]

                def gated(e):
                    v.wait_ge(hg_used, t * STEPS + (e + 1) * C + 2)
                    if e > 0:
                        v.wait_ge(y_free, t * E + e + 2)
                    for i in range(QT):
                        last = v.scalar_tensor_tensor(xs[:, i, :], y_ps[e % 2][:, i * P:(i + 1) * P],
                                                      gs[:, i, e:e + 1], xs[:, i, :], ALU.mult, ALU.add)
                    last.then_inc(y_free, 1)

                for n in range(STEPS + 2):
                    if n < STEPS:
                        v.wait_ge(silu_done, t * STEPS + n + 1)
                        v.wait_ge(h_full, t * STEPS + n + 1)
                        v.wait_ge(hg_used, t * STEPS + n + 1)
                        v.scalar_tensor_tensor(hg[:, n % 2, :], h_ps[n % 2][:, :], b0[:, n:n + 1], sg[:, n % 2, :],
                                               ALU.add, ALU.mult).then_inc(hg_done, 1)
                    if n >= 5 and n % C == 1:
                        gated(n // C - 1)
                v.wait_ge(gT_full, t + 1)
                v.tensor_copy(gT[:, :], m_ps[0][0:8, :]).then_inc(gT_ready, 1)
                v.wait_ge(b_full, t + 1)
                v.wait_ge(y_free, t * E + E + 2)
                v.tensor_tensor(xs, m_ps[1][:, :].rearrange("p (i d) -> p i d", d=P), xs, ALU.add).then_inc(acc_chain, 1)
                v.wait_ge(acc_chain, t + 1)


def selective_scan(nc, k, tag, d):
    S = 16
    NEAR = 99.0
    with ExitStack() as ctx:
        ph = Phase(nc, ctx, tag)
        w_in = ph.sb("w_in", [P, 2 * P])
        w_x = ph.sb("w_x", [P, S + 2 * P])
        w_dt = ph.sb("w_dt", [S, P])
        w_o = ph.sb("w_o", [P, P])
        b_o = ph.sb("b_o", [1, P])
        b_in = ph.sb("b_in", [P, 2])
        b_bc = ph.sb("b_bc", [P, 2])
        b_dl = ph.sb("b_dl", [S, 1])
        b_dt = ph.sb("b_dt", [P, 1])
        dpar = ph.sb("dpar", [P, 1])
        a_log = ph.sb("a_log", [P, S])
        a = ph.sb("a", [P, S])
        a_slow = ph.sb("a_slow", [P, 1])
        xi = ph.sb("xi", [P, T])
        res = ph.sb("res", [P, T])
        dl = ph.sb("dl", [S, T])
        cm = ph.sb("cm", [P, T])
        z = ph.sb("z", [P, T])
        s1 = ph.sb("s1", [P, T])
        s2 = ph.sb("s2", [P, T])
        delta = ph.sb("delta", [P, T])
        u = ph.sb("u", [P, T])
        da = ph.sb("da", [P, S, T])
        da_slow = ph.sb("da_slow", [P, T])
        h = ph.sb("h", [P, S, T])
        y = ph.sb("y", [P, T])
        peak = ph.sb("peak", [P, 1])
        top = ph.sb("top", [1, 1])
        flag = ph.sb("flag", [1, 1], I32)
        state = ph.sb("state", [P, S])
        ps = ph.banks("ps", 8)
        chain, loaded, a_raw, a_ready, in_full, in_read, dl_full, dl_ready, bc_full, dt_full, z_ready, e_ready = (
            ph.sem(s) for s in ("chain", "loaded", "a_raw", "a_ready", "in_full", "in_read", "dl_full", "dl_ready",
                                "bc_full", "dt_full", "z_ready", "e_ready"))
        delta_ready, da_ready, peak_ready, peak_full, y_ready, y_full, x_added, checked, mixed, state_set = (
            ph.sem(s) for s in ("delta_ready", "da_ready", "peak_ready", "peak_full", "y_ready", "y_full", "x_added",
                                "checked", "mixed", "state_set"))
        block = ctx.enter_context(nc.Block())
        loads = [(w_in[:, :], d["w_in"]), (w_x[:, :], d["w_x"]), (w_dt[:, :], d["w_dt"]), (w_o[:, :], d["w_o"]),
                 (b_o[:, :], d["b_o"]), (b_in[:, :], d["b_in"]), (b_bc[:, :], d["b_bc"]), (b_dl[:, :], d["b_dl"]),
                 (b_dt[:, :], d["b_dt"]), (dpar[:, :], d["dpar"]), (a_log[:, :], d["a_log"])]

        @block.sync
        def _(sp):
            for dst, src in loads:
                sp.dma_start(dst, src).then_inc(loaded, 16)

        @block.tensor
        def _(pe):
            pe.wait_ge(loaded, 16 * len(loads))
            with pe.Fori(0, B) as b:
                xs = k.xnT[:, bass.ds(b * T, T)]
                for i in range(2):
                    pe.matmul(ps[i][:, :], w_in[:, i * P:(i + 1) * P], xs, start=True, stop=True).then_inc(in_full, 1)
                pe.wait_ge(in_read, 2 * b + 2)
                pe.matmul(ps[2][0:S, :], w_x[:, 0:S], xi[:, :], start=True, stop=True).then_inc(dl_full, 1)
                for i in range(2):
                    last = pe.matmul(ps[3 + i][:, :], w_x[:, S + i * P:S + (i + 1) * P], xi[:, :], start=True, stop=True)
                last.then_inc(bc_full, 1)
                pe.wait_ge(dl_ready, b + 1)
                pe.matmul(ps[5][:, :], w_dt[:, :], dl[:, :], start=True, stop=True).then_inc(dt_full, 1)
                pe.wait_ge(peak_ready, b + 1)
                pe.transpose(ps[6][0:1, 0:P], peak[:, :], k.ident[:, :]).then_inc(peak_full, 1)
                pe.wait_ge(y_ready, b + 1)
                for i in range(QT):
                    out = ps[7][:, i * P:(i + 1) * P]
                    pe.matmul(out, y[:, i * P:(i + 1) * P], w_o[:, :], start=True, stop=False)
                    last = pe.matmul(out, k.ones[0:1, :], b_o[:, :], start=False, stop=True)
                last.then_inc(y_full, 1)
                pe.wait_ge(x_added, b + 1)

        @block.scalar
        def _(act):
            act.wait_ge(a_raw, 1)
            act.activation(a[:, :], a_log[:, :], ACT.Exp).then_inc(a_ready, 1)
            with act.Fori(0, B) as b:
                act.wait_ge(in_full, 2 * b + 1)
                act.activation(xi[:, :], ps[0][:, :], ACT.Silu, bias=b_in[:, 0:1]).then_inc(in_read, 1)
                act.wait_ge(in_full, 2 * b + 2)
                act.activation(res[:, :], ps[1][:, :], ACT.Silu, bias=b_in[:, 1:2]).then_inc(in_read, 1)
                act.wait_ge(z_ready, b + 1)
                act.activation(z[:, :], z[:, :], ACT.Exp).then_inc(e_ready, 1)
                act.wait_ge(delta_ready, b + 1)
                act.activation(da_slow[:, :], delta[:, :], ACT.Exp, scale=a_slow[:, 0:1]).then_inc(da_ready, 1)
                for n in range(S):
                    act.activation(da[:, n, :], delta[:, :], ACT.Exp, scale=a[:, n:n + 1]).then_inc(da_ready, 1)
                act.wait_ge(x_added, b + 1)

        @block.vector
        def _(v):
            v.wait_ge(loaded, 16 * len(loads))
            v.tensor_scalar(a_log[:, :], a_log[:, :], 2.0, -5.0, ALU.min, ALU.max).then_inc(a_raw, 1)
            v.wait_ge(a_ready, 1)
            v.tensor_scalar(a[:, :], a[:, :], -1.0, -5.0, ALU.mult, ALU.max).then_inc(a_raw, 1)
            v.wait_ge(a_raw, 2)
            v.tensor_scalar(a[:, :], a[:, :], -0.01, None, ALU.min).then_inc(a_raw, 1)
            v.wait_ge(a_raw, 3)
            v.tensor_reduce(a_slow[:, :], a[:, :], AX.X, ALU.max).then_inc(a_raw, 1)
            v.wait_ge(a_raw, 4)
            LINKS = 21
            with v.Fori(0, B) as b:
                done = [0]

                def link(ins):
                    done[0] += 1
                    ins.then_inc(chain, 1)
                    v.wait_ge(chain, b * LINKS + done[0])

                v.wait_ge(dl_full, b + 1)
                v.tensor_scalar(dl[:, :], ps[2][0:S, :], b_dl[:, 0:1], None, ALU.add).then_inc(dl_ready, 1)
                v.wait_ge(bc_full, b + 1)
                link(v.tensor_scalar(cm[:, :], ps[4][:, :], b_bc[:, 1:2], None, ALU.add))
                v.wait_ge(dt_full, b + 1)
                v.tensor_scalar(z[:, :], ps[5][:, :], b_dt[:, 0:1], 0.0, ALU.add, ALU.min).then_inc(z_ready, 1)
                v.wait_ge(e_ready, b + 1)
                link(v.tensor_scalar(z[:, :], z[:, :], 0.2, None, ALU.min))
                link(v.tensor_scalar(s1[:, :], z[:, :], 2.0, None, ALU.add))
                link(v.reciprocal(s1[:, :], s1[:, :]))
                link(v.tensor_tensor(s1[:, :], z[:, :], s1[:, :], ALU.mult))
                link(v.tensor_tensor(s2[:, :], s1[:, :], s1[:, :], ALU.mult))
                link(v.tensor_scalar(z[:, :], s2[:, :], 2.0 / 9, 2.0 / 7, ALU.mult, ALU.add))
                for c in (2.0 / 5, 2.0 / 3, 2.0):
                    link(v.tensor_tensor(z[:, :], z[:, :], s2[:, :], ALU.mult))
                    link(v.tensor_scalar(z[:, :], z[:, :], c, None, ALU.add))
                link(v.tensor_tensor(z[:, :], z[:, :], s1[:, :], ALU.mult))
                v.tensor_scalar(delta[:, :], z[:, :], 1e-5, 0.1, ALU.max, ALU.min).then_inc(delta_ready, 1)
                v.wait_ge(delta_ready, b + 1)
                link(v.scalar_tensor_tensor(u[:, :], ps[3][:, :], b_bc[:, 0:1], delta[:, :], ALU.add, ALU.mult))
                link(v.tensor_tensor(u[:, :], u[:, :], xi[:, :], ALU.mult))
                link(v.scalar_tensor_tensor(s1[:, :], u[:, :], -1.0, u[:, :], ALU.mult, ALU.max))
                v.wait_ge(da_ready, b * (S + 1) + 1)
                link(v.tensor_tensor_scan(s2[:, :], da_slow[:, :], s1[:, :], 0.0, ALU.mult, ALU.add))
                v.tensor_reduce(peak[:, :], s2[:, :], AX.X, ALU.max).then_inc(peak_ready, 1)
                for n in range(S):
                    v.wait_ge(da_ready, b * (S + 1) + n + 2)
                    last = v.tensor_tensor_scan(h[:, n, :], da[:, n, :], u[:, :], 0.0, ALU.mult, ALU.add)
                link(last)
                v.wait_ge(peak_full, b + 1)
                link(v.tensor_reduce(top[:, :], ps[6][0:1, 0:P], AX.X, ALU.max))
                v.tensor_scalar(flag[:, :], top[:, :], NEAR, None, ALU.is_lt).then_inc(checked, 1)
                v.wait_ge(checked, b + 1)
                v.memset(state[:, :], 0.0).then_inc(state_set, 1)
                small = v.value_load(flag[0:1, 0:1], min_val=0, max_val=1)
                with v.If(small < 1):
                    v.drain()
                    with v.Fori(0, T) as t:
                        v.tensor_tensor(state[:, :], state[:, :], da[:, :, bass.ds(t, 1)].rearrange("p n a -> p (n a)"),
                                        ALU.mult)
                        v.drain()
                        v.tensor_scalar(state[:, :], state[:, :], u[:, bass.ds(t, 1)], -100.0, ALU.add, ALU.max)
                        v.drain()
                        v.tensor_scalar(state[:, :], state[:, :], 100.0, None, ALU.min)
                        v.drain()
                        v.tensor_copy(h[:, :, bass.ds(t, 1)].rearrange("p n a -> p (n a)"), state[:, :])
                        v.drain()
                link(v.tensor_reduce(s1[:, :], h[:, :, :].rearrange("p n t -> p t n"), AX.X, ALU.add))
                assert done[0] == LINKS
                v.tensor_tensor(s1[:, :], s1[:, :], cm[:, :], ALU.mult).then_inc(mixed, 1)
                v.wait_ge(mixed, 3 * b + 1)
                v.scalar_tensor_tensor(s1[:, :], xi[:, :], dpar[:, 0:1], s1[:, :], ALU.mult, ALU.add).then_inc(mixed, 1)
                v.wait_ge(mixed, 3 * b + 2)
                v.wait_ge(in_read, 2 * b + 2)
                v.tensor_tensor(y[:, :], s1[:, :], res[:, :], ALU.mult).then_inc(y_ready, 1)
                v.wait_ge(y_full, b + 1)
                xs = k.x[:, bass.ds(b * QT, QT), :]
                v.tensor_tensor(xs, ps[7][:, :].rearrange("p (i d) -> p i d", d=P), xs, ALU.add).then_inc(x_added, 1)
                v.sem_inc(mixed, 1)


def shared_ffn(nc, k, tag, wg_d, wd_d):
    E = 8
    with ExitStack() as ctx:
        ph = Phase(nc, ctx, tag)
        wg = ph.sb("wg", [P, 2, P])
        wd = ph.sb("wd", [P, 2, E, P])
        hid = ph.sb("hid", [P, 2, T])
        gs = ph.sb("gs", [P, QT, 8])
        h_ps = ph.banks("h", 2)
        y_ps = ph.banks("y", 4)
        loaded, h_full, h_ready, y_full, y_free, gs_ready, chain = (ph.sem(s) for s in (
            "loaded", "h_full", "h_ready", "y_full", "y_free", "gs_ready", "chain"))
        block = ctx.enter_context(nc.Block())
        Y = 2 * QT

        @block.sync
        def _(sp):
            sp.dma_start(wg[:, :, :], wg_d).then_inc(loaded, 16)
            sp.dma_start(wd[:, :, :, :], wd_d).then_inc(loaded, 16)

        @block.tensor
        def _(pe):
            pe.wait_ge(loaded, 32)
            with pe.Fori(0, B) as t:
                xs = k.xnT[:, bass.ds(t * T, T)]
                for c in range(2):
                    pe.matmul(h_ps[c][:, :], wg[:, c, :], xs, start=True, stop=True).then_inc(h_full, 1)
                pe.wait_ge(h_ready, 2 * t + 2)
                for n in range(Y):
                    i, half = n // 2, n % 2
                    pe.wait_ge(y_free, t * Y + n + 1)
                    for c in range(2):
                        last = pe.matmul(y_ps[n % 4][:, :], hid[:, c, i * P:(i + 1) * P],
                                         wd[:, c, 4 * half:4 * half + 4, :].rearrange("p e d -> p (e d)"),
                                         start=(c == 0), stop=(c == 1))
                    last.then_inc(y_full, 1)

        @block.scalar
        def _(act):
            with act.Fori(0, B) as t:
                for c in range(2):
                    act.wait_ge(h_full, 2 * t + c + 1)
                    act.activation(hid[:, c, :], h_ps[c][:, :], ACT.Silu).then_inc(h_ready, 1)

        @block.vector
        def _(v):
            v.sem_inc(y_free, 4)
            with v.Fori(0, B) as t:
                v.tensor_copy(gs[:, :, :], k.gate[:, bass.ds(t * QT * 8, QT * 8)].rearrange("p (i e) -> p i e", e=8))\
                    .then_inc(gs_ready, 1)
                v.wait_ge(gs_ready, t + 1)
                xs = k.x[:, bass.ds(t * QT, QT), :]
                for n in range(Y):
                    i, half = n // 2, n % 2
                    v.wait_ge(y_full, t * Y + n + 1)
                    for e in range(4):
                        ins = v.scalar_tensor_tensor(xs[:, i, :], y_ps[n % 4][:, e * P:(e + 1) * P],
                                                     gs[:, i, 4 * half + e:4 * half + e + 1], xs[:, i, :],
                                                     ALU.mult, ALU.add)
                        if e < 3:
                            ins.then_inc(chain, 1)
                            v.wait_ge(chain, (t * Y + n) * 3 + e + 1)
                        else:
                            ins.then_inc(y_free, 1)
                            v.wait_ge(y_free, t * Y + n + 5)


def relative_rows(nc, k, tag, d, band):
    H, G, NB, W, HOLE = 16, 4, 10, 257, 129
    with ExitStack() as ctx:
        ph = Phase(nc, ctx, tag)
        wr = ph.sb("wr", [P, G, P])
        br = ph.sb("br", [P, G])
        rel = ph.sb("rel", [P, P])
        rT = ph.sb("rT", [P, 2, T])
        rows = ph.sb("rows", [P, 4, 4, P])
        hole = ph.sb("hole", [P, 4, QT, HOLE])
        r_ps = ph.banks("r", 2)
        e_ps = ph.banks("e", 4)
        loaded, hole_set, r_full, rT_ready, e_full, copied, written0, written1, written2, written3, filled = (
            ph.sem(s) for s in ("loaded", "hole_set", "r_full", "rT_ready", "e_full", "copied", "written0",
                                "written1", "written2", "written3", "filled"))
        written = (written0, written1, written2, written3)
        lead = band[0:P].rearrange("(a w) -> a w", a=1)
        main = band[P:P + B * H * T * W].rearrange("(h t w) -> h t w", t=T, w=W)
        block = ctx.enter_context(nc.Block())

        @block.sync
        def _(sp):
            for dst, src in ((wr[:, :, :], d["a3_wr"]), (br[:, :], d["a3_br"]), (rel[:, :], d["a3_rel"])):
                sp.dma_start(dst, src).then_inc(loaded, 16)
            with sp.Fori(0, B) as b:
                for n in range(16):
                    sp.wait_ge(copied, 16 * b + n + 1 + 4)
                    sp.dma_start(main[bass.ds(b * H + n, 1), :, 0:P].rearrange("h (i p) w -> (h p) i w", p=P),
                                 rows[:, n % 4, :, :]).then_inc(written[n % 4], 16)
            for s in written:
                sp.wait_ge(s, 16 * 16 + 16)

        @block.gpsimd
        def _(pool):
            pool.memset(hole[:, :, :, :], -1e9).then_inc(hole_set, 1)
            pool.wait_ge(hole_set, 1)
            pool.dma_start(lead, hole[0:1, 0, 0, 0:P]).then_inc(filled, 16)
            for b in range(B * H // 4):
                pool.dma_start(main[4 * b:4 * b + 4, :, P:W].rearrange("h (i p) w -> p h i w", p=P), hole[:, :, :, :])\
                    .then_inc(filled, 16)
            pool.wait_ge(filled, 16 * (1 + B * H // 4))

        @block.tensor
        def _(pe):
            pe.wait_ge(loaded, 48)
            with pe.Fori(0, B) as b:
                xs = k.xnT[:, bass.ds(b * T, T)]
                for g in range(G):
                    pe.wait_ge(rT_ready, G * b + g + 1)
                    pe.matmul(r_ps[g % 2][:, :], wr[:, g, :], xs, start=True, stop=True).then_inc(r_full, 1)
                    pe.wait_ge(rT_ready, G * b + g + 3)
                    pe.wait_ge(copied, 16 * b + 4 * g + 4)
                    for i in range(QT):
                        for j in range(4):
                            last = pe.matmul(e_ps[j][:, i * P:(i + 1) * P], rT[32 * j:32 * j + NB, g % 2, i * P:(i + 1) * P],
                                             rel[32 * j:32 * j + NB, :], start=True, stop=True)
                            if i == QT - 1:
                                last.then_inc(e_full, 1)

        @block.scalar
        def _(act):
            act.sem_inc(rT_ready, 2)
            act.wait_ge(loaded, 48)
            with act.Fori(0, B) as b:
                for g in range(G):
                    act.wait_ge(r_full, G * b + g + 1)
                    act.activation(rT[:, g % 2, :], r_ps[g % 2][:, :], ACT.Identity, bias=br[:, g:g + 1])\
                        .then_inc(rT_ready, 1)

        @block.vector
        def _(v):
            v.sem_inc(copied, 4)
            for s in written:
                v.sem_inc(s, 16)
            with v.Fori(0, B) as b:
                for n in range(16):
                    v.wait_ge(e_full, 16 * b + n + 1)
                    v.wait_ge(written[n % 4], 64 * b + 16 * (n // 4) + 16)
                    v.tensor_copy(rows[:, n % 4, :, :].rearrange("p j e -> p (j e)"), e_ps[n % 4][:, :]).then_inc(copied, 1)


def relative_heads(nc, k, tag, d, band):
    H, DH, C, W = 16, 64, 8, 257
    UNITS = H * QT
    with ExitStack() as ctx:
        ph = Phase(nc, ctx, tag)
        wq = ph.sb("wq", [P, C, P])
        wk = ph.sb("wk", [P, C, P])
        wv = ph.sb("wv", [P, 2, 512])
        wo = ph.sb("wo", [P, C, P])
        bq = ph.sb("bq", [P, C])
        bo = ph.sb("bo", [1, P])
        xb = ph.sb("xb", [P, T])
        qT = ph.sb("qT", [P, C, T])
        kT = ph.sb("kT", [P, C, T])
        val = ph.sb("val", [P, QT, H * DH])
        rel = ph.sb("rel", [P, 2, QT, 2 * P])
        lg = ph.sb("lg", [P, 2, 2 * P])
        mx = ph.sb("mx", [P, 4])
        nmax = ph.sb("nmax", [P, 4])
        spare = ph.sb("spare", [P, 2])
        prob = ph.sb("prob", [P, 2, 2 * P])
        pT = ph.sb("pT", [P, 2, QT, 2 * P])
        rsum = ph.sb("rsum", [P, 2, QT])
        rinv = ph.sb("rinv", [P, 2, QT])
        o = ph.sb("o", [P, QT, H * DH])
        oT = ph.sb("oT", [P, C, T])
        s_ps, t_ps, o_ps, m_ps = (ph.banks(s, 2) for s in ("s", "t", "o", "m"))
        loaded, xb_ready, m_full0, m_full1, m_free0, m_free1, rel_in0, rel_in1 = (ph.sem(s) for s in (
            "loaded", "xb_ready", "m_full0", "m_full1", "m_free0", "m_free1", "rel_in0", "rel_in1"))
        s_done, mx_done, max_done, exp_done, t_done, pt_copied, pv_done, o_free, rinv_ready, x_added = (
            ph.sem(s) for s in ("s_done", "mx_done", "max_done", "exp_done", "t_done", "pt_copied", "pv_done",
                                "o_free", "rinv_ready", "x_added"))
        m_full, m_free, rel_in = (m_full0, m_full1), (m_free0, m_free1), (rel_in0, rel_in1)
        M_Q, M_K, M_V, M_OT, M_Y, M_N = 0, 8, 16, 24, 32, 33
        PER = (17, 16)
        skewed = band[P - 1:P - 1 + B * H * T * W].rearrange("(h q r) -> h q r", q=QT, r=P * W)
        block = ctx.enter_context(nc.Block())

        def keys(qt):
            return (0, P) if qt == 0 else ((qt - 1) * P, 2 * P)

        @block.sync
        def _(sp):
            for dst, src in ((wq[:, :, :], d["a3_wq"]), (wk[:, :, :], d["a3_wk"]), (wv[:, :, :], d["a3_wv"]),
                             (bq[:, :], d["a3_bq"]), (wo[:, :, :], d["a3_wo"]), (bo[:, :], d["a3_bo"])):
                sp.dma_start(dst, src).then_inc(loaded, 16)
            with sp.Fori(0, B) as b:
                for h in range(H):
                    sp.wait_ge(mx_done, UNITS * b + QT * (h + 1))
                    sp.dma_start(rel[:, h % 2, :, :], skewed[bass.ds(b * H + h, 1), :, 0:2 * P * P]
                                 .rearrange("h q (t p) -> (h t) q p", p=2 * P)).then_inc(rel_in[h % 2], 16)

        @block.tensor
        def _(pe):
            pe.wait_ge(loaded, 16 * 6)
            with pe.Fori(0, B) as b:
                def m_open(m):
                    pe.wait_ge(m_free[m % 2], b * PER[m % 2] + m // 2 + 1)
                    return m_ps[m % 2]

                pe.wait_ge(xb_ready, b + 1)
                for m0, w in ((M_Q, wq), (M_K, wk)):
                    for c in range(C):
                        ps = m_open(m0 + c)
                        pe.matmul(ps[:, :], w[:, c, :], xb[:, :], start=True, stop=True).then_inc(m_full[c % 2], 1)
                for n in range(2 * QT):
                    ps = m_open(M_V + n)
                    pe.matmul(ps[:, :], xb[:, (n // 2) * P:(n // 2 + 1) * P], wv[:, n % 2, :], start=True, stop=True)\
                        .then_inc(m_full[n % 2], 1)
                for i in range(2):
                    pe.wait_ge(m_free[i], b * PER[i] + 13)

                def scores(u):
                    h, qt = u // QT, u % QT
                    k0, n = keys(qt)
                    r = slice(64 * (h % 2), 64 * (h % 2) + 64)
                    pe.wait_ge(mx_done, b * UNITS + u + QT + QT - 1)
                    pe.matmul(s_ps[u % 2][:, 0:n], qT[r, h // 2, qt * P:(qt + 1) * P], kT[r, h // 2, k0:k0 + n],
                              start=True, stop=True).then_inc(s_done, 1)

                def turn(u):
                    n = keys(u % QT)[1]
                    pe.wait_ge(exp_done, b * UNITS + u + 1)
                    pe.wait_ge(pt_copied, b * UNITS + u + 1)
                    for c in range(n // P):
                        last = pe.transpose(t_ps[u % 2][:, c * P:(c + 1) * P], prob[:, u % 2, c * P:(c + 1) * P],
                                            k.ident[:, :])
                    last.then_inc(t_done, 1)

                def values(h):
                    pe.wait_ge(pt_copied, b * UNITS + QT * (h + 1) + 2)
                    pe.wait_ge(o_free, b * H + h + 1)
                    for qt in range(QT):
                        k0, n = keys(qt)
                        for c in range(n // P):
                            last = pe.matmul(o_ps[h % 2][:, qt * DH:(qt + 1) * DH], pT[:, h % 2, qt, c * P:(c + 1) * P],
                                             val[:, k0 // P + c, h * DH:(h + 1) * DH], start=(c == 0),
                                             stop=(c == n // P - 1))
                    last.then_inc(pv_done, 1)

                for u in range(UNITS + 3):
                    if u < UNITS:
                        scores(u)
                    if 1 <= u < UNITS + 1:
                        turn(u - 1)
                    if u >= 6 and u % QT == 2:
                        values(u // QT - 1)
                pe.wait_ge(o_free, b * H + H + 2)
                for c in range(C):
                    ps = m_open(M_OT + c)
                    for qt in range(QT):
                        last = pe.transpose(ps[:, qt * P:(qt + 1) * P], o[:, qt, c * P:(c + 1) * P], k.ident[:, :])
                    last.then_inc(m_full[c % 2], 1)
                pe.wait_ge(m_free[1], b * PER[1] + 17)
                ps = m_open(M_Y)
                for qt in range(QT):
                    out = ps[:, qt * P:(qt + 1) * P]
                    for c in range(C):
                        pe.matmul(out, oT[:, c, qt * P:(qt + 1) * P], wo[:, c, :], start=(c == 0), stop=False)
                    last = pe.matmul(out, k.ones[0:1, :], bo[:, :], start=False, stop=True)
                last.then_inc(m_full[M_Y % 2], 1)

        @block.scalar
        def _(act):
            with act.Fori(0, B) as b:
                def m_wait(m):
                    act.wait_ge(m_full[m % 2], b * PER[m % 2] + m // 2 + 1)
                    return m_ps[m % 2]

                for c in range(C):
                    ps = m_wait(M_K + c)
                    act.copy(kT[:, c, :], ps[:, :]).then_inc(m_free[c % 2], 1)
                for u in range(UNITS):
                    h, qt = u // QT, u % QT
                    n = keys(qt)[1]
                    act.wait_ge(max_done, b * UNITS + u + 1)
                    act.wait_ge(t_done, b * UNITS + u + 1)
                    act.activation(prob[:, u % 2, 0:n], lg[:, u % 2, 0:n], ACT.Exp, bias=nmax[:, u % 4:u % 4 + 1],
                                   accum_out=rsum[:, h % 2, qt:qt + 1]).then_inc(exp_done, 1)
                for c in range(C):
                    ps = m_wait(M_OT + c)
                    act.copy(oT[:, c, :], ps[:, :]).then_inc(m_free[c % 2], 1)

        @block.vector
        def _(v):
            v.sem_inc(t_done, 2)
            v.sem_inc(pt_copied, 2)
            v.sem_inc(pv_done, 2)
            v.sem_inc(o_free, 2)
            v.sem_inc(m_free0, 1)
            v.sem_inc(m_free1, 1)
            v.sem_inc(mx_done, 2 * QT)
            v.wait_ge(loaded, 16 * 6)
            with v.Fori(0, B) as b:
                def m_wait(m):
                    v.wait_ge(m_full[m % 2], b * PER[m % 2] + m // 2 + 1)
                    return m_ps[m % 2]

                v.tensor_copy(xb[:, :], k.xnT[:, bass.ds(b * T, T)]).then_inc(xb_ready, 1)
                for c in range(C):
                    ps = m_wait(M_Q + c)
                    v.tensor_scalar(qT[:, c, :], ps[:, :], bq[:, c:c + 1], DH ** -0.5, ALU.add, ALU.mult)\
                        .then_inc(m_free[c % 2], 1)
                for n in range(2 * QT):
                    ps = m_wait(M_V + n)
                    v.tensor_copy(val[:, n // 2, (n % 2) * 512:(n % 2 + 1) * 512], ps[:, :]).then_inc(m_free[n % 2], 1)

                def scores_ready(u):
                    v.wait_ge(s_done, b * UNITS + u + 1)
                    if u % QT == 0:
                        v.wait_ge(rel_in[u // QT % 2], 16 * (b * (H // 2) + u // QT // 2 + 1))
                    if u >= 2:
                        v.wait_ge(exp_done, b * UNITS + u - 1)
                    else:
                        v.memset(spare[:, u:u + 1], 0.0)

                def row_max(u):
                    h, qt = u // QT, u % QT
                    n = keys(qt)[1]
                    v.tensor_tensor_reduce(lg[:, u % 2, 0:n], s_ps[u % 2][:, 0:n], rel[:, h % 2, qt, 2 * P - n:2 * P],
                                           1.0, -3.0e38, ALU.add, ALU.max, mx[:, u % 4:u % 4 + 1]).then_inc(mx_done, 1)
                    v.wait_ge(mx_done, b * UNITS + u + 1 + 2 * QT)
                    v.tensor_scalar(nmax[:, u % 4:u % 4 + 1], mx[:, u % 4:u % 4 + 1], -1.0, None, ALU.mult)\
                        .then_inc(max_done, 1)

                def copy_t(u):
                    h, qt = u // QT, u % QT
                    n = keys(qt)[1]
                    v.wait_ge(t_done, b * UNITS + u + 3)
                    if qt == 0:
                        v.wait_ge(pv_done, b * H + h + 1)
                    v.tensor_copy(pT[:, h % 2, qt, 0:n], t_ps[u % 2][:, 0:n]).then_inc(pt_copied, 1)

                def norm(h):
                    v.wait_ge(exp_done, b * UNITS + QT * (h + 1))
                    v.reciprocal(rinv[:, h % 2, :], rsum[:, h % 2, :]).then_inc(rinv_ready, 1)
                    v.wait_ge(rinv_ready, b * H + h + 1)
                    v.wait_ge(pv_done, b * H + h + 3)
                    v.tensor_tensor(o[:, :, h * DH:(h + 1) * DH],
                                    o_ps[h % 2][:, 0:QT * DH].rearrange("p (t e) -> p t e", t=QT),
                                    bc(rinv[:, h % 2, :].unsqueeze(2), [P, QT, DH]), ALU.mult).then_inc(o_free, 1)

                for u in range(UNITS + 4):
                    if u < UNITS:
                        scores_ready(u)
                    if 2 <= u < UNITS + 2:
                        copy_t(u - 2)
                    if u < UNITS:
                        row_max(u)
                    if u >= 7 and u % QT == 3:
                        norm(u // QT - 1)
                ps = m_wait(M_Y)
                xs = k.x[:, bass.ds(b * QT, QT), :]
                v.tensor_tensor(xs, ps[:, :].rearrange("p (t d) -> p t d", t=QT), xs, ALU.add)\
                    .then_inc(m_free[M_Y % 2], 1)


def switch_heads(nc, k, tag, d):
    H, E = 8, 8
    UNITS = H * QT
    order = []
    for h in range(H + 1):
        if h < H:
            order += [("q", h), ("k", h)] + [("v", h, i) for i in range(2 * QT)]
        if h >= 1:
            order += [("t", h - 1)] + [("y", h - 1, i) for i in range(2 * QT)]
    place = {name: n for n, name in enumerate(order)}
    PER = len(order) // 4
    with ExitStack() as ctx:
        ph = Phase(nc, ctx, tag)
        wq = ph.sb("wq", [P, H, P])
        wk = ph.sb("wk", [P, H, P])
        wv = ph.sb("wv", [P, 2, 2, 512])
        wo = ph.sb("wo", [P, 2, 2, 512])
        xb = ph.sb("xb", [P, T])
        gs = ph.sb("gs", [P, QT, 2, H, E])
        acc = ph.sb("acc", [P, QT, P])
        qT = ph.sb("qT", [P, 2, T])
        kT = ph.sb("kT", [P, 2, T])
        val = ph.sb("val", [P, 2, QT, P])
        nmax = ph.sb("nmax", [P, 4])
        prob = ph.sb("prob", [P, 2, T])
        pT = ph.sb("pT", [P, 2, QT, T])
        rsum = ph.sb("rsum", [P, 2, QT])
        rinv = ph.sb("rinv", [P, 2, QT])
        o = ph.sb("o", [P, 2, QT, P])
        oT = ph.sb("oT", [P, 2, T])
        s_ps = ph.banks("s", 2)
        t_ps, o_ps = ph.banks("t", 1), ph.banks("o", 1)
        m_ps = ph.banks("m", 4)
        m_full = [ph.sem(f"m_full{i}") for i in range(4)]
        m_free = [ph.sem(f"m_free{i}") for i in range(4)]
        loaded, wv_in0, wv_in1, wo_in0, wo_in1, xb_ready, gs_ready, vlink, ylink, v_ready, y_ready = (ph.sem(s) for s in (
            "loaded", "wv_in0", "wv_in1", "wo_in0", "wo_in1", "xb_ready", "gs_ready", "vlink", "ylink", "v_ready",
            "y_ready"))
        s_done, max_done, exp_done, t_done, pt_copied, pv_done, o_ready, rinv_ready, added = (
            ph.sem(s) for s in ("s_done", "max_done", "exp_done", "t_done", "pt_copied", "pv_done", "o_ready",
                                "rinv_ready", "added"))
        wv_in, wo_in = (wv_in0, wv_in1), (wo_in0, wo_in1)
        block = ctx.enter_context(nc.Block())

        @block.sync
        def _(sp):
            for dst, src in ((wq[:, :, :], d["f3_wq"]), (wk[:, :, :], d["f3_wk"])):
                sp.dma_start(dst, src).then_inc(loaded, 16)
            with sp.Fori(0, B) as b:
                for h in range(H):
                    sp.wait_ge(v_ready, b * H + h + 1)
                    sp.dma_start(wv[:, h % 2, :, :], d["f3_wv"][h]).then_inc(wv_in[h % 2], 16)
                    sp.wait_ge(y_ready, b * H + h + 1)
                    sp.dma_start(wo[:, h % 2, :, :], d["f3_wo"][h]).then_inc(wo_in[h % 2], 16)

        @block.tensor
        def _(pe):
            pe.wait_ge(loaded, 32)
            with pe.Fori(0, B) as b:
                def m_open(*name):
                    n = place[name]
                    pe.wait_ge(m_free[n % 4], b * PER + n // 4 + 1)
                    return m_ps[n % 4], m_full[n % 4]

                def m_read(*name):
                    n = place[name]
                    pe.wait_ge(m_free[n % 4], b * PER + n // 4 + 2)

                def out_products(h):
                    pe.wait_ge(o_ready, b * H + h + 1)
                    ps, full = m_open("t", h)
                    for qt in range(QT):
                        last = pe.transpose(ps[:, qt * P:(qt + 1) * P], o[:, h % 2, qt, :], k.ident[:, :])
                    last.then_inc(full, 1)
                    m_read("t", h)
                    pe.wait_ge(wo_in[h % 2], 16 * (b * (H // 2) + h // 2 + 1))
                    for i in range(2 * QT):
                        ps, full = m_open("y", h, i)
                        pe.matmul(ps[:, :], oT[:, h % 2, (i // 2) * P:(i // 2 + 1) * P], wo[:, h % 2, i % 2, :],
                                  start=True, stop=True).then_inc(full, 1)

                pe.wait_ge(xb_ready, b + 1)
                for h in range(H):
                    for kind, w in (("q", wq), ("k", wk)):
                        ps, full = m_open(kind, h)
                        pe.matmul(ps[:, :], w[:, h, :], xb[:, :], start=True, stop=True).then_inc(full, 1)
                    pe.wait_ge(wv_in[h % 2], 16 * (b * (H // 2) + h // 2 + 1))
                    for i in range(2 * QT):
                        ps, full = m_open("v", h, i)
                        pe.matmul(ps[:, :], xb[:, (i // 2) * P:(i // 2 + 1) * P], wv[:, h % 2, i % 2, :],
                                  start=True, stop=True).then_inc(full, 1)
                    m_read("q", h)
                    m_read("k", h)

                    def scores(qt):
                        u = QT * h + qt
                        pe.wait_ge(exp_done, b * UNITS + u + 1)
                        pe.matmul(s_ps[u % 2][:, :], qT[:, h % 2, qt * P:(qt + 1) * P], kT[:, h % 2, :],
                                  start=True, stop=True).then_inc(s_done, 1)

                    def turn(qt):
                        u = QT * h + qt
                        pe.wait_ge(exp_done, b * UNITS + u + 3)
                        pe.wait_ge(pt_copied, b * UNITS + u + 1)
                        for kt in range(QT):
                            last = pe.transpose(t_ps[0][:, kt * P:(kt + 1) * P], prob[:, u % 2, kt * P:(kt + 1) * P],
                                                k.ident[:, :])
                        last.then_inc(t_done, 1)

                    scores(0)
                    scores(1)
                    if h >= 1:
                        out_products(h - 1)
                    turn(0)
                    scores(2)
                    turn(1)
                    scores(3)
                    turn(2)
                    turn(3)
                    pe.wait_ge(pt_copied, b * UNITS + QT * (h + 1) + 1)
                    pe.wait_ge(v_ready, b * H + h + 3)
                    pe.wait_ge(o_ready, b * H + h) if h else None
                    for qt in range(QT):
                        for kt in range(QT):
                            last = pe.matmul(o_ps[0][:, qt * P:(qt + 1) * P], pT[:, h % 2, kt, qt * P:(qt + 1) * P],
                                             val[:, h % 2, kt, :], start=(kt == 0), stop=(kt == QT - 1))
                    last.then_inc(pv_done, 1)
                out_products(H - 1)

        @block.scalar
        def _(act):
            act.sem_inc(exp_done, 2)
            with act.Fori(0, B) as b:
                def m_wait(*name):
                    n = place[name]
                    act.wait_ge(m_full[n % 4], b * PER + n // 4 + 1)
                    return m_ps[n % 4], m_free[n % 4]

                def exps(h, qt):
                    u = QT * h + qt
                    act.wait_ge(max_done, b * UNITS + u + 1)
                    act.wait_ge(t_done, b * UNITS + u + 1)
                    act.activation(prob[:, u % 2, :], s_ps[u % 2][:, :], ACT.Exp, bias=nmax[:, u % 4:u % 4 + 1],
                                   accum_out=rsum[:, h % 2, qt:qt + 1]).then_inc(exp_done, 1)

                def turned(h):
                    ps, free = m_wait("t", h)
                    act.copy(oT[:, h % 2, :], ps[:, :]).then_inc(free, 1)

                for h in range(H):
                    ps, free = m_wait("q", h)
                    act.mul(qT[:, h % 2, :], ps[:, :], float(P) ** -0.5).then_inc(free, 1)
                    ps, free = m_wait("k", h)
                    act.copy(kT[:, h % 2, :], ps[:, :]).then_inc(free, 1)
                    exps(h, 0)
                    exps(h, 1)
                    if h >= 1:
                        turned(h - 1)
                    exps(h, 2)
                    exps(h, 3)
                turned(H - 1)

        @block.vector
        def _(v):
            v.sem_inc(t_done, 2)
            v.sem_inc(pt_copied, 1)
            v.sem_inc(v_ready, 2)
            v.sem_inc(y_ready, 2)
            for s in m_free:
                v.sem_inc(s, 1)
            VL = H * (2 * QT * 4 - QT)
            YL = H * (2 * QT * 4)
            with v.Fori(0, B) as b:
                links = {"v": 0, "y": 0}

                def m_wait(*name):
                    n = place[name]
                    v.wait_ge(m_full[n % 4], b * PER + n // 4 + 1)
                    return m_ps[n % 4], m_free[n % 4]

                v.tensor_copy(xb[:, :], k.xnT[:, bass.ds(b * T, T)]).then_inc(xb_ready, 1)
                v.tensor_copy(gs[:, :, :, :, :].rearrange("p i s h e -> p (i s h e)"),
                              k.gate[:, bass.ds(b * QT * 2 * H * E, QT * 2 * H * E)]).then_inc(gs_ready, 1)
                v.wait_ge(gs_ready, 2 * b + 1)
                v.tensor_copy(acc[:, :, :], k.x[:, bass.ds(b * QT, QT), :]).then_inc(gs_ready, 1)
                v.wait_ge(gs_ready, 2 * b + 2)

                def gather_values(h):
                    for i in range(2 * QT):
                        ps, free = m_wait("v", h, i)
                        out = val[:, h % 2, i // 2, :]
                        for e in range(4):
                            g = gs[:, i // 2, 0, h, 4 * (i % 2) + e:4 * (i % 2) + e + 1]
                            if i % 2 == 0 and e == 0:
                                ins = v.tensor_scalar(out, ps[:, 0:P], g, None, ALU.mult)
                            else:
                                ins = v.scalar_tensor_tensor(out, ps[:, e * P:(e + 1) * P], g, out, ALU.mult, ALU.add)
                            if e == 3:
                                ins.then_inc(free, 1)
                                n = place[("v", h, i)]
                                v.wait_ge(free, b * PER + n // 4 + 2)
                            else:
                                links["v"] += 1
                                ins.then_inc(vlink, 1)
                                v.wait_ge(vlink, b * H * 6 * QT + links["v"])
                    v.sem_inc(v_ready, 1)

                def gather_out(h):
                    for i in range(2 * QT):
                        ps, free = m_wait("y", h, i)
                        out = acc[:, i // 2, :]
                        for e in range(4):
                            g = gs[:, i // 2, 1, h, 4 * (i % 2) + e:4 * (i % 2) + e + 1]
                            ins = v.scalar_tensor_tensor(out, ps[:, e * P:(e + 1) * P], g, out, ALU.mult, ALU.add)
                            if e == 3:
                                ins.then_inc(free, 1)
                                n = place[("y", h, i)]
                                v.wait_ge(free, b * PER + n // 4 + 2)
                            else:
                                links["y"] += 1
                                ins.then_inc(ylink, 1)
                                v.wait_ge(ylink, b * H * 6 * QT + links["y"])
                    v.sem_inc(y_ready, 1)

                for h in range(H):
                    gather_values(h)

                    def row_max(qt):
                        u = QT * h + qt
                        v.wait_ge(s_done, b * UNITS + u + 1)
                        v.tensor_reduce(nmax[:, u % 4:u % 4 + 1], s_ps[u % 2][:, :], AX.X, ALU.max, negate=True)\
                            .then_inc(max_done, 1)

                    def copy_t(qt):
                        u = QT * h + qt
                        v.wait_ge(t_done, b * UNITS + u + 3)
                        v.tensor_copy(pT[:, h % 2, :, qt * P:(qt + 1) * P],
                                      t_ps[0][:, :].rearrange("p (a q) -> p a q", q=P)).then_inc(pt_copied, 1)

                    row_max(0)
                    row_max(1)
                    if h >= 1:
                        gather_out(h - 1)
                    copy_t(0)
                    row_max(2)
                    copy_t(1)
                    row_max(3)
                    copy_t(2)
                    copy_t(3)
                    v.wait_ge(exp_done, b * UNITS + QT * (h + 1) + 2)
                    v.reciprocal(rinv[:, h % 2, :], rsum[:, h % 2, :]).then_inc(rinv_ready, 1)
                    v.wait_ge(rinv_ready, b * H + h + 1)
                    v.wait_ge(pv_done, b * H + h + 1)
                    v.tensor_tensor(o[:, h % 2, :, :], o_ps[0][:, :].rearrange("p (t e) -> p t e", t=QT),
                                    bc(rinv[:, h % 2, :].unsqueeze(2), [P, QT, P]), ALU.mult).then_inc(o_ready, 1)
                gather_out(H - 1)
                v.tensor_copy(k.x[:, bass.ds(b * QT, QT), :], acc[:, :, :]).then_inc(added, 1)
                v.wait_ge(added, b + 1)


def layer3(nc, k, d):
    token_logits(nc, k, "r3", d["f3_wr"], P)
    top2_gates(nc, k, "g3", 16, "sigmoid", scale_dram=d["f3_scale"])
    band = nc.dram_tensor("band", (P + B * 16 * T * 257,), F32, kind="Internal").ap()
    relative_rows(nc, k, "b3", d, band)
    switch_heads(nc, k, "f3", d)
    relative_heads(nc, k, "a3", d, band)


def layer3_layout(a, d):
    f = np.float32
    z = np.zeros((P, 4, 4, 32), f)
    z[..., 0:10] = a["L3_attn_Wr"].reshape(P, 4, 4, 10)
    d["a3_wr"] = z.reshape(P, 4, P)
    z = np.zeros((4, 4, 32), f)
    z[..., 0:10] = a["L3_attn_br"].reshape(4, 4, 10)
    d["a3_br"] = z.reshape(4, P).T
    z = np.zeros((4, 32, P), f)
    z[:, 0:10, :] = a["L3_attn_b_nd"][None, :, ::-1]
    d["a3_rel"] = z.reshape(P, P)
    d["a3_wq"], d["a3_wk"] = (a["L3_attn_" + n].reshape(P, 8, P) for n in ("Wq", "Wk"))
    d["a3_wv"] = a["L3_attn_Wv"].reshape(P, 2, 512)
    d["a3_bq"] = a["L3_attn_bq"].reshape(8, P).T
    d["a3_wo"] = a["L3_attn_Wproj"].reshape(8, P, P).transpose(1, 0, 2)
    d["a3_bo"] = a["L3_attn_bproj"][None]
    d["f3_wr"] = np.concatenate([a["L3_ffn_sel_v_w"], a["L3_ffn_sel_o_w"]]).T
    d["f3_scale"] = np.tile(a["L3_ffn_route_scale"], (P, 1))
    d["f3_wq"], d["f3_wk"] = (a["L3_ffn_" + n].reshape(8, P, P).transpose(2, 0, 1) for n in ("q_w", "k_w"))
    for n, s in (("f3_wv", "v_w"), ("f3_wo", "o_w")):
        d[n] = a["L3_ffn_" + s].reshape(8, 2, 4, P, P).transpose(0, 3, 1, 2, 4).reshape(8, P, 2, 512)

STOP = 6



class State:
    pass


def program(nc, d, out, stop_after):
    with ExitStack() as ctx:
        def sb(name, shape, dtype=F32):
            return ctx.enter_context(nc.sbuf_tensor(name, shape, dtype))

        k = State()
        Phase.counted = []
        k.x = sb("x", [P, NT, P])
        k.xn = sb("xn", [P, NT, P])
        k.xnT = sb("xnT", [P, N])
        k.ident = sb("ident", [P, P])
        k.ident_bf = sb("ident_bf", [P, P], BF16)
        k.ones = sb("ones", [1, P])
        k.ones_bf = sb("ones_bf", [P, P], BF16)
        k.earlier = sb("earlier", [P, P], BF16)
        k.later = sb("later", [P, P], BF16)
        k.iota = sb("iota", [P, 64])
        k.logits = sb("logits", [P, NT * P])

        with ExitStack() as c1:
            ph = Phase(nc, c1, "setup")
            tmp = ph.sb("tmp", [P, 2, P])
            loaded, made = ph.sem("loaded"), ph.sem("made")
            block = c1.enter_context(nc.Block())

            @block.sync
            def _(sp):
                for dst, src in ((k.x[:, :, :], d["x"].rearrange("(t p) d -> p t d", p=P)), (k.ident[:, :], d["ident"]),
                                 (tmp[:, 0, :], d["earlier"]), (tmp[:, 1, :], d["later"]), (k.iota[:, :], d["iota"])):
                    sp.dma_start(dst, src).then_inc(loaded, 16)

            @block.vector
            def _(v):
                v.memset(k.ones[:, :], 1.0).then_inc(made, 1)
                v.memset(k.ones_bf[:, :], 1.0).then_inc(made, 1)
                v.wait_ge(loaded, 80)
                v.tensor_copy(k.ident_bf[:, :], k.ident[:, :]).then_inc(made, 1)
                v.tensor_copy(k.earlier[:, :], tmp[:, 0, :]).then_inc(made, 1)
                v.tensor_copy(k.later[:, :], tmp[:, 1, :]).then_inc(made, 1)
                v.wait_ge(made, 5)

        layer_norm(nc, k, "n0")
        if stop_after >= 0:
          small_heads(nc, k, "a0", d["a0_wq"], d["a0_wk"], d["a0_wv"], d["a0_wo"], d["a0_bq"], d["a0_bk"], d["a0_rs"],
                    d["a0_bv"], d["a0_bo"], None, None)
        if stop_after >= 1:
          token_logits(nc, k, "r0", d["f0_wr"], 64)
          with ExitStack() as c2:
            k.weight = c2.enter_context(nc.sbuf_tensor("weight", [P, NT, 64], F32))
            k.place = c2.enter_context(nc.sbuf_tensor("place", [P, NT, 64], F32))
            k.slots_x = c2.enter_context(nc.sbuf_tensor("slots_x", [P, 64 * 32], F32))
            k.slots_y = c2.enter_context(nc.sbuf_tensor("slots_y", [P, 16, P], F32))
            top8_slots(nc, k, "p0")
            slot_dispatch(nc, k, "d0")
            slot_experts(nc, k, "e0", d["f0_wgu"], d["f0_wd"])
            slot_combine(nc, k, "c0")
        if stop_after >= 2:
          Phase.retire(nc)
          layer_norm(nc, k, "n1")
          small_heads(nc, k, "a1", d["a1_wq"], d["a1_wk"], d["a1_wv"], d["a1_wo"], d["a1_bz"], d["a1_bz"], d["a1_rs"],
                    d["a1_br"], d["a1_br"], (d["a1_fa"], d["a1_fk"], d["a1_trig"]), k.later)
        if stop_after >= 3:
          with ExitStack() as c2:
            k.gate = c2.enter_context(nc.sbuf_tensor("gate1", [P, NT * 8], F32))
            token_logits(nc, k, "r1", d["f1_wr"], 8, d["f1_br"])
            top2_gates(nc, k, "g1", 1, "softmax2")
            gated_ffn(nc, k, "f1", d["f1_w0"], d["f1_w1"], d["f1_w2"], d["f1_b0"], d["f1_b1"], d["f1_b2"])
        if stop_after >= 4:
          Phase.retire(nc)
          layer_norm(nc, k, "n2")
          selective_scan(nc, k, "s2", {n[3:]: a for n, a in d.items() if n.startswith("s2_")})
        if stop_after >= 5:
          with ExitStack() as c2:
            k.gate = c2.enter_context(nc.sbuf_tensor("gate2", [P, NT * 8], F32))
            token_logits(nc, k, "r2", d["f2_wr"], 8)
            top2_gates(nc, k, "g2", 1, "capacity", capacity=N * 5 // 32)
            shared_ffn(nc, k, "f2", d["f2_wg"], d["f2_wd"])
        if stop_after >= 6:
          Phase.retire(nc)
          layer_norm(nc, k, "n3")
          with ExitStack() as c2:
            k.gate = c2.enter_context(nc.sbuf_tensor("gate3", [P, NT * P], F32))
            layer3(nc, k, d)

        with ExitStack() as c1:
            ph = Phase(nc, c1, "store")
            stored = ph.sem("stored")
            block = c1.enter_context(nc.Block())

            @block.sync
            def _(sp):
                sp.dma_start(out.rearrange("b (t p) d -> p (b t) d", p=P), k.x[:, :, :]).then_inc(stored, 16)
                sp.wait_ge(stored, 16)


def laid_out(a):
    def heads(w):
        z = np.zeros((w.shape[0], 4, 4, 32), np.float32)
        z[:, :, :, 0:8] = w.reshape(w.shape[0], 4, 4, 8)
        return z.reshape(w.shape[0], 4, 128)

    def col(v, n):
        return np.ascontiguousarray(v.reshape(n, 128).T)

    d = {}
    f = np.float32
    d["x"] = a["L0_attn_x"].reshape(N, P)
    d["ident"] = np.eye(P, dtype=f)
    d["earlier"] = np.triu(np.ones((P, P), f), 1)
    d["later"] = np.triu(np.full((P, P), -BIG, f), 1)
    d["iota"] = np.tile(np.arange(64, dtype=f), (P, 1))
    w, bias = a["L0_attn_qkv_w"], a["L0_attn_qkv_b"]
    d["a0_wq"], d["a0_wk"], d["a0_wv"] = heads(w[:, 0:128]), heads(w[:, 128:256]), w[:, 256:384]
    d["a0_bq"], d["a0_bk"] = (np.ascontiguousarray(heads(bias[None, i:i + 128])[0].T) for i in (0, 128))
    d["a0_bv"], d["a0_bo"] = bias[None, 256:384], a["L0_attn_proj_b"][None]
    d["a0_wo"] = a["L0_attn_proj_w"]
    d["a0_rs"] = np.full((P, 1), 8 ** -0.5, f)
    d["f0_wr"] = a["L0_ffn_gate_w"].T
    gu = np.concatenate([a["L0_ffn_w_gate"], a["L0_ffn_w_up"]], axis=1)
    d["f0_wgu"] = gu.reshape(16, 4, 192, P).transpose(0, 3, 1, 2)
    d["f0_wd"] = a["L0_ffn_w_down"].reshape(16, 4, P, 96).transpose(0, 3, 1, 2)
    w = a["L1_attn_Wqkv"].T
    d["a1_wq"], d["a1_wk"], d["a1_wv"] = heads(w[:, 0:128]), heads(w[:, 128:256]), w[:, 256:384]
    d["a1_bz"], d["a1_br"] = np.zeros((P, 4), f), np.zeros((1, P), f)
    d["a1_wo"] = a["L1_attn_Wout"].T
    rs = np.ones((4, 32), f)
    rs[:, 0:8] = 8 ** -0.5
    d["a1_rs"] = rs.reshape(P, 1)
    fa, fk = np.zeros((12, 4, 4, 32), f), np.zeros((12, 4, 4, 32), f)
    al, be = a["L1_attn_alpha"].reshape(4, 4, 4), a["L1_attn_beta"].reshape(4, 4, 4)
    for r in range(4):
        fa[r, :, :, 8 + r], fa[4 + r, :, :, 8 + r] = al[:, :, r], be[:, :, r]
        fa[4 + r, :, :, 12 + r], fa[8 + r, :, :, 12 + r] = al[:, :, r], be[:, :, r]
        fk[r, :, :, 8 + r], fk[4 + r, :, :, 12 + r] = 1.0, 1.0
    d["a1_fa"], d["a1_fk"] = fa.reshape(12, 4, P), fk.reshape(12, 4, P)
    ang = (10000.0 ** (-2.0 * np.arange(4) / 8))[:, None] * np.arange(T)[None, :]
    d["a1_trig"] = np.concatenate([np.cos(ang), np.sin(ang), -np.cos(ang)]).astype(f)
    d["f1_wr"], d["f1_br"] = a["L1_ffn_Wg"], a["L1_ffn_bg"][None]
    for n, s in (("f1_w0", "W0"), ("f1_w1", "W1")):
        d[n] = a["L1_ffn_" + s].reshape(8, P, 4, P).transpose(1, 0, 2, 3)
    d["f1_w2"] = a["L1_ffn_W2"].reshape(8, 4, P, P).transpose(2, 0, 1, 3)
    d["f1_b0"], d["f1_b1"] = col(a["L1_ffn_b0"], 32), col(a["L1_ffn_b1"], 32)
    d["f1_b2"] = a["L1_ffn_b2"]
    d["s2_w_in"], d["s2_w_x"] = a["L2_attn_in_proj_w"].T, a["L2_attn_x_proj_w"].T
    d["s2_w_dt"], d["s2_w_o"] = a["L2_attn_dt_proj_w"].T, a["L2_attn_out_proj_w"].T
    d["s2_b_o"], d["s2_b_in"] = a["L2_attn_out_proj_b"][None], col(a["L2_attn_in_proj_b"], 2)
    xb = a["L2_attn_x_proj_b"]
    d["s2_b_dl"], d["s2_b_bc"] = xb[0:16, None], col(xb[16:], 2)
    d["s2_b_dt"], d["s2_dpar"], d["s2_a_log"] = a["L2_attn_dt_proj_b"][:, None], a["L2_attn_D_param"][:, None], a["L2_attn_A_log"]
    d["f2_wr"] = a["L2_ffn_w_router"].T
    d["f2_wg"] = a["L2_ffn_w_gate"].T.reshape(P, 2, P)
    d["f2_wd"] = a["L2_ffn_w_down"].transpose(2, 0, 1).reshape(2, P, 8, P).transpose(1, 0, 2, 3)
    layer3_layout(a, d)
    return {n: np.ascontiguousarray(v) for n, v in d.items()}


def kernel(**inputs):
    import concourse.bacc as bacc
    from concourse.bass_utils import run_bass_kernel_spmd

    nc = bacc.Bacc("TRN2", target_bir_lowering=False, num_devices=1)
    nc.disable_value_cache = True
    arrays = laid_out({n: np.asarray(v) for n, v in inputs.items()})
    aps = {n: nc.dram_tensor(f"{n}_in", v.shape, F32, kind="ExternalInput").ap() for n, v in arrays.items()}
    out = nc.dram_tensor("out_dram", (B, T, P), F32, kind="ExternalOutput").ap()
    program(nc, aps, out, STOP)
    r = run_bass_kernel_spmd(nc, [{f"{n}_in": v for n, v in arrays.items()}], core_ids=[0])
    return r.results[0]["out_dram"]
```

```python
from contextlib import ExitStack

import numpy as np

import concourse.bass as bass
from concourse import mybir

F32 = mybir.dt.float32
BF16 = mybir.dt.bfloat16
I32 = mybir.dt.int32
ALU = mybir.AluOpType
ACT = mybir.ActivationFunctionType
AX = mybir.AxisListType

P = 128
B, T = 4, 512
N = B * T
NT = N // P
QT = T // P
EPS = 1e-5
BIG = 1.0e30


def bc(ap, shape):
    return ap.broadcast_to(shape)


class Phase:

    counted = []

    def __init__(self, nc, ctx, tag):
        self.nc, self.ctx, self.tag = nc, ctx, tag

    def sem(self, name):
        s = self.nc.alloc_semaphore(f"{self.tag}_{name}")
        self.counted.append(s)
        return s

    @classmethod
    def retire(cls, nc):
        nc.clear_and_free_semaphores(cls.counted)
        cls.counted = []
        nc.all_engine_barrier()

    def sb(self, name, shape, dtype=F32):
        return self.ctx.enter_context(self.nc.sbuf_tensor(f"{self.tag}_{name}", shape, dtype))

    def banks(self, name, n):
        return [self.ctx.enter_context(self.nc.psum_tensor(f"{self.tag}_{name}{i}", [P, 512], F32)) for i in range(n)]


def layer_norm(nc, k, tag):
    with ExitStack() as ctx:
        ph = Phase(nc, ctx, tag)
        stats = ph.sb("stats", [P, NT, 6])
        mv = ph.sb("mv", [P, NT, 2])
        ve = ph.sb("ve", [P, NT])
        std = ph.sb("std", [P, NT])
        y = ph.sb("y", [P, NT])
        t = ph.sb("t", [P, NT])
        tps = ph.banks("tps", 4)
        chain, var_ready, std_ready, xn_ready, turned = (ph.sem(s) for s in (
            "chain", "var_ready", "std_ready", "xn_ready", "turned"))
        copied = ph.sem("copied")
        block = ctx.enter_context(nc.Block())

        @block.vector
        def _(v):
            done = [0]

            def link(ins):
                done[0] += 1
                ins.then_inc(chain, 1)

            def settle():
                v.wait_ge(chain, done[0])

            for i in range(NT):
                link(v.bn_stats(stats[:, i, :], k.x[:, i, :]))
            settle()
            for i in range(NT):
                link(v.bn_aggr(mv[:, i, :], stats[:, i, :]))
            settle()
            v.tensor_scalar(ve[:, :], mv[:, :, 1], EPS, None, ALU.add).then_inc(var_ready, 1)
            v.wait_ge(std_ready, 1)
            link(v.reciprocal(y[:, :], std[:, :]))
            settle()
            for _ in range(2):
                link(v.tensor_tensor(t[:, :], y[:, :], y[:, :], ALU.mult))
                settle()
                link(v.tensor_tensor(t[:, :], t[:, :], ve[:, :], ALU.mult))
                settle()
                link(v.tensor_scalar(t[:, :], t[:, :], -0.5, 1.5, ALU.mult, ALU.add))
                settle()
                link(v.tensor_tensor(y[:, :], y[:, :], t[:, :], ALU.mult))
                settle()
            for i in range(NT):
                v.tensor_scalar(k.xn[:, i, :], k.x[:, i, :], mv[:, i, 0:1], y[:, i:i + 1],
                                ALU.subtract, ALU.mult).then_inc(xn_ready, 1)

        @block.tensor
        def _(pe):
            for i in range(NT):
                pe.wait_ge(xn_ready, i + 1)
                pe.transpose(tps[i // 4][:, (i % 4) * P:(i % 4 + 1) * P], k.xn[:, i, :],
                             k.ident[:, :]).then_inc(turned, 1)

        @block.scalar
        def _(act):
            act.wait_ge(var_ready, 1)
            act.activation(std[:, :], ve[:, :], ACT.Sqrt).then_inc(std_ready, 1)
            for j in range(4):
                act.wait_ge(turned, 4 * j + 4)
                act.copy(k.xnT[:, j * 512:(j + 1) * 512], tps[j][:, :]).then_inc(copied, 1)
            act.wait_ge(copied, 4)


PAIRS = ((0, 0), (0, 1), (1, 0), (1, 1), (0, 2), (2, 0))


def split_heads(nc, k, tag, w_q, w_k, w_v, q_bias, k_bias, v_bias, scale, parts, fourier):
    with ExitStack() as ctx:
        ph = Phase(nc, ctx, tag)
        wq, wk, wv = (ph.sb(s, [P, P]) for s in ("wq", "wk", "wv"))
        qb, kb = ph.sb("qb", [P, 1]), ph.sb("kb", [P, 1])
        vb = ph.sb("vb", [1, P])
        whole = ph.sb("whole", [P, 2, N])
        rest = ph.sb("rest", [P, 2, N])
        part = ph.sb("part", [P, 2, 3, N], BF16)
        q_ps, k_ps = ph.banks("q", 2), ph.banks("k", 2)
        v_ps = ph.banks("v", 3 if fourier else 4)
        NV = len(v_ps)
        loaded, full_q, full_k, full_v, read_q, read_k, read_v, c1, c2, c3, c4, stored = (ph.sem(s) for s in (
            "loaded", "full_q", "full_k", "full_v", "read_q", "read_k", "read_v", "first", "rest1", "second",
            "third", "stored"))
        n_loads = 6
        if fourier:
            fa, trig = ph.sb("fa", [12, P]), ph.sb("trig", [12, T])
            f_whole, f_rest = ph.sb("f_whole", [P, T]), ph.sb("f_rest", [P, 2, T])
            f_part = ph.sb("f_part", [P, 2, 3, T], BF16)
            f_ps = ph.banks("f", 1)[0]
            full_f, f_chain = ph.sem("full_f"), ph.sem("f_chain")
            n_loads += 2
        block = ctx.enter_context(nc.Block())

        @block.sync
        def _(sp):
            pairs = [(wq[:, :], w_q), (wk[:, :], w_k), (wv[:, :], w_v), (qb[:, :], q_bias), (kb[:, :], k_bias),
                     (vb[:, :], v_bias)]
            if fourier:
                pairs += [(fa[:, :], fourier[0]), (trig[:, :], fourier[1])]
            for dst, src in pairs:
                sp.dma_start(dst, src).then_inc(loaded, 16)
            for i, sem in ((0, c1), (1, c3), (2, c4)):
                for s in range(2):
                    sp.wait_ge(sem, 2)
                    sp.dma_start(parts[s, i], part[:, s, i, :]).then_inc(stored, 16)
            n = 6
            if fourier:
                sp.wait_ge(f_chain, 9)
                sp.dma_start(fourier[2][0].rearrange("i h t -> h i t"), f_part[:, 0, :, :]).then_inc(stored, 16)
                sp.dma_start(fourier[2][1, :, 0:8].rearrange("i h t -> h i t"), f_part[0:8, 1, :, :]).then_inc(stored, 16)
                n = 8
            sp.wait_ge(stored, 16 * n)

        @block.tensor
        def _(pe):
            pe.wait_ge(loaded, 16 * n_loads)
            if fourier:
                pe.matmul(f_ps[:, :], fa[:, :], trig[:, :], start=True, stop=True).then_inc(full_f, 1)
            for c in range(B):
                for w, ps, full, read in ((wq, q_ps, full_q, read_q), (wk, k_ps, full_k, read_k)):
                    if c >= 2:
                        pe.wait_ge(read, c - 1)
                    pe.matmul(ps[c % 2][:, :], w[:, :], k.xnT[:, c * T:(c + 1) * T], start=True, stop=True)\
                        .then_inc(full, 1)
            for c in range(B):
                if c >= NV:
                    pe.wait_ge(read_v, c - NV + 1)
                for i in range(QT):
                    out = v_ps[c % NV][:, i * P:(i + 1) * P]
                    pe.matmul(out, k.xnT[:, (c * QT + i) * P:(c * QT + i + 1) * P], wv[:, :], start=True, stop=False)
                    last = pe.matmul(out, k.ones[0:1, :], vb[:, :], start=False, stop=True)
                last.then_inc(full_v, 1)

        @block.scalar
        def _(act):
            act.wait_ge(loaded, 16 * n_loads)
            for c in range(B):
                act.wait_ge(full_k, c + 1)
                act.activation(whole[:, 1, c * T:(c + 1) * T], k_ps[c % 2][:, :], ACT.Identity, bias=kb[:, 0:1])\
                    .then_inc(read_k, 1)
            act.wait_ge(read_k, B)
            act.copy(part[:, 1, 0, :], whole[:, 1, :]).then_inc(c1, 1)
            for c in range(B):
                act.wait_ge(full_v, c + 1)
                act.copy(k.v[:, c * QT:(c + 1) * QT, :].rearrange("p i d -> p (i d)"), v_ps[c % NV][:, :])\
                    .then_inc(read_v, 1)
            for s, sem in ((1, c2), (0, c2)):
                act.wait_ge(sem, 2 - s)
                act.copy(part[:, s, 1, :], rest[:, s, :]).then_inc(c3, 1)
            act.wait_ge(read_v, B)

        @block.vector
        def _(v):
            v.wait_ge(loaded, 16 * n_loads)
            for c in range(B):
                v.wait_ge(full_q, c + 1)
                v.tensor_scalar(whole[:, 0, c * T:(c + 1) * T], q_ps[c % 2][:, :], qb[:, 0:1], scale, ALU.add, ALU.mult)\
                    .then_inc(read_q, 1)
            v.wait_ge(read_q, B)
            v.tensor_copy(part[:, 0, 0, :], whole[:, 0, :]).then_inc(c1, 1)
            v.wait_ge(c1, 2)
            for s in (1, 0):
                v.tensor_tensor(rest[:, s, :], whole[:, s, :], part[:, s, 0, :], ALU.subtract).then_inc(c2, 1)
            if fourier:
                v.wait_ge(full_f, 1)
                n = [0]

                def link(ins):
                    n[0] += 1
                    ins.then_inc(f_chain, 1)
                    v.wait_ge(f_chain, n[0])

                link(v.tensor_copy(f_whole[:, :], f_ps[:, :]))
                for s, rows, src in ((0, P, f_whole), (1, 8, trig)):
                    link(v.tensor_copy(f_part[0:rows, s, 0, :], src[0:rows, :]))
                    link(v.tensor_tensor(f_rest[0:rows, s, :], src[0:rows, :], f_part[0:rows, s, 0, :], ALU.subtract))
                    link(v.tensor_copy(f_part[0:rows, s, 1, :], f_rest[0:rows, s, :]))
                    link(v.tensor_tensor(f_part[0:rows, s, 2, :], f_rest[0:rows, s, :], f_part[0:rows, s, 1, :],
                                         ALU.subtract))
            v.wait_ge(c3, 2)
            for s in (1, 0):
                v.tensor_tensor(part[:, s, 2, :], rest[:, s, :], part[:, s, 1, :], ALU.subtract).then_inc(c4, 1)


def small_heads(nc, k, tag, parts, w_out, out_bias, f_parts, causal):
    H, G, DH = 16, 4, 8
    ROWS = 16 if f_parts is not None else 8
    KS = len(PAIRS) * ROWS
    MR = -(-KS // 32) * 32
    KT = MR + 3
    with ExitStack() as ctx:
        ph = Phase(nc, ctx, tag)
        wo = ph.sb("wo", [P, P])
        ob = ph.sb("ob", [1, P])
        qp = ph.sb("qp", [P, H, T], BF16)
        kp = ph.sb("kp", [P, H, T], BF16)
        vp = ph.sb("vp", [P, G, QT, 4, 32])
        nmax = ph.sb("nmax", [P, 4, QT])
        zero = ph.sb("zero", [P, QT])
        mrest = ph.sb("mrest", [P, 2, QT])
        m3 = ph.sb("m3", [P, 2, QT, 3], BF16)
        pT = ph.sb("pT", [P, 2, 4, QT, T])
        rinv = ph.sb("rinv", [P, QT, 4])
        og = ph.sb("og", [P, T])
        o = ph.sb("o", [P, QT, P])
        oT = ph.sb("oT", [P, T])
        s_ps = ph.banks("s", 2)
        st_ps = [ctx.enter_context(nc.psum_tensor(f"{tag}_st{i}", [P, 2, 512], F32)) for i in range(2)]
        o_ps, m_ps = ph.banks("o", 1)[0], ph.banks("m", 1)[0]
        loaded, fixed_in, filled = (ph.sem(s) for s in ("loaded", "fixed_in", "filled"))
        heads_in = [ph.sem(f"heads_in{c}") for c in range(4)]
        s_done, max_done, split_done, mchain, mt_full, mt_read, st_done, exp_done, pv_done, v_in, og_read = (
            ph.sem(s) for s in ("s_done", "max_done", "split_done", "mchain", "mt_full", "mt_read", "st_done",
                                "exp_done", "pv_done", "v_in", "og_read"))
        og_full, to_full, to_read, rinv_ready, ot_full, ot_read, y_full, y_read = (ph.sem(s) for s in (
            "og_full", "to_full", "to_read", "rinv_ready", "ot_full", "ot_read", "y_full", "y_read"))
        block = ctx.enter_context(nc.Block())
        n_fixed = 2 * len(PAIRS) if f_parts is not None else 0
        LOADS = 2 * len(PAIRS) * 16

        def run(eng, step):
            for h in range(H):
                step(0, h, lambda i: i >= 0)
            with eng.Fori(1, B) as b:
                for h in range(H):
                    step(b, h, lambda i: True)
            for h in range(H):
                step(B, h, lambda i: i < 0)

        @block.sync
        def _(sp):
            sp.dma_start(wo[:, :], w_out).then_inc(loaded, 16)
            sp.dma_start(ob[:, :], out_bias).then_inc(loaded, 16)
            sp.wait_ge(filled, 6)
            if f_parts is not None:
                for c, (i, j) in enumerate(PAIRS):
                    r = slice(ROWS * c + DH, ROWS * c + 2 * DH)
                    sp.dma_start(qp[r, :, :], f_parts[0, i].rearrange("(h r) t -> r h t", r=DH)).then_inc(fixed_in, 16)
                    sp.dma_start(kp[r, :, :], bc(f_parts[1, j, 0:DH].unsqueeze(1), [DH, H, T])).then_inc(fixed_in, 16)

            def load(b, g):
                for c, (i, j) in enumerate(PAIRS):
                    r = slice(ROWS * c, ROWS * c + DH)
                    for dst, s, part in ((qp, 0, i), (kp, 1, j)):
                        sp.dma_start(dst[r, 4 * g:4 * g + 4, :],
                                     parts[s, part, 32 * g:32 * g + 32, bass.ds(b * T, T)]
                                     .rearrange("(h r) t -> r h t", r=DH)).then_inc(heads_in[g], 16)

            for g in range(G):
                load(0, g)
            with sp.Fori(1, B) as b:
                for g in range(G):
                    sp.wait_ge(st_done, (b - 1) * 2 * H + 2 * (4 * g + 4))
                    load(b, g)

        @block.tensor
        def _(pe):
            pe.wait_ge(loaded, 32)
            if n_fixed:
                pe.wait_ge(fixed_in, 16 * n_fixed)

            def misc_free(b, h, after_mt):
                ended = isinstance(b, int) and b == B
                pe.wait_ge(mt_read, B * H + 1 if ended and h else b * H + h + (1 if after_mt else 0))
                pe.wait_ge(to_read, b * G + min((h - 12) // 4, -1 if ended else h) + 4)
                pe.wait_ge(ot_read, b + (1 if h > 10 else 0) + 1)
                pe.wait_ge(y_read, b + (1 if h > 12 else 0) + 1)

            def step(b, h, live):
                def scores(qt):
                    u = QT * h + qt
                    if qt == 0 and h % 4 == 0:
                        pe.wait_ge(heads_in[h // 4], (b + 1) * LOADS)
                    pe.wait_ge(max_done, b * H * QT + u + 1)
                    n = (qt + 1) * P if causal else T
                    last = pe.matmul(s_ps[u % 2][:, 0:n], qp[0:KS, h, qt * P:(qt + 1) * P], kp[0:KS, h, 0:n],
                                     start=True, stop=not causal)
                    if causal:
                        last = pe.matmul(s_ps[u % 2][:, n - P:n], k.ident_bf[:, :], k.later[:, :],
                                         start=False, stop=True)
                    last.then_inc(s_done, 1)

                def maxima(i):
                    pe.wait_ge(split_done, b * H + i + 1)
                    misc_free(b, h, False)
                    for qt in range(QT):
                        last = pe.matmul(m_ps[MR:MR + 3, qt * P:(qt + 1) * P], m3[:, i % 2, qt, :], k.ident_bf[:, :],
                                         start=True, stop=True)
                    last.then_inc(mt_full, 1)

                def turned_scores(i, pair):
                    if pair == 0:
                        pe.wait_ge(mt_read, b * H + i + 2)
                    pe.wait_ge(exp_done, b * 2 * H + 2 * i + pair + 1)
                    for kt in (2 * pair, 2 * pair + 1):
                        q0 = kt * P if causal else 0
                        out = st_ps[pair][:, kt % 2, :]
                        last = pe.matmul(out[:, q0:T], kp[0:KT, i % H, kt * P:(kt + 1) * P], qp[0:KT, i % H, q0:T],
                                         start=True, stop=not causal)
                        if causal:
                            last = pe.matmul(out[:, q0:q0 + P], k.later[:, :], k.ident_bf[:, :], start=False, stop=True)
                    last.then_inc(st_done, 1)

                def values(i):
                    g, kt = i // 4, i % 4
                    pe.wait_ge(exp_done, b * 2 * H + 2 * (4 * g + 3) + kt // 2 + 3)
                    if kt == 0:
                        pe.wait_ge(v_in, b * G + g + 1)
                        pe.wait_ge(og_read, b * G + g + 1)
                    q0 = kt * P if causal else 0
                    for j in range(4):
                        last = pe.matmul(o_ps[32 * j:32 * j + 32, q0:T], vp[:, g % 4, kt, j, :],
                                         pT[:, g % 2, j, kt, q0:T], start=(kt == 0), stop=(kt == QT - 1),
                                         skip_group_check=True)
                    if kt == QT - 1:
                        last.then_inc(pv_done, 1)

                def turn_o(g):
                    pe.wait_ge(og_read, b * G + g + 2)
                    misc_free(b, h, True)
                    for qt in range(QT):
                        last = pe.transpose(m_ps[:, qt * P:(qt + 1) * P], og[:, qt * P:(qt + 1) * P], k.ident[:, :])
                    last.then_inc(to_full, 1)

                new = live(0)
                if new:
                    scores(0)
                    scores(1)
                if live(h - 1):
                    maxima(h - 1)
                if new:
                    scores(2)
                if live(h - 2):
                    turned_scores(h - 2, 0)
                if new:
                    scores(3)
                if live(h - 2):
                    turned_scores(h - 2, 1)
                if live(h - 6):
                    values(h - 6)
                if h % 4 == 3 and live(h - 11):
                    turn_o((h - 11) // 4)
                if h == 10 and live(-1):
                    pe.wait_ge(to_read, b * G + 3)
                    misc_free(b, h, True)
                    for qt in range(QT):
                        last = pe.transpose(m_ps[:, qt * P:(qt + 1) * P], o[:, qt, :], k.ident[:, :])
                    last.then_inc(ot_full, 1)
                if h == 12 and live(-1):
                    pe.wait_ge(ot_read, b + 2)
                    misc_free(b, h, True)
                    for qt in range(QT):
                        out = m_ps[:, qt * P:(qt + 1) * P]
                        pe.matmul(out, oT[:, qt * P:(qt + 1) * P], wo[:, :], start=True, stop=False)
                        last = pe.matmul(out, k.ones[0:1, :], ob[:, :], start=False, stop=True)
                    last.then_inc(y_full, 1)

            run(pe, step)

        @block.scalar
        def _(act):
            act.sem_inc(exp_done, 2)
            act.sem_inc(mt_read, 1)

            def step(b, h, live):
                if live(h - 1):
                    i = h - 1
                    act.wait_ge(mt_full, b * H + i + 1)
                    act.copy(qp[MR:MR + 3, i % H, :], m_ps[MR:MR + 3, :]).then_inc(mt_read, 1)
                if live(h - 2):
                    i = h - 2
                    g = i // 4
                    for pair in range(2):
                        act.wait_ge(st_done, b * 2 * H + 2 * i + pair + 1)
                        if pair == 0 and i % 4 == 0:
                            act.wait_ge(pv_done, b * G + g + 1)
                        if causal:
                            for kt in (2 * pair, 2 * pair + 1):
                                last = act.activation(pT[:, g % 2, i % 4, kt, kt * P:T], st_ps[pair][:, kt % 2, kt * P:T],
                                                      ACT.Exp)
                        else:
                            last = act.activation(pT[:, g % 2, i % 4, 2 * pair:2 * pair + 2, :], st_ps[pair][:, :, :],
                                                  ACT.Exp)
                        last.then_inc(exp_done, 1)
                if h == 10 and live(-1):
                    act.wait_ge(ot_full, b)
                    act.copy(oT[:, :], m_ps[:, :]).then_inc(ot_read, 1)

            run(act, step)

        @block.gpsimd
        def _(pool):
            pool.memset(vp[:, :, :, :, :], 0.0).then_inc(filled, 1)
            pool.memset(qp[:, :, :], 0.0).then_inc(filled, 1)
            pool.memset(kp[:, :, :], 0.0).then_inc(filled, 1)
            pool.wait_ge(filled, 3)
            pool.memset(zero[:, :], 0.0).then_inc(filled, 1)
            pool.memset(vp[:, :, :, :, DH:DH + 1], 1.0).then_inc(filled, 1)
            pool.wait_ge(filled, 5)
            pool.memset(kp[MR:MR + 3, :, :], 1.0).then_inc(filled, 1)
            pool.wait_ge(filled, 6)

            def step(b, h, live):
                if live(0):
                    pool.wait_ge(max_done, b * H * QT + QT * (h + 1) + 2)
                    pool.wait_ge(mt_full, b * H + h - 1) if not (isinstance(b, int) and b == 0 and h < 2) else None
                    nm, rest, m = nmax[:, h % 4, :], mrest[:, h % 2, :], m3[:, h % 2, :, :]
                    c = b * 3 * H + 3 * h
                    pool.tensor_tensor(m[:, :, 0], nm, zero[:, :], ALU.add).then_inc(mchain, 1)
                    pool.wait_ge(mchain, c + 1)
                    pool.tensor_tensor(rest, nm, m[:, :, 0], ALU.subtract).then_inc(mchain, 1)
                    pool.wait_ge(mchain, c + 2)
                    pool.tensor_tensor(m[:, :, 1], rest, zero[:, :], ALU.add).then_inc(mchain, 1)
                    pool.wait_ge(mchain, c + 3)
                    pool.tensor_tensor(m[:, :, 2], rest, m[:, :, 1], ALU.subtract).then_inc(split_done, 1)

            run(pool, step)

        @block.vector
        def _(v):
            v.sem_inc(max_done, 2)
            v.sem_inc(pv_done, 2)
            v.sem_inc(og_read, 1)
            v.sem_inc(to_read, 3)
            v.sem_inc(ot_read, 2)
            v.sem_inc(y_read, 2)

            def step(b, h, live):
                def row_max(qt):
                    u = QT * h + qt
                    n = (qt + 1) * P if causal else T
                    v.wait_ge(s_done, b * H * QT + u + 1)
                    if qt == 0:
                        if not (isinstance(b, int) and b == 0 and h < 4):
                            v.wait_ge(split_done, b * H + h - 3)
                    v.tensor_reduce(nmax[:, h % 4, qt:qt + 1], s_ps[u % 2][:, 0:n], AX.X, ALU.max, negate=True)\
                        .then_inc(max_done, 1)

                if live(0):
                    row_max(0)
                    row_max(1)
                if h % 4 == 2 and live(h - 10):
                    g = (h - 10) // 4
                    v.wait_ge(pv_done, b * G + g + 3)
                    v.tensor_copy(og[:, :], o_ps[:, :]).then_inc(og_read, 1)
                if h % 4 == 1 and live(0):
                    g = h // 4
                    v.wait_ge(filled, 6)
                    if not (isinstance(b, int) and b == 0):
                        v.wait_ge(pv_done, b * G + g - G + 3)
                    v.tensor_scalar(vp[:, g, :, :, 0:DH], k.v[:, bass.ds(b * QT, QT), 32 * g:32 * g + 32]
                                    .rearrange("p t (j d) -> p t j d", j=4), 1.0, None, ALU.mult).then_inc(v_in, 1)
                if h % 4 == 0 and live(h - 12):
                    g = (h - 12) // 4
                    v.wait_ge(to_full, b * G + g + 1)
                    w = m_ps[:, :].rearrange("p (t h d) -> p t h d", t=QT, h=4)
                    v.reciprocal(rinv[:, :, :], w[:, :, :, DH]).then_inc(rinv_ready, 1)
                    v.wait_ge(rinv_ready, b * G + g + 1)
                    for qt in range(QT):
                        c = 32 * (g % 4)
                        ins = v.tensor_tensor(o[:, qt, c:c + 32].rearrange("p (h d) -> p h d", h=4),
                                              w[:, qt, :, 0:DH], bc(rinv[:, qt, :].unsqueeze(2), [P, 4, DH]), ALU.mult)
                    ins.then_inc(to_read, 1)
                if h == 13 and live(-1):
                    v.wait_ge(y_full, b)
                    xs = k.x[:, bass.ds((b - 1) * QT, QT), :]
                    v.tensor_tensor(xs, m_ps[:, :].rearrange("p (t d) -> p t d", t=QT), xs, ALU.add).then_inc(y_read, 1)
                if live(0):
                    row_max(2)
                    row_max(3)

            run(v, step)


def token_logits(nc, k, tag, w_dram, width, bias_dram=None):
    per_bank = min(512 // width, NT)
    n_banks = NT // per_bank
    with ExitStack() as ctx:
        ph = Phase(nc, ctx, tag)
        w = ph.sb("w", [P, width])
        bias = ph.sb("bias", [1, width])
        ps = ph.banks("ps", n_banks)
        loaded, filled, copied = (ph.sem(s) for s in ("loaded", "filled", "copied"))
        block = ctx.enter_context(nc.Block())
        n_loads = 2 if bias_dram is not None else 1

        @block.sync
        def _(sp):
            sp.dma_start(w[:, :], w_dram).then_inc(loaded, 16)
            if bias_dram is not None:
                sp.dma_start(bias[:, :], bias_dram).then_inc(loaded, 16)

        @block.tensor
        def _(pe):
            pe.wait_ge(loaded, 16 * n_loads)
            for i in range(NT):
                c = (i % per_bank) * width
                out = ps[i // per_bank][:, c:c + width]
                last = pe.matmul(out, k.xnT[:, i * P:(i + 1) * P], w[:, :], start=True, stop=bias_dram is None)
                if bias_dram is not None:
                    last = pe.matmul(out, k.ones[0:1, :], bias[:, :], start=False, stop=True)
                if i % per_bank == per_bank - 1:
                    last.then_inc(filled, 1)

        @block.scalar
        def _(act):
            for j in range(n_banks):
                act.wait_ge(filled, j + 1)
                act.copy(k.logits[:, j * per_bank * width:(j + 1) * per_bank * width],
                         ps[j][:, 0:per_bank * width]).then_inc(copied, 1)
            act.wait_ge(copied, n_banks)


def top8_slots(nc, k, tag):
    E = 64
    M = NT * E
    with ExitStack() as ctx:
        ph = Phase(nc, ctx, tag)
        best = ph.sb("best", [P, NT, 8])
        rest = ph.sb("rest", [P, NT, E])
        chosen = ph.sb("chosen", [P, NT, E])
        chosen_bf = ph.sb("chosen_bf", [P, NT, E], BF16)
        before = ph.sb("before", [P, NT, E], BF16)
        ex = ph.sb("ex", [P, NT, E])
        tot = ph.sb("tot", [P, NT])
        rtot = ph.sb("rtot", [P, NT])
        ps = ph.banks("ps", 2)
        chain, shifted, exp_done, before_ready, counted = (ph.sem(s) for s in (
            "chain", "shifted", "exp_done", "before_ready", "counted"))
        lg = k.logits[:, 0:M].rearrange("p (t e) -> p t e", e=E)
        block = ctx.enter_context(nc.Block())

        @block.vector
        def _(v):
            done = [0]

            def link(ins):
                done[0] += 1
                ins.then_inc(chain, 1)

            def settle():
                v.wait_ge(chain, done[0])

            for i in range(NT):
                link(v.max(best[:, i, :], lg[:, i, :]))
            settle()
            v.tensor_tensor(ex[:, :, :], lg, bc(best[:, :, 0:1], [P, NT, E]), ALU.subtract).then_inc(shifted, 1)
            for i in range(NT):
                link(v.match_replace(rest[:, i, :], best[:, i, :], lg[:, i, :], -BIG))
            settle()
            link(v.tensor_tensor(chosen[:, :, :], rest[:, :, :], lg, ALU.not_equal))
            settle()
            link(v.tensor_copy(chosen_bf[:, :, :], chosen[:, :, :]))
            link(v.memset(before[:, 0, :], 0.0))
            settle()
            for i in range(1, NT):
                link(v.tensor_tensor(before[:, i, :], before[:, i - 1, :], chosen_bf[:, i - 1, :], ALU.add))
                settle()
            v.sem_inc(before_ready, 1)
            v.wait_ge(exp_done, 1)
            link(v.tensor_tensor(ex[:, :, :], ex[:, :, :], chosen[:, :, :], ALU.mult))
            settle()
            link(v.tensor_reduce(tot[:, :], ex[:, :, :], AX.X, ALU.add))
            settle()
            link(v.reciprocal(rtot[:, :], tot[:, :]))
            settle()
            link(v.tensor_tensor(k.weight[:, :, :], ex[:, :, :], bc(rtot[:, :].unsqueeze(2), [P, NT, E]), ALU.mult))
            link(v.tensor_scalar(chosen[:, :, :], chosen[:, :, :], -4096.0, 4096.0, ALU.mult, ALU.add))
            settle()
            for j in range(2):
                v.wait_ge(counted, j + 1)
                link(v.tensor_tensor(k.place[:, 8 * j:8 * j + 8, :], ps[j][:, :].rearrange("p (t e) -> p t e", e=E),
                                     chosen[:, 8 * j:8 * j + 8, :], ALU.add))
            settle()

        @block.scalar
        def _(act):
            act.wait_ge(shifted, 1)
            act.activation(ex[:, :, :], ex[:, :, :], ACT.Exp).then_inc(exp_done, 1)

        @block.tensor
        def _(pe):
            pe.wait_ge(before_ready, 1)
            for i in range(NT):
                out = ps[i // 8][:, (i % 8) * E:(i % 8 + 1) * E]
                pe.matmul(out, k.earlier[:, :], chosen_bf[:, i, :], start=True, stop=False)
                last = pe.matmul(out, k.ones_bf[:, :], before[:, i, :], start=False, stop=True)
                if i % 8 == 7:
                    last.then_inc(counted, 1)


def slot_dispatch(nc, k, tag):
    E, C = 64, 32
    with ExitStack() as ctx:
        ph = Phase(nc, ctx, tag)
        xs = ph.sb("xs", [P, 2, P])
        hot = ph.sb("hot", [P, 2, E, C])
        zeros = ph.sb("zeros", [P, 512], BF16)
        ps = ph.banks("ps", 4)
        zeroed, ready, used, copied = (ph.sem(s) for s in ("zeroed", "ready", "used", "copied"))
        filled = ph.sem("filled")
        block = ctx.enter_context(nc.Block())

        @block.vector
        def _(v):
            v.memset(zeros[:, :], 0.0).then_inc(zeroed, 1)
            v.sem_inc(used, 2)
            with v.Fori(0, NT // 2) as i:
                for s in range(2):
                    v.wait_ge(used, 2 * i + s + 1)
                    v.tensor_copy(xs[:, s, :], k.xn[:, bass.ds(2 * i + s, 1), :].rearrange("p a d -> p (a d)"))
                    v.tensor_tensor(hot[:, s, :, :],
                                    bc(k.place[:, bass.ds(2 * i + s, 1), :].rearrange("p a e -> p (a e)").unsqueeze(2), [P, E, C]),
                                    bc(k.iota[:, 0:C].unsqueeze(1), [P, E, C]), ALU.is_equal).then_inc(ready, 1)

        @block.tensor
        def _(pe):
            pe.wait_ge(zeroed, 1)
            for c in range(4):
                pe.matmul(ps[c][:, :], zeros[:, 0:P], zeros[:, :], start=True, stop=False, skip_group_check=True)
            with pe.Fori(0, NT // 2) as i:
                for s in range(2):
                    pe.wait_ge(ready, 2 * i + s + 1)
                    for c in range(4):
                        last = pe.matmul(ps[c][:, :], xs[:, s, :],
                                         hot[:, s, 16 * c:16 * c + 16, :].rearrange("p e c -> p (e c)"),
                                         start=False, stop=False, skip_group_check=True)
                    last.then_inc(used, 1)
            for c in range(4):
                pe.matmul(ps[c][:, :], zeros[:, 0:P], zeros[:, :], start=False, stop=True,
                          skip_group_check=True).then_inc(filled, 1)

        @block.scalar
        def _(act):
            for c in range(4):
                act.wait_ge(filled, c + 1)
                act.copy(k.slots_x[:, c * 512:(c + 1) * 512], ps[c][:, :]).then_inc(copied, 1)
            act.wait_ge(copied, 4)


def slot_experts(nc, k, tag, gate_up, down):
    F, GROUPS = 96, 16
    with ExitStack() as ctx:
        ph = Phase(nc, ctx, tag)
        wgu = ph.sb("wgu", [P, 2, 4, 2 * F])
        wd = ph.sb("wd", [F, 2, 4, P])
        sg = ph.sb("sg", [F, 2, P])
        h = ph.sb("h", [F, 2, P])
        yT = ph.sb("yT", [P, 2, P])
        gu_ps, y_ps, t_ps = (ph.banks(s, 2) for s in ("gu", "y", "t"))
        in_a, in_b, loaded0, loaded1, gu_done, silu_done, h_done, y_done, yT_done, turned, stored = (
            ph.sem(s) for s in ("in_a", "in_b", "loaded0", "loaded1", "gu_done", "silu_done", "h_done",
                                "y_done", "yT_done", "turned", "stored"))
        loaded = (loaded0, loaded1)
        block = ctx.enter_context(nc.Block())

        @block.sync
        def _(sp):
            for s in range(2):
                sp.dma_start(wgu[:, s, :, :], gate_up[s]).then_inc(loaded[s], 16)
                sp.dma_start(wd[:, s, :, :], down[s]).then_inc(loaded[s], 16)
            with sp.Fori(1, GROUPS // 2) as i:
                for s in range(2):
                    sp.wait_ge(y_done, 2 * i + s - 1)
                    sp.dma_start(wgu[:, s, :, :], gate_up[bass.ds(2 * i + s, 1)].rearrange("a p e f -> (a p) e f"))\
                        .then_inc(loaded[s], 16)
                    sp.dma_start(wd[:, s, :, :], down[bass.ds(2 * i + s, 1)].rearrange("a p e f -> (a p) e f"))\
                        .then_inc(loaded[s], 16)

        @block.tensor
        def _(pe):
            with pe.Fori(0, GROUPS // 2) as i:
                for s in range(2):
                    pe.wait_ge(loaded[s], 32 * i + 32)
                    pe.wait_ge(h_done, 2 * i + s + 1)
                    for f in range(2):
                        for e in range(4):
                            last = pe.matmul(gu_ps[s][0:F, f * P + 32 * e:f * P + 32 * e + 32],
                                             wgu[:, s, e, f * F:(f + 1) * F],
                                             k.slots_x[:, bass.ds((2 * i + s) * P + 32 * e, 32)], start=True, stop=True)
                    last.then_inc(gu_done, 1)
                for s in range(2):
                    pe.wait_ge(h_done, 2 * i + s + 3)
                    pe.wait_ge(yT_done, 2 * i + s + 1)
                    for e in range(4):
                        last = pe.matmul(y_ps[s][:, 32 * e:32 * e + 32], wd[:, s, e, :], h[:, s, 32 * e:32 * e + 32],
                                         start=True, stop=True)
                    last.then_inc(y_done, 1)
                for s in range(2):
                    pe.wait_ge(yT_done, 2 * i + s + 3)
                    pe.wait_ge(stored, 2 * i + s + 1)
                    pe.transpose(t_ps[s][:, 0:P], yT[:, s, :], k.ident[:, :]).then_inc(turned, 1)

        @block.scalar
        def _(act):
            act.sem_inc(stored, 2)
            with act.Fori(0, GROUPS // 2) as i:
                for s in range(2):
                    act.wait_ge(gu_done, 2 * i + s + 1)
                    act.activation(sg[:, s, :], gu_ps[s][0:F, 0:P], ACT.Silu).then_inc(silu_done, 1)
                for s in range(2):
                    act.wait_ge(turned, 2 * i + s + 1)
                    act.copy(k.slots_y[:, bass.ds(2 * i + s, 1), :].rearrange("p a d -> p (a d)"), t_ps[s][:, 0:P])\
                        .then_inc(stored, 1)

        @block.vector
        def _(v):
            v.sem_inc(h_done, 2)
            v.sem_inc(yT_done, 2)
            with v.Fori(0, GROUPS // 2) as i:
                for s in range(2):
                    v.wait_ge(silu_done, 2 * i + s + 1)
                    v.tensor_tensor(h[:, s, :], sg[:, s, :], gu_ps[s][0:F, P:2 * P], ALU.mult).then_inc(h_done, 1)
                for s in range(2):
                    v.wait_ge(y_done, 2 * i + s + 1)
                    v.tensor_copy(yT[:, s, :], y_ps[s][:, 0:P]).then_inc(yT_done, 1)


def slot_combine(nc, k, tag):
    E, C, GROUPS = 64, 32, 16
    with ExitStack() as ctx:
        ph = Phase(nc, ctx, tag)
        hot = ph.sb("hot", [P, 2, E, C])
        share = ph.sb("share", [P, 2, E, C])
        shareT = ph.sb("shareT", [P, 2, GROUPS, P])
        t_ps = ph.banks("t", 4)
        y_ps = ph.banks("y", 2)
        hot_ready, share_ready, turned, copied, summed, added = (
            ph.sem(s) for s in ("hot_ready", "share_ready", "turned", "copied", "summed", "added"))
        block = ctx.enter_context(nc.Block())

        @block.vector
        def _(v):
            v.sem_inc(turned, 8)
            v.sem_inc(summed, 2)
            v.sem_inc(added, 2)
            with v.Fori(0, NT // 2) as i:
                for s in range(2):
                    t = 2 * i + s
                    v.wait_ge(turned, 8 * i + 4 * s + 4)
                    v.tensor_tensor(hot[:, s, :, :],
                                    bc(k.place[:, bass.ds(t, 1), :].rearrange("p a e -> p (a e)").unsqueeze(2), [P, E, C]),
                                    bc(k.iota[:, 0:C].unsqueeze(1), [P, E, C]), ALU.is_equal).then_inc(hot_ready, 1)
                    v.wait_ge(hot_ready, 2 * i + s + 1)
                    v.tensor_tensor(share[:, s, :, :], hot[:, s, :, :],
                                    bc(k.weight[:, bass.ds(t, 1), :].rearrange("p a e -> p (a e)").unsqueeze(2), [P, E, C]),
                                    ALU.mult).then_inc(share_ready, 1)
                for s in range(2):
                    t = 2 * i + s
                    v.wait_ge(summed, 2 * i + s + 3)
                    xs = k.x[:, bass.ds(t, 1), :].rearrange("p a d -> p (a d)")
                    v.tensor_tensor(xs, y_ps[s][:, 0:P], xs, ALU.add).then_inc(added, 1)

        @block.tensor
        def _(pe):
            with pe.Fori(0, NT // 2) as i:
                for s in range(2):
                    pe.wait_ge(share_ready, 2 * i + s + 1)
                    sh = share[:, s, :, :].rearrange("p e c -> p (e c)")
                    for c in range(4):
                        pe.wait_ge(copied, 8 * i + 4 * s + c + 1)
                        for g in range(4):
                            last = pe.transpose(t_ps[c][:, g * P:(g + 1) * P],
                                                sh[:, (4 * c + g) * P:(4 * c + g + 1) * P], k.ident[:, :])
                        last.then_inc(turned, 1)
                    pe.wait_ge(copied, 8 * i + 4 * s + 4 + 4)
                    pe.wait_ge(added, 2 * i + s + 1)
                    for g in range(GROUPS):
                        last = pe.matmul(y_ps[s][:, 0:P], shareT[:, s, g, :], k.slots_y[:, g, :],
                                         start=(g == 0), stop=(g == GROUPS - 1))
                    last.then_inc(summed, 1)

        @block.scalar
        def _(act):
            act.sem_inc(copied, 4)
            with act.Fori(0, NT // 2) as i:
                for s in range(2):
                    act.wait_ge(summed, 2 * i + s + 1)
                    for c in range(4):
                        act.wait_ge(turned, 8 * i + 4 * s + c + 1 + 8)
                        act.copy(shareT[:, s, 4 * c:4 * c + 4, :].rearrange("p g t -> p (g t)"), t_ps[c][:, :])\
                            .then_inc(copied, 1)


def top2_gates(nc, k, tag, groups, rule, scale_dram=None, capacity=None):
    M = NT * groups
    with ExitStack() as ctx:
        ph = Phase(nc, ctx, tag)
        below = ph.sb("below", [P, M, 8])
        first = ph.sb("first", [P, M, 8])
        second = ph.sb("second", [P, M, 8])
        left = ph.sb("left", [P, M, 8])
        m = ph.sb("m", [P, 2, M])
        e = ph.sb("e", [P, 2, M])
        where = ph.sb("where", [P, M])
        tot = ph.sb("tot", [P, M])
        chain, best_ready, exp_done, scale_in, both_ready, counted = (
            ph.sem(s) for s in ("chain", "best_ready", "exp_done", "scale_in", "both_ready", "counted"))
        if rule == "capacity":
            both = ph.sb("both", [P, NT, 8], BF16)
            before = ph.sb("before", [P, NT, 8], BF16)
            ex = ph.sb("ex", [P, M, 8])
            ps = ph.banks("ps", 1)
        if rule == "sigmoid":
            rscale = ph.sb("rscale", [P, 1])
        lg = k.logits[:, 0:M * 8].rearrange("p (m e) -> p m e", e=8)
        gate = k.gate[:, 0:M * 8].rearrange("p (m e) -> p m e", e=8)
        wide = [P, M, 8]
        iota8 = bc(k.iota[:, 0:8].unsqueeze(1), wide)
        block = ctx.enter_context(nc.Block())

        @block.sync
        def _(sp):
            if rule == "sigmoid":
                sp.dma_start(rscale[:, :], scale_dram).then_inc(scale_in, 16)

        @block.vector
        def _(v):
            done = [0]

            def link(ins):
                done[0] += 1
                ins.then_inc(chain, 1)
                v.wait_ge(chain, done[0])

            def over8(ap):
                return bc(ap.unsqueeze(2), wide)

            def best(src, i, hot):
                link(v.tensor_reduce(m[:, i, :], src, AX.X, ALU.max))
                link(v.tensor_tensor(below[:, :, :], src, over8(m[:, i, :]), ALU.is_lt))
                link(v.scalar_tensor_tensor(below[:, :, :], below[:, :, :], 1024.0, iota8, ALU.mult, ALU.add))
                link(v.tensor_reduce(where[:, :], below[:, :, :], AX.X, ALU.min))
                link(v.tensor_tensor(hot[:, :, :], iota8, over8(where[:, :]), ALU.is_equal))

            best(lg, 0, first)
            link(v.scalar_tensor_tensor(left[:, :, :], first[:, :, :], -BIG, lg, ALU.mult, ALU.add))
            best(left[:, :, :], 1, second)
            if rule == "sigmoid":
                v.sem_inc(best_ready, 1)
                v.wait_ge(exp_done, 1)
                link(v.tensor_scalar(e[:, :, :], e[:, :, :], 1.0, None, ALU.add))
                link(v.reciprocal(e[:, :, :], e[:, :, :]))
                link(v.tensor_tensor(tot[:, :], e[:, 0, :], e[:, 1, :], ALU.add))
                link(v.tensor_scalar(tot[:, :], tot[:, :], 1e-9, None, ALU.max))
                link(v.reciprocal(tot[:, :], tot[:, :]))
                v.wait_ge(scale_in, 16)
                link(v.tensor_scalar(tot[:, :], tot[:, :], rscale[:, 0:1], None, ALU.mult))
                for i in range(2):
                    link(v.tensor_tensor(e[:, i, :], e[:, i, :], tot[:, :], ALU.mult))
            else:
                link(v.tensor_tensor(e[:, 1, :], m[:, 1, :], m[:, 0, :], ALU.subtract))
                if rule == "capacity":
                    link(v.tensor_tensor(ex[:, :, :], lg, over8(m[:, 0, :]), ALU.subtract))
                v.sem_inc(best_ready, 1)
                v.wait_ge(exp_done, 1)
                if rule == "softmax2":
                    link(v.tensor_scalar(tot[:, :], e[:, 1, :], 1.0, None, ALU.add))
                else:
                    link(v.tensor_reduce(tot[:, :], ex[:, :, :], AX.X, ALU.add))
                link(v.reciprocal(e[:, 0, :], tot[:, :]))
                link(v.tensor_tensor(e[:, 1, :], e[:, 1, :], e[:, 0, :], ALU.mult))
            if rule == "capacity":
                link(v.tensor_tensor(both[:, :, :], first[:, :, :], second[:, :, :], ALU.add))
                link(v.memset(before[:, 0, :], 0.0))
                for i in range(1, NT):
                    link(v.tensor_tensor(before[:, i, :], before[:, i - 1, :], both[:, i - 1, :], ALU.add))
                v.sem_inc(both_ready, 1)
            link(v.tensor_tensor(first[:, :, :], first[:, :, :], over8(e[:, 0, :]), ALU.mult))
            link(v.tensor_tensor(second[:, :, :], second[:, :, :], over8(e[:, 1, :]), ALU.mult))
            link(v.tensor_tensor(gate, first[:, :, :], second[:, :, :], ALU.add))
            if rule == "capacity":
                v.wait_ge(counted, 1)
                link(v.tensor_scalar(left[:, :, :], ps[0][:, 0:M * 8].rearrange("p (m e) -> p m e", e=8),
                                     float(capacity), None, ALU.is_lt))
                link(v.tensor_tensor(gate, gate, left[:, :, :], ALU.mult))
                link(v.tensor_reduce(tot[:, :], gate, AX.X, ALU.add))
                link(v.tensor_scalar(tot[:, :], tot[:, :], 1e-6, None, ALU.add))
                link(v.reciprocal(tot[:, :], tot[:, :]))
                link(v.tensor_tensor(gate, gate, over8(tot[:, :]), ALU.mult))

        @block.scalar
        def _(act):
            act.wait_ge(best_ready, 1)
            if rule == "sigmoid":
                act.activation(e[:, :, :], m[:, :, :], ACT.Exp, scale=-1.0).then_inc(exp_done, 1)
            elif rule == "softmax2":
                act.activation(e[:, 1, :], e[:, 1, :], ACT.Exp).then_inc(exp_done, 1)
            else:
                act.activation(ex[:, :, :], ex[:, :, :], ACT.Exp)
                act.activation(e[:, 1, :], e[:, 1, :], ACT.Exp).then_inc(exp_done, 1)

        if rule == "capacity":
            @block.tensor
            def _(pe):
                pe.wait_ge(both_ready, 1)
                for i in range(NT):
                    out = ps[0][:, i * 8:(i + 1) * 8]
                    pe.matmul(out, k.earlier[:, :], both[:, i, :], start=True, stop=False)
                    last = pe.matmul(out, k.ones_bf[:, :], before[:, i, :], start=False, stop=True)
                last.then_inc(counted, 1)


def gated_ffn(nc, k, tag, w0d, w1d, w2d, b0d, b1d, b2d):
    E, C = 8, 4
    STEPS = E * C
    with ExitStack() as ctx:
        ph = Phase(nc, ctx, tag)
        w0 = ph.sb("w0", [P, E, C, P])
        w1 = ph.sb("w1", [P, E, C, P])
        w2 = ph.sb("w2", [P, E, C, P])
        b0 = ph.sb("b0", [P, E * C])
        b1 = ph.sb("b1", [P, E * C])
        b2 = ph.sb("b2", [8, P])
        sg = ph.sb("sg", [P, 2, T])
        hg = ph.sb("hg", [P, 2, T])
        gs = ph.sb("gs", [P, QT, 8])
        gT = ph.sb("gT", [8, T])
        h_ps, g_ps, y_ps, m_ps = (ph.banks(s, 2) for s in ("h", "g", "y", "m"))
        loaded, h_full, g_full, silu_done, hg_done, hg_used, y_full, y_free, gs_ready, gT_full, gT_ready, b_full = (
            ph.sem(s) for s in ("loaded", "h_full", "g_full", "silu_done", "hg_done", "hg_used", "y_full",
                                "y_free", "gs_ready", "gT_full", "gT_ready", "b_full"))
        acc_chain = ph.sem("acc_chain")
        block = ctx.enter_context(nc.Block())

        @block.sync
        def _(sp):
            for dst, src in ((w1[:, :, :, :], w1d), (w0[:, :, :, :], w0d), (w2[:, :, :, :], w2d), (b0[:, :], b0d),
                             (b1[:, :], b1d), (b2[:, :], b2d)):
                sp.dma_start(dst, src).then_inc(loaded, 16)

        @block.tensor
        def _(pe):
            pe.wait_ge(loaded, 16 * 6)
            with pe.Fori(0, B) as t:
                xs = k.xnT[:, bass.ds(t * T, T)]

                def up(n):
                    pe.wait_ge(hg_done, t * STEPS + n + 1)
                    pe.matmul(g_ps[n % 2][:, :], w1[:, n // C, n % C, :], xs, start=True, stop=True).then_inc(g_full, 1)
                    pe.matmul(h_ps[n % 2][:, :], w0[:, n // C, n % C, :], xs, start=True, stop=True).then_inc(h_full, 1)

                def down(n):
                    e, c = n // C, n % C
                    pe.wait_ge(hg_done, t * STEPS + n + 3)
                    if c == 0:
                        pe.wait_ge(y_free, t * E + e + 1)
                    for i in range(QT):
                        last = pe.matmul(y_ps[e % 2][:, i * P:(i + 1) * P], hg[:, n % 2, i * P:(i + 1) * P],
                                         w2[:, e, c, :], start=(c == 0 and i == 0), stop=(c == C - 1),
                                         skip_group_check=True)
                    last.then_inc(hg_used, 1)

                for n in range(STEPS + 1):
                    if n < STEPS:
                        up(n)
                    if n >= 1:
                        down(n - 1)
                pe.wait_ge(gs_ready, t + 1)
                for i in range(QT):
                    last = pe.transpose(m_ps[0][0:8, i * P:(i + 1) * P], gs[:, i, :], k.ident[:, :])
                last.then_inc(gT_full, 1)
                pe.wait_ge(gT_ready, t + 1)
                for i in range(QT):
                    last = pe.matmul(m_ps[1][:, i * P:(i + 1) * P], gT[:, i * P:(i + 1) * P], b2[:, :],
                                     start=True, stop=True)
                last.then_inc(b_full, 1)

        @block.scalar
        def _(act):
            act.wait_ge(loaded, 16 * 6)
            with act.Fori(0, B) as t:
                for n in range(STEPS):
                    act.wait_ge(g_full, t * STEPS + n + 1)
                    act.wait_ge(hg_done, t * STEPS + n + 1)
                    act.activation(sg[:, n % 2, :], g_ps[n % 2][:, :], ACT.Silu, bias=b1[:, n:n + 1]).then_inc(silu_done, 1)

        @block.vector
        def _(v):
            v.sem_inc(hg_done, 2)
            v.sem_inc(hg_used, 2)
            v.sem_inc(y_free, 2)
            v.wait_ge(loaded, 16 * 6)
            with v.Fori(0, B) as t:
                v.tensor_copy(gs[:, :, :], k.gate[:, bass.ds(t * QT * 8, QT * 8)].rearrange("p (i e) -> p i e", e=8))\
                    .then_inc(gs_ready, 1)
                v.wait_ge(gs_ready, t + 1)
                xs = k.x[:, bass.ds(t * QT, QT), :]

                def gated(e):
                    v.wait_ge(hg_used, t * STEPS + (e + 1) * C + 2)
                    if e > 0:
                        v.wait_ge(y_free, t * E + e + 2)
                    for i in range(QT):
                        last = v.scalar_tensor_tensor(xs[:, i, :], y_ps[e % 2][:, i * P:(i + 1) * P],
                                                      gs[:, i, e:e + 1], xs[:, i, :], ALU.mult, ALU.add)
                    last.then_inc(y_free, 1)

                for n in range(STEPS + 2):
                    if n < STEPS:
                        v.wait_ge(silu_done, t * STEPS + n + 1)
                        v.wait_ge(h_full, t * STEPS + n + 1)
                        v.wait_ge(hg_used, t * STEPS + n + 1)
                        v.scalar_tensor_tensor(hg[:, n % 2, :], h_ps[n % 2][:, :], b0[:, n:n + 1], sg[:, n % 2, :],
                                               ALU.add, ALU.mult).then_inc(hg_done, 1)
                    if n >= 5 and n % C == 1:
                        gated(n // C - 1)
                v.wait_ge(gT_full, t + 1)
                v.tensor_copy(gT[:, :], m_ps[0][0:8, :]).then_inc(gT_ready, 1)
                v.wait_ge(b_full, t + 1)
                v.wait_ge(y_free, t * E + E + 2)
                v.tensor_tensor(xs, m_ps[1][:, :].rearrange("p (i d) -> p i d", d=P), xs, ALU.add).then_inc(acc_chain, 1)
                v.wait_ge(acc_chain, t + 1)


def selective_scan(nc, k, tag, d):
    S = 16
    NEAR = 99.0
    with ExitStack() as ctx:
        ph = Phase(nc, ctx, tag)
        w_in = ph.sb("w_in", [P, 2 * P])
        w_x = ph.sb("w_x", [P, S + 2 * P])
        w_dt = ph.sb("w_dt", [S, P])
        w_o = ph.sb("w_o", [P, P])
        b_o = ph.sb("b_o", [1, P])
        b_in = ph.sb("b_in", [P, 2])
        b_bc = ph.sb("b_bc", [P, 2])
        b_dl = ph.sb("b_dl", [S, 1])
        b_dt = ph.sb("b_dt", [P, 1])
        dpar = ph.sb("dpar", [P, 1])
        a_log = ph.sb("a_log", [P, S])
        a = ph.sb("a", [P, S])
        a_slow = ph.sb("a_slow", [P, 1])
        xi = ph.sb("xi", [P, T])
        res = ph.sb("res", [P, T])
        dl = ph.sb("dl", [S, T])
        cm = ph.sb("cm", [P, T])
        z = ph.sb("z", [P, T])
        s1 = ph.sb("s1", [P, T])
        s2 = ph.sb("s2", [P, T])
        delta = ph.sb("delta", [P, T])
        u = ph.sb("u", [P, T])
        da = ph.sb("da", [P, S, T])
        da_slow = ph.sb("da_slow", [P, T])
        h = ph.sb("h", [P, S, T])
        y = ph.sb("y", [P, T])
        peak = ph.sb("peak", [P, 1])
        top = ph.sb("top", [1, 1])
        flag = ph.sb("flag", [1, 1], I32)
        state = ph.sb("state", [P, S])
        ps = ph.banks("ps", 8)
        chain, loaded, a_raw, a_ready, in_full, in_read, dl_full, dl_ready, bc_full, dt_full, z_ready, e_ready = (
            ph.sem(s) for s in ("chain", "loaded", "a_raw", "a_ready", "in_full", "in_read", "dl_full", "dl_ready",
                                "bc_full", "dt_full", "z_ready", "e_ready"))
        delta_ready, da_ready, peak_ready, peak_full, y_ready, y_full, x_added, checked, mixed, state_set = (
            ph.sem(s) for s in ("delta_ready", "da_ready", "peak_ready", "peak_full", "y_ready", "y_full", "x_added",
                                "checked", "mixed", "state_set"))
        block = ctx.enter_context(nc.Block())
        loads = [(w_in[:, :], d["w_in"]), (w_x[:, :], d["w_x"]), (w_dt[:, :], d["w_dt"]), (w_o[:, :], d["w_o"]),
                 (b_o[:, :], d["b_o"]), (b_in[:, :], d["b_in"]), (b_bc[:, :], d["b_bc"]), (b_dl[:, :], d["b_dl"]),
                 (b_dt[:, :], d["b_dt"]), (dpar[:, :], d["dpar"]), (a_log[:, :], d["a_log"])]

        @block.sync
        def _(sp):
            for dst, src in loads:
                sp.dma_start(dst, src).then_inc(loaded, 16)

        @block.tensor
        def _(pe):
            pe.wait_ge(loaded, 16 * len(loads))
            with pe.Fori(0, B) as b:
                xs = k.xnT[:, bass.ds(b * T, T)]
                for i in range(2):
                    pe.matmul(ps[i][:, :], w_in[:, i * P:(i + 1) * P], xs, start=True, stop=True).then_inc(in_full, 1)
                pe.wait_ge(in_read, 2 * b + 2)
                pe.matmul(ps[2][0:S, :], w_x[:, 0:S], xi[:, :], start=True, stop=True).then_inc(dl_full, 1)
                for i in range(2):
                    last = pe.matmul(ps[3 + i][:, :], w_x[:, S + i * P:S + (i + 1) * P], xi[:, :], start=True, stop=True)
                last.then_inc(bc_full, 1)
                pe.wait_ge(dl_ready, b + 1)
                pe.matmul(ps[5][:, :], w_dt[:, :], dl[:, :], start=True, stop=True).then_inc(dt_full, 1)
                pe.wait_ge(peak_ready, b + 1)
                pe.transpose(ps[6][0:1, 0:P], peak[:, :], k.ident[:, :]).then_inc(peak_full, 1)
                pe.wait_ge(y_ready, b + 1)
                for i in range(QT):
                    out = ps[7][:, i * P:(i + 1) * P]
                    pe.matmul(out, y[:, i * P:(i + 1) * P], w_o[:, :], start=True, stop=False)
                    last = pe.matmul(out, k.ones[0:1, :], b_o[:, :], start=False, stop=True)
                last.then_inc(y_full, 1)
                pe.wait_ge(x_added, b + 1)

        @block.scalar
        def _(act):
            act.wait_ge(a_raw, 1)
            act.activation(a[:, :], a_log[:, :], ACT.Exp).then_inc(a_ready, 1)
            with act.Fori(0, B) as b:
                act.wait_ge(in_full, 2 * b + 1)
                act.activation(xi[:, :], ps[0][:, :], ACT.Silu, bias=b_in[:, 0:1]).then_inc(in_read, 1)
                act.wait_ge(in_full, 2 * b + 2)
                act.activation(res[:, :], ps[1][:, :], ACT.Silu, bias=b_in[:, 1:2]).then_inc(in_read, 1)
                act.wait_ge(z_ready, b + 1)
                act.activation(z[:, :], z[:, :], ACT.Exp).then_inc(e_ready, 1)
                act.wait_ge(delta_ready, b + 1)
                act.activation(da_slow[:, :], delta[:, :], ACT.Exp, scale=a_slow[:, 0:1]).then_inc(da_ready, 1)
                for n in range(S):
                    act.activation(da[:, n, :], delta[:, :], ACT.Exp, scale=a[:, n:n + 1]).then_inc(da_ready, 1)
                act.wait_ge(x_added, b + 1)

        @block.vector
        def _(v):
            v.wait_ge(loaded, 16 * len(loads))
            v.tensor_scalar(a_log[:, :], a_log[:, :], 2.0, -5.0, ALU.min, ALU.max).then_inc(a_raw, 1)
            v.wait_ge(a_ready, 1)
            v.tensor_scalar(a[:, :], a[:, :], -1.0, -5.0, ALU.mult, ALU.max).then_inc(a_raw, 1)
            v.wait_ge(a_raw, 2)
            v.tensor_scalar(a[:, :], a[:, :], -0.01, None, ALU.min).then_inc(a_raw, 1)
            v.wait_ge(a_raw, 3)
            v.tensor_reduce(a_slow[:, :], a[:, :], AX.X, ALU.max).then_inc(a_raw, 1)
            v.wait_ge(a_raw, 4)
            LINKS = 21
            with v.Fori(0, B) as b:
                done = [0]

                def link(ins):
                    done[0] += 1
                    ins.then_inc(chain, 1)
                    v.wait_ge(chain, b * LINKS + done[0])

                v.wait_ge(dl_full, b + 1)
                v.tensor_scalar(dl[:, :], ps[2][0:S, :], b_dl[:, 0:1], None, ALU.add).then_inc(dl_ready, 1)
                v.wait_ge(bc_full, b + 1)
                link(v.tensor_scalar(cm[:, :], ps[4][:, :], b_bc[:, 1:2], None, ALU.add))
                v.wait_ge(dt_full, b + 1)
                v.tensor_scalar(z[:, :], ps[5][:, :], b_dt[:, 0:1], 0.0, ALU.add, ALU.min).then_inc(z_ready, 1)
                v.wait_ge(e_ready, b + 1)
                link(v.tensor_scalar(z[:, :], z[:, :], 0.2, None, ALU.min))
                link(v.tensor_scalar(s1[:, :], z[:, :], 2.0, None, ALU.add))
                link(v.reciprocal(s1[:, :], s1[:, :]))
                link(v.tensor_tensor(s1[:, :], z[:, :], s1[:, :], ALU.mult))
                link(v.tensor_tensor(s2[:, :], s1[:, :], s1[:, :], ALU.mult))
                link(v.tensor_scalar(z[:, :], s2[:, :], 2.0 / 9, 2.0 / 7, ALU.mult, ALU.add))
                for c in (2.0 / 5, 2.0 / 3, 2.0):
                    link(v.tensor_tensor(z[:, :], z[:, :], s2[:, :], ALU.mult))
                    link(v.tensor_scalar(z[:, :], z[:, :], c, None, ALU.add))
                link(v.tensor_tensor(z[:, :], z[:, :], s1[:, :], ALU.mult))
                v.tensor_scalar(delta[:, :], z[:, :], 1e-5, 0.1, ALU.max, ALU.min).then_inc(delta_ready, 1)
                v.wait_ge(delta_ready, b + 1)
                link(v.scalar_tensor_tensor(u[:, :], ps[3][:, :], b_bc[:, 0:1], delta[:, :], ALU.add, ALU.mult))
                link(v.tensor_tensor(u[:, :], u[:, :], xi[:, :], ALU.mult))
                link(v.scalar_tensor_tensor(s1[:, :], u[:, :], -1.0, u[:, :], ALU.mult, ALU.max))
                v.wait_ge(da_ready, b * (S + 1) + 1)
                link(v.tensor_tensor_scan(s2[:, :], da_slow[:, :], s1[:, :], 0.0, ALU.mult, ALU.add))
                v.tensor_reduce(peak[:, :], s2[:, :], AX.X, ALU.max).then_inc(peak_ready, 1)
                for n in range(S):
                    v.wait_ge(da_ready, b * (S + 1) + n + 2)
                    last = v.tensor_tensor_scan(h[:, n, :], da[:, n, :], u[:, :], 0.0, ALU.mult, ALU.add)
                link(last)
                v.wait_ge(peak_full, b + 1)
                link(v.tensor_reduce(top[:, :], ps[6][0:1, 0:P], AX.X, ALU.max))
                v.tensor_scalar(flag[:, :], top[:, :], NEAR, None, ALU.is_lt).then_inc(checked, 1)
                v.wait_ge(checked, b + 1)
                v.memset(state[:, :], 0.0).then_inc(state_set, 1)
                small = v.value_load(flag[0:1, 0:1], min_val=0, max_val=1)
                with v.If(small < 1):
                    v.drain()
                    with v.Fori(0, T) as t:
                        v.tensor_tensor(state[:, :], state[:, :], da[:, :, bass.ds(t, 1)].rearrange("p n a -> p (n a)"),
                                        ALU.mult)
                        v.drain()
                        v.tensor_scalar(state[:, :], state[:, :], u[:, bass.ds(t, 1)], -100.0, ALU.add, ALU.max)
                        v.drain()
                        v.tensor_scalar(state[:, :], state[:, :], 100.0, None, ALU.min)
                        v.drain()
                        v.tensor_copy(h[:, :, bass.ds(t, 1)].rearrange("p n a -> p (n a)"), state[:, :])
                        v.drain()
                link(v.tensor_reduce(s1[:, :], h[:, :, :].rearrange("p n t -> p t n"), AX.X, ALU.add))
                assert done[0] == LINKS
                v.tensor_tensor(s1[:, :], s1[:, :], cm[:, :], ALU.mult).then_inc(mixed, 1)
                v.wait_ge(mixed, 3 * b + 1)
                v.scalar_tensor_tensor(s1[:, :], xi[:, :], dpar[:, 0:1], s1[:, :], ALU.mult, ALU.add).then_inc(mixed, 1)
                v.wait_ge(mixed, 3 * b + 2)
                v.wait_ge(in_read, 2 * b + 2)
                v.tensor_tensor(y[:, :], s1[:, :], res[:, :], ALU.mult).then_inc(y_ready, 1)
                v.wait_ge(y_full, b + 1)
                xs = k.x[:, bass.ds(b * QT, QT), :]
                v.tensor_tensor(xs, ps[7][:, :].rearrange("p (i d) -> p i d", d=P), xs, ALU.add).then_inc(x_added, 1)
                v.sem_inc(mixed, 1)


def shared_ffn(nc, k, tag, wg_d, wd_d):
    E = 8
    with ExitStack() as ctx:
        ph = Phase(nc, ctx, tag)
        wg = ph.sb("wg", [P, 2, P])
        wd = ph.sb("wd", [P, 2, E, P])
        hid = ph.sb("hid", [P, 2, T])
        gs = ph.sb("gs", [P, QT, 8])
        h_ps = ph.banks("h", 2)
        y_ps = ph.banks("y", 4)
        loaded, h_full, h_ready, y_full, y_free, gs_ready, chain = (ph.sem(s) for s in (
            "loaded", "h_full", "h_ready", "y_full", "y_free", "gs_ready", "chain"))
        block = ctx.enter_context(nc.Block())
        Y = 2 * QT

        @block.sync
        def _(sp):
            sp.dma_start(wg[:, :, :], wg_d).then_inc(loaded, 16)
            sp.dma_start(wd[:, :, :, :], wd_d).then_inc(loaded, 16)

        @block.tensor
        def _(pe):
            pe.wait_ge(loaded, 32)
            with pe.Fori(0, B) as t:
                xs = k.xnT[:, bass.ds(t * T, T)]
                for c in range(2):
                    pe.matmul(h_ps[c][:, :], wg[:, c, :], xs, start=True, stop=True).then_inc(h_full, 1)
                pe.wait_ge(h_ready, 2 * t + 2)
                for n in range(Y):
                    i, half = n // 2, n % 2
                    pe.wait_ge(y_free, t * Y + n + 1)
                    for c in range(2):
                        last = pe.matmul(y_ps[n % 4][:, :], hid[:, c, i * P:(i + 1) * P],
                                         wd[:, c, 4 * half:4 * half + 4, :].rearrange("p e d -> p (e d)"),
                                         start=(c == 0), stop=(c == 1))
                    last.then_inc(y_full, 1)

        @block.scalar
        def _(act):
            with act.Fori(0, B) as t:
                for c in range(2):
                    act.wait_ge(h_full, 2 * t + c + 1)
                    act.activation(hid[:, c, :], h_ps[c][:, :], ACT.Silu).then_inc(h_ready, 1)

        @block.vector
        def _(v):
            v.sem_inc(y_free, 4)
            with v.Fori(0, B) as t:
                v.tensor_copy(gs[:, :, :], k.gate[:, bass.ds(t * QT * 8, QT * 8)].rearrange("p (i e) -> p i e", e=8))\
                    .then_inc(gs_ready, 1)
                v.wait_ge(gs_ready, t + 1)
                xs = k.x[:, bass.ds(t * QT, QT), :]
                for n in range(Y):
                    i, half = n // 2, n % 2
                    v.wait_ge(y_full, t * Y + n + 1)
                    for e in range(4):
                        ins = v.scalar_tensor_tensor(xs[:, i, :], y_ps[n % 4][:, e * P:(e + 1) * P],
                                                     gs[:, i, 4 * half + e:4 * half + e + 1], xs[:, i, :],
                                                     ALU.mult, ALU.add)
                        if e < 3:
                            ins.then_inc(chain, 1)
                            v.wait_ge(chain, (t * Y + n) * 3 + e + 1)
                        else:
                            ins.then_inc(y_free, 1)
                            v.wait_ge(y_free, t * Y + n + 5)


def relative_rows(nc, k, tag, d, band):
    H, G, NB, W, HOLE = 16, 4, 10, 257, 129
    with ExitStack() as ctx:
        ph = Phase(nc, ctx, tag)
        wr = ph.sb("wr", [P, G, P])
        br = ph.sb("br", [P, G])
        rel = ph.sb("rel", [P, P])
        rT = ph.sb("rT", [P, 2, T])
        rows = ph.sb("rows", [P, 4, 4, P])
        hole = ph.sb("hole", [P, 4, QT, HOLE])
        r_ps = ph.banks("r", 2)
        e_ps = ph.banks("e", 4)
        loaded, hole_set, r_full, rT_ready, e_full, copied, written0, written1, written2, written3, filled = (
            ph.sem(s) for s in ("loaded", "hole_set", "r_full", "rT_ready", "e_full", "copied", "written0",
                                "written1", "written2", "written3", "filled"))
        written = (written0, written1, written2, written3)
        lead = band[0:P].rearrange("(a w) -> a w", a=1)
        main = band[P:P + B * H * T * W].rearrange("(h t w) -> h t w", t=T, w=W)
        block = ctx.enter_context(nc.Block())

        @block.sync
        def _(sp):
            for dst, src in ((wr[:, :, :], d["a3_wr"]), (br[:, :], d["a3_br"]), (rel[:, :], d["a3_rel"])):
                sp.dma_start(dst, src).then_inc(loaded, 16)
            with sp.Fori(0, B) as b:
                for n in range(16):
                    sp.wait_ge(copied, 16 * b + n + 1 + 4)
                    sp.dma_start(main[bass.ds(b * H + n, 1), :, 0:P].rearrange("h (i p) w -> (h p) i w", p=P),
                                 rows[:, n % 4, :, :]).then_inc(written[n % 4], 16)
            for s in written:
                sp.wait_ge(s, 16 * 16 + 16)

        @block.gpsimd
        def _(pool):
            pool.memset(hole[:, :, :, :], -1e9).then_inc(hole_set, 1)
            pool.wait_ge(hole_set, 1)
            pool.dma_start(lead, hole[0:1, 0, 0, 0:P]).then_inc(filled, 16)
            for b in range(B * H // 4):
                pool.dma_start(main[4 * b:4 * b + 4, :, P:W].rearrange("h (i p) w -> p h i w", p=P), hole[:, :, :, :])\
                    .then_inc(filled, 16)
            pool.wait_ge(filled, 16 * (1 + B * H // 4))

        @block.tensor
        def _(pe):
            pe.wait_ge(loaded, 48)
            with pe.Fori(0, B) as b:
                xs = k.xnT[:, bass.ds(b * T, T)]
                for g in range(G):
                    pe.wait_ge(rT_ready, G * b + g + 1)
                    pe.matmul(r_ps[g % 2][:, :], wr[:, g, :], xs, start=True, stop=True).then_inc(r_full, 1)
                    pe.wait_ge(rT_ready, G * b + g + 3)
                    pe.wait_ge(copied, 16 * b + 4 * g + 4)
                    for i in range(QT):
                        for j in range(4):
                            last = pe.matmul(e_ps[j][:, i * P:(i + 1) * P], rT[32 * j:32 * j + NB, g % 2, i * P:(i + 1) * P],
                                             rel[32 * j:32 * j + NB, :], start=True, stop=True)
                            if i == QT - 1:
                                last.then_inc(e_full, 1)

        @block.scalar
        def _(act):
            act.sem_inc(rT_ready, 2)
            act.wait_ge(loaded, 48)
            with act.Fori(0, B) as b:
                for g in range(G):
                    act.wait_ge(r_full, G * b + g + 1)
                    act.activation(rT[:, g % 2, :], r_ps[g % 2][:, :], ACT.Identity, bias=br[:, g:g + 1])\
                        .then_inc(rT_ready, 1)

        @block.vector
        def _(v):
            v.sem_inc(copied, 4)
            for s in written:
                v.sem_inc(s, 16)
            with v.Fori(0, B) as b:
                for n in range(16):
                    v.wait_ge(e_full, 16 * b + n + 1)
                    v.wait_ge(written[n % 4], 64 * b + 16 * (n // 4) + 16)
                    v.tensor_copy(rows[:, n % 4, :, :].rearrange("p j e -> p (j e)"), e_ps[n % 4][:, :]).then_inc(copied, 1)


def relative_heads(nc, k, tag, d, band):
    H, DH, C, W = 16, 64, 8, 257
    UNITS = H * QT
    with ExitStack() as ctx:
        ph = Phase(nc, ctx, tag)
        wq = ph.sb("wq", [P, C, P])
        wk = ph.sb("wk", [P, C, P])
        wv = ph.sb("wv", [P, 2, 512])
        wo = ph.sb("wo", [P, C, P])
        bq = ph.sb("bq", [P, C])
        bo = ph.sb("bo", [1, P])
        xb = ph.sb("xb", [P, T])
        qT = ph.sb("qT", [P, C, T])
        kT = ph.sb("kT", [P, C, T])
        val = ph.sb("val", [P, QT, H * DH])
        rel = ph.sb("rel", [P, 2, QT, 2 * P])
        lg = ph.sb("lg", [P, 2, 2 * P])
        mx = ph.sb("mx", [P, 4])
        nmax = ph.sb("nmax", [P, 4])
        spare = ph.sb("spare", [P, 2])
        prob = ph.sb("prob", [P, 2, 2 * P])
        pT = ph.sb("pT", [P, 2, QT, 2 * P])
        rsum = ph.sb("rsum", [P, 2, QT])
        rinv = ph.sb("rinv", [P, 2, QT])
        o = ph.sb("o", [P, QT, H * DH])
        oT = ph.sb("oT", [P, C, T])
        s_ps, t_ps, o_ps, m_ps = (ph.banks(s, 2) for s in ("s", "t", "o", "m"))
        loaded, xb_ready, m_full0, m_full1, m_free0, m_free1, rel_in0, rel_in1 = (ph.sem(s) for s in (
            "loaded", "xb_ready", "m_full0", "m_full1", "m_free0", "m_free1", "rel_in0", "rel_in1"))
        s_done, mx_done, max_done, exp_done, t_done, pt_copied, pv_done, o_free, rinv_ready, x_added = (
            ph.sem(s) for s in ("s_done", "mx_done", "max_done", "exp_done", "t_done", "pt_copied", "pv_done",
                                "o_free", "rinv_ready", "x_added"))
        m_full, m_free, rel_in = (m_full0, m_full1), (m_free0, m_free1), (rel_in0, rel_in1)
        M_Q, M_K, M_V, M_OT, M_Y, M_N = 0, 8, 16, 24, 32, 33
        PER = (17, 16)
        skewed = band[P - 1:P - 1 + B * H * T * W].rearrange("(h q r) -> h q r", q=QT, r=P * W)
        block = ctx.enter_context(nc.Block())

        def keys(qt):
            return (0, P) if qt == 0 else ((qt - 1) * P, 2 * P)

        @block.sync
        def _(sp):
            for dst, src in ((wq[:, :, :], d["a3_wq"]), (wk[:, :, :], d["a3_wk"]), (wv[:, :, :], d["a3_wv"]),
                             (bq[:, :], d["a3_bq"]), (wo[:, :, :], d["a3_wo"]), (bo[:, :], d["a3_bo"])):
                sp.dma_start(dst, src).then_inc(loaded, 16)
            with sp.Fori(0, B) as b:
                for h in range(H):
                    sp.wait_ge(mx_done, UNITS * b + QT * (h + 1))
                    sp.dma_start(rel[:, h % 2, :, :], skewed[bass.ds(b * H + h, 1), :, 0:2 * P * P]
                                 .rearrange("h q (t p) -> (h t) q p", p=2 * P)).then_inc(rel_in[h % 2], 16)

        @block.tensor
        def _(pe):
            pe.wait_ge(loaded, 16 * 6)
            with pe.Fori(0, B) as b:
                def m_open(m):
                    pe.wait_ge(m_free[m % 2], b * PER[m % 2] + m // 2 + 1)
                    return m_ps[m % 2]

                pe.wait_ge(xb_ready, b + 1)
                for m0, w in ((M_Q, wq), (M_K, wk)):
                    for c in range(C):
                        ps = m_open(m0 + c)
                        pe.matmul(ps[:, :], w[:, c, :], xb[:, :], start=True, stop=True).then_inc(m_full[c % 2], 1)
                for n in range(2 * QT):
                    ps = m_open(M_V + n)
                    pe.matmul(ps[:, :], xb[:, (n // 2) * P:(n // 2 + 1) * P], wv[:, n % 2, :], start=True, stop=True)\
                        .then_inc(m_full[n % 2], 1)
                for i in range(2):
                    pe.wait_ge(m_free[i], b * PER[i] + 13)

                def scores(u):
                    h, qt = u // QT, u % QT
                    k0, n = keys(qt)
                    r = slice(64 * (h % 2), 64 * (h % 2) + 64)
                    pe.wait_ge(mx_done, b * UNITS + u + QT + QT - 1)
                    pe.matmul(s_ps[u % 2][:, 0:n], qT[r, h // 2, qt * P:(qt + 1) * P], kT[r, h // 2, k0:k0 + n],
                              start=True, stop=True).then_inc(s_done, 1)

                def turn(u):
                    n = keys(u % QT)[1]
                    pe.wait_ge(exp_done, b * UNITS + u + 1)
                    pe.wait_ge(pt_copied, b * UNITS + u + 1)
                    for c in range(n // P):
                        last = pe.transpose(t_ps[u % 2][:, c * P:(c + 1) * P], prob[:, u % 2, c * P:(c + 1) * P],
                                            k.ident[:, :])
                    last.then_inc(t_done, 1)

                def values(h):
                    pe.wait_ge(pt_copied, b * UNITS + QT * (h + 1) + 2)
                    pe.wait_ge(o_free, b * H + h + 1)
                    for qt in range(QT):
                        k0, n = keys(qt)
                        for c in range(n // P):
                            last = pe.matmul(o_ps[h % 2][:, qt * DH:(qt + 1) * DH], pT[:, h % 2, qt, c * P:(c + 1) * P],
                                             val[:, k0 // P + c, h * DH:(h + 1) * DH], start=(c == 0),
                                             stop=(c == n // P - 1))
                    last.then_inc(pv_done, 1)

                for u in range(UNITS + 3):
                    if u < UNITS:
                        scores(u)
                    if 1 <= u < UNITS + 1:
                        turn(u - 1)
                    if u >= 6 and u % QT == 2:
                        values(u // QT - 1)
                pe.wait_ge(o_free, b * H + H + 2)
                for c in range(C):
                    ps = m_open(M_OT + c)
                    for qt in range(QT):
                        last = pe.transpose(ps[:, qt * P:(qt + 1) * P], o[:, qt, c * P:(c + 1) * P], k.ident[:, :])
                    last.then_inc(m_full[c % 2], 1)
                pe.wait_ge(m_free[1], b * PER[1] + 17)
                ps = m_open(M_Y)
                for qt in range(QT):
                    out = ps[:, qt * P:(qt + 1) * P]
                    for c in range(C):
                        pe.matmul(out, oT[:, c, qt * P:(qt + 1) * P], wo[:, c, :], start=(c == 0), stop=False)
                    last = pe.matmul(out, k.ones[0:1, :], bo[:, :], start=False, stop=True)
                last.then_inc(m_full[M_Y % 2], 1)

        @block.scalar
        def _(act):
            with act.Fori(0, B) as b:
                def m_wait(m):
                    act.wait_ge(m_full[m % 2], b * PER[m % 2] + m // 2 + 1)
                    return m_ps[m % 2]

                for c in range(C):
                    ps = m_wait(M_K + c)
                    act.copy(kT[:, c, :], ps[:, :]).then_inc(m_free[c % 2], 1)
                for u in range(UNITS):
                    h, qt = u // QT, u % QT
                    n = keys(qt)[1]
                    act.wait_ge(max_done, b * UNITS + u + 1)
                    act.wait_ge(t_done, b * UNITS + u + 1)
                    act.activation(prob[:, u % 2, 0:n], lg[:, u % 2, 0:n], ACT.Exp, bias=nmax[:, u % 4:u % 4 + 1],
                                   accum_out=rsum[:, h % 2, qt:qt + 1]).then_inc(exp_done, 1)
                for c in range(C):
                    ps = m_wait(M_OT + c)
                    act.copy(oT[:, c, :], ps[:, :]).then_inc(m_free[c % 2], 1)

        @block.vector
        def _(v):
            v.sem_inc(t_done, 2)
            v.sem_inc(pt_copied, 2)
            v.sem_inc(pv_done, 2)
            v.sem_inc(o_free, 2)
            v.sem_inc(m_free0, 1)
            v.sem_inc(m_free1, 1)
            v.sem_inc(mx_done, 2 * QT)
            v.wait_ge(loaded, 16 * 6)
            with v.Fori(0, B) as b:
                def m_wait(m):
                    v.wait_ge(m_full[m % 2], b * PER[m % 2] + m // 2 + 1)
                    return m_ps[m % 2]

                v.tensor_copy(xb[:, :], k.xnT[:, bass.ds(b * T, T)]).then_inc(xb_ready, 1)
                for c in range(C):
                    ps = m_wait(M_Q + c)
                    v.tensor_scalar(qT[:, c, :], ps[:, :], bq[:, c:c + 1], DH ** -0.5, ALU.add, ALU.mult)\
                        .then_inc(m_free[c % 2], 1)
                for n in range(2 * QT):
                    ps = m_wait(M_V + n)
                    v.tensor_copy(val[:, n // 2, (n % 2) * 512:(n % 2 + 1) * 512], ps[:, :]).then_inc(m_free[n % 2], 1)

                def scores_ready(u):
                    v.wait_ge(s_done, b * UNITS + u + 1)
                    if u % QT == 0:
                        v.wait_ge(rel_in[u // QT % 2], 16 * (b * (H // 2) + u // QT // 2 + 1))
                    if u >= 2:
                        v.wait_ge(exp_done, b * UNITS + u - 1)
                    else:
                        v.memset(spare[:, u:u + 1], 0.0)

                def row_max(u):
                    h, qt = u // QT, u % QT
                    n = keys(qt)[1]
                    v.tensor_tensor_reduce(lg[:, u % 2, 0:n], s_ps[u % 2][:, 0:n], rel[:, h % 2, qt, 2 * P - n:2 * P],
                                           1.0, -3.0e38, ALU.add, ALU.max, mx[:, u % 4:u % 4 + 1]).then_inc(mx_done, 1)
                    v.wait_ge(mx_done, b * UNITS + u + 1 + 2 * QT)
                    v.tensor_scalar(nmax[:, u % 4:u % 4 + 1], mx[:, u % 4:u % 4 + 1], -1.0, None, ALU.mult)\
                        .then_inc(max_done, 1)

                def copy_t(u):
                    h, qt = u // QT, u % QT
                    n = keys(qt)[1]
                    v.wait_ge(t_done, b * UNITS + u + 3)
                    if qt == 0:
                        v.wait_ge(pv_done, b * H + h + 1)
                    v.tensor_copy(pT[:, h % 2, qt, 0:n], t_ps[u % 2][:, 0:n]).then_inc(pt_copied, 1)

                def norm(h):
                    v.wait_ge(exp_done, b * UNITS + QT * (h + 1))
                    v.reciprocal(rinv[:, h % 2, :], rsum[:, h % 2, :]).then_inc(rinv_ready, 1)
                    v.wait_ge(rinv_ready, b * H + h + 1)
                    v.wait_ge(pv_done, b * H + h + 3)
                    v.tensor_tensor(o[:, :, h * DH:(h + 1) * DH],
                                    o_ps[h % 2][:, 0:QT * DH].rearrange("p (t e) -> p t e", t=QT),
                                    bc(rinv[:, h % 2, :].unsqueeze(2), [P, QT, DH]), ALU.mult).then_inc(o_free, 1)

                for u in range(UNITS + 4):
                    if u < UNITS:
                        scores_ready(u)
                    if 2 <= u < UNITS + 2:
                        copy_t(u - 2)
                    if u < UNITS:
                        row_max(u)
                    if u >= 7 and u % QT == 3:
                        norm(u // QT - 1)
                ps = m_wait(M_Y)
                xs = k.x[:, bass.ds(b * QT, QT), :]
                v.tensor_tensor(xs, ps[:, :].rearrange("p (t d) -> p t d", t=QT), xs, ALU.add)\
                    .then_inc(m_free[M_Y % 2], 1)


def switch_heads(nc, k, tag, d):
    H, E = 8, 8
    UNITS = H * QT
    pairs = {-1: [[("v", 0, i), ("v", 0, i + 2)] for i in (0, 1, 4, 5)]}
    for u in range(UNITS + 3):
        h, r = u // QT, u % QT
        hv, hy, y0 = h + 1, (h - 1 if r == 3 else h - 2), (0 if r == 3 else 2 * r + 2)
        pairs[u] = [[f for f in (("v", hv, 2 * r + i), ("y", hy, y0 + i)) if 0 <= f[1] < (H if f[0] == "v" else H - 1)]
                    for i in range(2)]
    pairs[UNITS + 3] = [[("y", H - 1, i), ("y", H - 1, i + 2)] for i in (0, 1, 4, 5)]
    LAST = UNITS + 3

    def is_turned(u):
        return u // QT - 1 if u % QT == 2 and u >= QT else None

    order = []
    for u in range(-1, LAST + 1):
        if u == -1 or u % QT == 0 and u // QT + 1 < H:
            order += [("q", (u + QT) // QT if u >= 0 else 0), ("k", (u + QT) // QT if u >= 0 else 0)]
        order += pairs[u][0]
        if is_turned(u) is not None:
            order += [("t", is_turned(u))]
        for pair in pairs[u][1:]:
            order += pair
    place = {name: n for n, name in enumerate(order)}
    PER = len(order) // 4
    LINKS = 3 * 2 * H * 2 * QT
    with ExitStack() as ctx:
        ph = Phase(nc, ctx, tag)
        wq = ph.sb("wq", [P, H, P])
        wk = ph.sb("wk", [P, H, P])
        wv = ph.sb("wv", [P, 2, 2, 512])
        wo = ph.sb("wo", [P, 2, 2, 512])
        xb = ph.sb("xb", [P, T])
        gs = ph.sb("gs", [P, QT, 2, H, E])
        acc = ph.sb("acc", [P, QT, P])
        qT = ph.sb("qT", [P, 2, T])
        kT = ph.sb("kT", [P, 2, T])
        val = ph.sb("val", [P, 3, QT, P])
        nmax = ph.sb("nmax", [P, 4])
        prob = ph.sb("prob", [P, 2, T])
        pT = ph.sb("pT", [P, 2, QT, T])
        rsum = ph.sb("rsum", [P, 2, QT])
        rinv = ph.sb("rinv", [P, 2, QT])
        o = ph.sb("o", [P, 2, QT, P])
        oT = ph.sb("oT", [P, 2, T])
        s_ps = ph.banks("s", 2)
        t_ps, o_ps = ph.banks("t", 1), ph.banks("o", 1)
        m_ps = ph.banks("m", 4)
        m_full = [ph.sem(f"m_full{i}") for i in range(4)]
        m_free = [ph.sem(f"m_free{i}") for i in range(4)]
        loaded, wv_in0, wv_in1, wo_in0, wo_in1, xb_ready, gs_ready, link, v_ready, y_ready = (ph.sem(s) for s in (
            "loaded", "wv_in0", "wv_in1", "wo_in0", "wo_in1", "xb_ready", "gs_ready", "link", "v_ready", "y_ready"))
        s_done, max_done, exp_done, t_done, pt_copied, pv_done, o_ready, rinv_ready, added = (
            ph.sem(s) for s in ("s_done", "max_done", "exp_done", "t_done", "pt_copied", "pv_done", "o_ready",
                                "rinv_ready", "added"))
        wv_in, wo_in = (wv_in0, wv_in1), (wo_in0, wo_in1)
        block = ctx.enter_context(nc.Block())

        @block.sync
        def _(sp):
            for dst, src in ((wq[:, :, :], d["f3_wq"]), (wk[:, :, :], d["f3_wk"])):
                sp.dma_start(dst, src).then_inc(loaded, 16)
            with sp.Fori(0, B) as b:
                for h in range(H + 2):
                    if h < H:
                        sp.wait_ge(v_ready, b * H + h + 1)
                        sp.dma_start(wv[:, h % 2, :, :], d["f3_wv"][h]).then_inc(wv_in[h % 2], 16)
                    if h >= 2:
                        sp.wait_ge(y_ready, b * H + h - 1)
                        sp.dma_start(wo[:, h % 2, :, :], d["f3_wo"][h - 2]).then_inc(wo_in[h % 2], 16)

        @block.tensor
        def _(pe):
            pe.wait_ge(loaded, 32)
            with pe.Fori(0, B) as b:
                def m_open(*name):
                    n = place[name]
                    pe.wait_ge(m_free[n % 4], b * PER + n // 4 + 1)
                    return m_ps[n % 4], m_full[n % 4]

                def m_read(*name):
                    n = place[name]
                    pe.wait_ge(m_free[n % 4], b * PER + n // 4 + 2)

                def queries_keys(h):
                    for kind, w in (("q", wq), ("k", wk)):
                        ps, full = m_open(kind, h)
                        pe.matmul(ps[:, :], w[:, h, :], xb[:, :], start=True, stop=True).then_inc(full, 1)

                def fill(pair):
                    for kind, h, i in pair:
                        ps, full = m_open(kind, h, i)
                        if kind == "v":
                            left, w, w_in = xb[:, (i // 2) * P:(i // 2 + 1) * P], wv, wv_in
                        else:
                            left, w, w_in = oT[:, h % 2, (i // 2) * P:(i // 2 + 1) * P], wo, wo_in
                        if i == 0:
                            pe.wait_ge(w_in[h % 2], 16 * (b * (H // 2) + h // 2 + 1))
                        pe.matmul(ps[:, :], left, w[:, h % 2, i % 2, :], start=True, stop=True).then_inc(full, 1)

                def scores(u):
                    h, qt = u // QT, u % QT
                    if qt == 0:
                        m_read("q", h)
                        m_read("k", h)
                    pe.wait_ge(exp_done, b * UNITS + u + 1)
                    pe.matmul(s_ps[u % 2][:, :], qT[:, h % 2, qt * P:(qt + 1) * P], kT[:, h % 2, :],
                              start=True, stop=True).then_inc(s_done, 1)

                def turn(u):
                    pe.wait_ge(exp_done, b * UNITS + u + 3)
                    pe.wait_ge(pt_copied, b * UNITS + u + 1)
                    for kt in range(QT):
                        last = pe.transpose(t_ps[0][:, kt * P:(kt + 1) * P], prob[:, u % 2, kt * P:(kt + 1) * P],
                                            k.ident[:, :])
                    last.then_inc(t_done, 1)

                def values(h):
                    pe.wait_ge(pt_copied, b * UNITS + QT * (h + 1) + 1)
                    m_read("v", h, 2 * QT - 1)
                    pe.wait_ge(o_ready, b * H + h + 1)
                    for qt in range(QT):
                        for kt in range(QT):
                            last = pe.matmul(o_ps[0][:, qt * P:(qt + 1) * P], pT[:, h % 2, kt, qt * P:(qt + 1) * P],
                                             val[:, h % 3, kt, :], start=(kt == 0), stop=(kt == QT - 1))
                    last.then_inc(pv_done, 1)

                def turn_out(h):
                    pe.wait_ge(o_ready, b * H + h + 2)
                    ps, full = m_open("t", h)
                    for qt in range(QT):
                        last = pe.transpose(ps[:, qt * P:(qt + 1) * P], o[:, h % 2, qt, :], k.ident[:, :])
                    last.then_inc(full, 1)

                pe.wait_ge(xb_ready, b + 1)
                queries_keys(0)
                for pair in pairs[-1]:
                    fill(pair)
                for u in range(LAST + 1):
                    if u < UNITS:
                        scores(u)
                    if u % QT == 0 and u // QT + 1 < H:
                        queries_keys(u // QT + 1)
                    if u == LAST or u % QT == 3 and u > QT:
                        m_read("t", u // QT - 1)
                    fill(pairs[u][0])
                    if 1 <= u <= UNITS:
                        turn(u - 1)
                    if u % QT == 1 and u > QT:
                        values(u // QT - 1)
                    if is_turned(u) is not None:
                        turn_out(is_turned(u))
                    for pair in pairs[u][1:]:
                        fill(pair)

        @block.scalar
        def _(act):
            act.sem_inc(exp_done, 2)
            act.sem_inc(pt_copied, 1)
            with act.Fori(0, B) as b:
                def m_wait(*name):
                    n = place[name]
                    act.wait_ge(m_full[n % 4], b * PER + n // 4 + 1)
                    return m_ps[n % 4], m_free[n % 4]

                def queries_keys(h):
                    ps, free = m_wait("q", h)
                    act.mul(qT[:, h % 2, :], ps[:, :], float(P) ** -0.5).then_inc(free, 1)
                    ps, free = m_wait("k", h)
                    act.copy(kT[:, h % 2, :], ps[:, :]).then_inc(free, 1)

                queries_keys(0)
                for u in range(LAST):
                    if u % QT == 0 and u // QT + 1 < H:
                        queries_keys(u // QT + 1)
                    if 1 <= u <= UNITS:
                        h, qt = (u - 1) // QT, (u - 1) % QT
                        act.wait_ge(t_done, b * UNITS + u + 2)
                        act.copy(pT[:, h % 2, :, qt * P:(qt + 1) * P],
                                 t_ps[0][:, :].rearrange("p (a q) -> p a q", q=P)).then_inc(pt_copied, 1)
                    if u < UNITS:
                        h, qt = u // QT, u % QT
                        act.wait_ge(max_done, b * UNITS + u + 1)
                        act.wait_ge(t_done, b * UNITS + u + 1)
                        act.activation(prob[:, u % 2, :], s_ps[u % 2][:, :], ACT.Exp, bias=nmax[:, u % 4:u % 4 + 1],
                                       accum_out=rsum[:, h % 2, qt:qt + 1]).then_inc(exp_done, 1)
                    if is_turned(u) is not None:
                        h = is_turned(u)
                        ps, free = m_wait("t", h)
                        act.copy(oT[:, h % 2, :], ps[:, :]).then_inc(free, 1)

        @block.vector
        def _(v):
            v.sem_inc(t_done, 2)
            v.sem_inc(v_ready, 2)
            v.sem_inc(y_ready, 2)
            v.sem_inc(o_ready, 1)
            for s in m_free:
                v.sem_inc(s, 1)
            with v.Fori(0, B) as b:
                links = [0]

                v.tensor_copy(xb[:, :], k.xnT[:, bass.ds(b * T, T)]).then_inc(xb_ready, 1)
                v.tensor_copy(gs[:, :, :, :, :].rearrange("p i s h e -> p (i s h e)"),
                              k.gate[:, bass.ds(b * QT * 2 * H * E, QT * 2 * H * E)]).then_inc(gs_ready, 1)
                v.wait_ge(gs_ready, 2 * b + 1)
                v.tensor_copy(acc[:, :, :], k.x[:, bass.ds(b * QT, QT), :]).then_inc(gs_ready, 1)
                v.wait_ge(gs_ready, 2 * b + 2)

                def summed(*name):
                    n = place[name]
                    v.wait_ge(m_free[n % 4], b * PER + n // 4 + 2)

                def gather(pair):
                    count = [0] * len(pair)
                    for e in range(4):
                        for j, (kind, h, i) in enumerate(pair):
                            n = place[(kind, h, i)]
                            ps, free = m_ps[n % 4], m_free[n % 4]
                            if kind == "v":
                                out, s = val[:, h % 3, i // 2, :], 0
                            else:
                                out, s = acc[:, i // 2, :], 1
                            g = gs[:, i // 2, s, h, 4 * (i % 2) + e:4 * (i % 2) + e + 1]
                            if e == 0:
                                if i % 2 == 1:
                                    summed(kind, h, i - 1)
                                elif kind == "y" and h >= 1:
                                    summed(kind, h - 1, i + 1)
                                v.wait_ge(m_full[n % 4], b * PER + n // 4 + 1)
                            else:
                                v.wait_ge(link, b * LINKS + count[j])
                            if kind == "v" and i % 2 == 0 and e == 0:
                                ins = v.tensor_scalar(out, ps[:, 0:P], g, None, ALU.mult)
                            else:
                                ins = v.scalar_tensor_tensor(out, ps[:, e * P:(e + 1) * P], g, out, ALU.mult, ALU.add)
                            if e == 3:
                                ins.then_inc(free, 1)
                            else:
                                ins.then_inc(link, 1)
                                links[0] += 1
                                count[j] = links[0]
                    for kind, h, i in pair:
                        if i == 2 * QT - 1:
                            summed(kind, h, i)
                            v.sem_inc(v_ready if kind == "v" else y_ready, 1)

                def normalised(h):
                    v.wait_ge(exp_done, b * UNITS + QT * (h + 1) + 2)
                    v.reciprocal(rinv[:, h % 2, :], rsum[:, h % 2, :]).then_inc(rinv_ready, 1)
                    v.wait_ge(rinv_ready, b * H + h + 1)
                    v.wait_ge(pv_done, b * H + h + 1)
                    v.tensor_tensor(o[:, h % 2, :, :], o_ps[0][:, :].rearrange("p (t e) -> p t e", t=QT),
                                    bc(rinv[:, h % 2, :].unsqueeze(2), [P, QT, P]), ALU.mult).then_inc(o_ready, 1)

                for pair in pairs[-1]:
                    gather(pair)
                for u in range(LAST + 1):
                    if u < UNITS:
                        v.wait_ge(s_done, b * UNITS + u + 1)
                        v.tensor_reduce(nmax[:, u % 4:u % 4 + 1], s_ps[u % 2][:, :], AX.X, ALU.max, negate=True)\
                            .then_inc(max_done, 1)
                    gather(pairs[u][0])
                    if u % QT == 1 and u > QT:
                        normalised(u // QT - 1)
                    for pair in pairs[u][1:]:
                        gather(pair)
                v.tensor_copy(k.x[:, bass.ds(b * QT, QT), :], acc[:, :, :]).then_inc(added, 1)
                v.wait_ge(added, b + 1)


def layer3(nc, k, d):
    token_logits(nc, k, "r3", d["f3_wr"], P)
    top2_gates(nc, k, "g3", 16, "sigmoid", scale_dram=d["f3_scale"])
    band = nc.dram_tensor("band", (P + B * 16 * T * 257,), F32, kind="Internal").ap()
    relative_rows(nc, k, "b3", d, band)
    switch_heads(nc, k, "f3", d)
    relative_heads(nc, k, "a3", d, band)


def layer3_layout(a, d):
    f = np.float32
    z = np.zeros((P, 4, 4, 32), f)
    z[..., 0:10] = a["L3_attn_Wr"].reshape(P, 4, 4, 10)
    d["a3_wr"] = z.reshape(P, 4, P)
    z = np.zeros((4, 4, 32), f)
    z[..., 0:10] = a["L3_attn_br"].reshape(4, 4, 10)
    d["a3_br"] = z.reshape(4, P).T
    z = np.zeros((4, 32, P), f)
    z[:, 0:10, :] = a["L3_attn_b_nd"][None, :, ::-1]
    d["a3_rel"] = z.reshape(P, P)
    d["a3_wq"], d["a3_wk"] = (a["L3_attn_" + n].reshape(P, 8, P) for n in ("Wq", "Wk"))
    d["a3_wv"] = a["L3_attn_Wv"].reshape(P, 2, 512)
    d["a3_bq"] = a["L3_attn_bq"].reshape(8, P).T
    d["a3_wo"] = a["L3_attn_Wproj"].reshape(8, P, P).transpose(1, 0, 2)
    d["a3_bo"] = a["L3_attn_bproj"][None]
    d["f3_wr"] = np.concatenate([a["L3_ffn_sel_v_w"], a["L3_ffn_sel_o_w"]]).T
    d["f3_scale"] = np.tile(a["L3_ffn_route_scale"], (P, 1))
    d["f3_wq"], d["f3_wk"] = (a["L3_ffn_" + n].reshape(8, P, P).transpose(2, 0, 1) for n in ("q_w", "k_w"))
    for n, s in (("f3_wv", "v_w"), ("f3_wo", "o_w")):
        d[n] = a["L3_ffn_" + s].reshape(8, 2, 4, P, P).transpose(0, 3, 1, 2, 4).reshape(8, P, 2, 512)

STOP = 6



class State:
    pass


def program(nc, d, out, stop_after):
    with ExitStack() as ctx:
        def sb(name, shape, dtype=F32):
            return ctx.enter_context(nc.sbuf_tensor(name, shape, dtype))

        k = State()
        Phase.counted = []
        k.x = sb("x", [P, NT, P])
        k.xn = sb("xn", [P, NT, P])
        k.xnT = sb("xnT", [P, N])
        k.ident = sb("ident", [P, P])
        k.ident_bf = sb("ident_bf", [P, P], BF16)
        k.ones = sb("ones", [1, P])
        k.ones_bf = sb("ones_bf", [P, P], BF16)
        k.earlier = sb("earlier", [P, P], BF16)
        k.later = sb("later", [P, P], BF16)
        k.iota = sb("iota", [P, 64])
        k.logits = sb("logits", [P, NT * P])

        with ExitStack() as c1:
            ph = Phase(nc, c1, "setup")
            tmp = ph.sb("tmp", [P, 2, P])
            loaded, made = ph.sem("loaded"), ph.sem("made")
            block = c1.enter_context(nc.Block())

            @block.sync
            def _(sp):
                for dst, src in ((k.x[:, :, :], d["x"].rearrange("(t p) d -> p t d", p=P)), (k.ident[:, :], d["ident"]),
                                 (tmp[:, 0, :], d["earlier"]), (tmp[:, 1, :], d["later"]), (k.iota[:, :], d["iota"])):
                    sp.dma_start(dst, src).then_inc(loaded, 16)

            @block.vector
            def _(v):
                v.memset(k.ones[:, :], 1.0).then_inc(made, 1)
                v.memset(k.ones_bf[:, :], 1.0).then_inc(made, 1)
                v.wait_ge(loaded, 80)
                v.tensor_copy(k.ident_bf[:, :], k.ident[:, :]).then_inc(made, 1)
                v.tensor_copy(k.earlier[:, :], tmp[:, 0, :]).then_inc(made, 1)
                v.tensor_copy(k.later[:, :], tmp[:, 1, :]).then_inc(made, 1)
                v.wait_ge(made, 5)

        layer_norm(nc, k, "n0")
        if stop_after >= 0:
          with ExitStack() as c2:
            k.v = c2.enter_context(nc.sbuf_tensor("v0", [P, NT, P], F32))
            parts = nc.dram_tensor("parts0", (2, 3, P, N), BF16, kind="Internal").ap()
            split_heads(nc, k, "q0", d["a0_wq"], d["a0_wk"], d["a0_wv"], d["a0_bq"], d["a0_bk"], d["a0_bv"],
                        8 ** -0.5, parts, None)
            small_heads(nc, k, "a0", parts, d["a0_wo"], d["a0_bo"], None, False)
        if stop_after >= 1:
          token_logits(nc, k, "r0", d["f0_wr"], 64)
          with ExitStack() as c2:
            k.weight = c2.enter_context(nc.sbuf_tensor("weight", [P, NT, 64], F32))
            k.place = c2.enter_context(nc.sbuf_tensor("place", [P, NT, 64], F32))
            k.slots_x = c2.enter_context(nc.sbuf_tensor("slots_x", [P, 64 * 32], F32))
            k.slots_y = c2.enter_context(nc.sbuf_tensor("slots_y", [P, 16, P], F32))
            top8_slots(nc, k, "p0")
            slot_dispatch(nc, k, "d0")
            slot_experts(nc, k, "e0", d["f0_wgu"], d["f0_wd"])
            slot_combine(nc, k, "c0")
        if stop_after >= 2:
          Phase.retire(nc)
          layer_norm(nc, k, "n1")
          with ExitStack() as c2:
            k.v = c2.enter_context(nc.sbuf_tensor("v1", [P, NT, P], F32))
            parts = nc.dram_tensor("parts1", (2, 3, P, N), BF16, kind="Internal").ap()
            f_parts = nc.dram_tensor("f_parts", (2, 3, P, T), BF16, kind="Internal").ap()
            split_heads(nc, k, "q1", d["a1_wq"], d["a1_wk"], d["a1_wv"], d["a1_bz"], d["a1_bz"], d["a1_br"],
                        8 ** -0.5, parts, (d["a1_fa"], d["a1_trig"], f_parts))
            small_heads(nc, k, "a1", parts, d["a1_wo"], d["a1_br"], f_parts, True)
        if stop_after >= 3:
          with ExitStack() as c2:
            k.gate = c2.enter_context(nc.sbuf_tensor("gate1", [P, NT * 8], F32))
            token_logits(nc, k, "r1", d["f1_wr"], 8, d["f1_br"])
            top2_gates(nc, k, "g1", 1, "softmax2")
            gated_ffn(nc, k, "f1", d["f1_w0"], d["f1_w1"], d["f1_w2"], d["f1_b0"], d["f1_b1"], d["f1_b2"])
        if stop_after >= 4:
          Phase.retire(nc)
          layer_norm(nc, k, "n2")
          selective_scan(nc, k, "s2", {n[3:]: a for n, a in d.items() if n.startswith("s2_")})
        if stop_after >= 5:
          with ExitStack() as c2:
            k.gate = c2.enter_context(nc.sbuf_tensor("gate2", [P, NT * 8], F32))
            token_logits(nc, k, "r2", d["f2_wr"], 8)
            top2_gates(nc, k, "g2", 1, "capacity", capacity=N * 5 // 32)
            shared_ffn(nc, k, "f2", d["f2_wg"], d["f2_wd"])
        if stop_after >= 6:
          Phase.retire(nc)
          layer_norm(nc, k, "n3")
          with ExitStack() as c2:
            k.gate = c2.enter_context(nc.sbuf_tensor("gate3", [P, NT * P], F32))
            layer3(nc, k, d)

        with ExitStack() as c1:
            ph = Phase(nc, c1, "store")
            stored = ph.sem("stored")
            block = c1.enter_context(nc.Block())

            @block.sync
            def _(sp):
                sp.dma_start(out.rearrange("b (t p) d -> p (b t) d", p=P), k.x[:, :, :]).then_inc(stored, 16)
                sp.wait_ge(stored, 16)


def laid_out(a):
    def col(v, n):
        return np.ascontiguousarray(v.reshape(n, 128).T)

    d = {}
    f = np.float32
    d["x"] = a["L0_attn_x"].reshape(N, P)
    d["ident"] = np.eye(P, dtype=f)
    d["earlier"] = np.triu(np.ones((P, P), f), 1)
    d["later"] = np.triu(np.full((P, P), -BIG, f), 1)
    d["iota"] = np.tile(np.arange(64, dtype=f), (P, 1))
    w, bias = a["L0_attn_qkv_w"], a["L0_attn_qkv_b"]
    d["a0_wq"], d["a0_wk"], d["a0_wv"] = w[:, 0:128], w[:, 128:256], w[:, 256:384]
    d["a0_bq"], d["a0_bk"] = bias[0:128, None], bias[128:256, None]
    d["a0_bv"], d["a0_bo"] = bias[None, 256:384], a["L0_attn_proj_b"][None]
    d["a0_wo"] = a["L0_attn_proj_w"]
    d["f0_wr"] = a["L0_ffn_gate_w"].T
    gu = np.concatenate([a["L0_ffn_w_gate"], a["L0_ffn_w_up"]], axis=1)
    d["f0_wgu"] = gu.reshape(16, 4, 192, P).transpose(0, 3, 1, 2)
    d["f0_wd"] = a["L0_ffn_w_down"].reshape(16, 4, P, 96).transpose(0, 3, 1, 2)
    w = a["L1_attn_Wqkv"].T
    d["a1_wq"], d["a1_wk"], d["a1_wv"] = w[:, 0:128], w[:, 128:256], w[:, 256:384]
    d["a1_bz"], d["a1_br"] = np.zeros((P, 1), f), np.zeros((1, P), f)
    d["a1_wo"] = a["L1_attn_Wout"].T
    fa = np.zeros((12, 16, 8), f)
    al, be = a["L1_attn_alpha"], a["L1_attn_beta"]
    for r in range(4):
        fa[r, :, r], fa[4 + r, :, r] = al[:, r], be[:, r]
        fa[4 + r, :, 4 + r], fa[8 + r, :, 4 + r] = al[:, r], be[:, r]
    d["a1_fa"] = fa.reshape(12, P)
    ang = (10000.0 ** (-2.0 * np.arange(4) / 8))[:, None] * np.arange(T)[None, :]
    d["a1_trig"] = np.concatenate([np.cos(ang), np.sin(ang), -np.cos(ang)]).astype(f)
    d["f1_wr"], d["f1_br"] = a["L1_ffn_Wg"], a["L1_ffn_bg"][None]
    for n, s in (("f1_w0", "W0"), ("f1_w1", "W1")):
        d[n] = a["L1_ffn_" + s].reshape(8, P, 4, P).transpose(1, 0, 2, 3)
    d["f1_w2"] = a["L1_ffn_W2"].reshape(8, 4, P, P).transpose(2, 0, 1, 3)
    d["f1_b0"], d["f1_b1"] = col(a["L1_ffn_b0"], 32), col(a["L1_ffn_b1"], 32)
    d["f1_b2"] = a["L1_ffn_b2"]
    d["s2_w_in"], d["s2_w_x"] = a["L2_attn_in_proj_w"].T, a["L2_attn_x_proj_w"].T
    d["s2_w_dt"], d["s2_w_o"] = a["L2_attn_dt_proj_w"].T, a["L2_attn_out_proj_w"].T
    d["s2_b_o"], d["s2_b_in"] = a["L2_attn_out_proj_b"][None], col(a["L2_attn_in_proj_b"], 2)
    xb = a["L2_attn_x_proj_b"]
    d["s2_b_dl"], d["s2_b_bc"] = xb[0:16, None], col(xb[16:], 2)
    d["s2_b_dt"], d["s2_dpar"], d["s2_a_log"] = a["L2_attn_dt_proj_b"][:, None], a["L2_attn_D_param"][:, None], a["L2_attn_A_log"]
    d["f2_wr"] = a["L2_ffn_w_router"].T
    d["f2_wg"] = a["L2_ffn_w_gate"].T.reshape(P, 2, P)
    d["f2_wd"] = a["L2_ffn_w_down"].transpose(2, 0, 1).reshape(2, P, 8, P).transpose(1, 0, 2, 3)
    layer3_layout(a, d)
    return {n: np.ascontiguousarray(v) for n, v in d.items()}


def kernel(**inputs):
    import concourse.bacc as bacc
    from concourse.bass_utils import run_bass_kernel_spmd

    nc = bacc.Bacc("TRN2", target_bir_lowering=False, num_devices=1)
    nc.disable_value_cache = True
    arrays = laid_out({n: np.asarray(v) for n, v in inputs.items()})
    aps = {n: nc.dram_tensor(f"{n}_in", v.shape, F32, kind="ExternalInput").ap() for n, v in arrays.items()}
    out = nc.dram_tensor("out_dram", (B, T, P), F32, kind="ExternalOutput").ap()
    program(nc, aps, out, STOP)
    r = run_bass_kernel_spmd(nc, [{f"{n}_in": v for n, v in arrays.items()}], core_ids=[0])
    return r.results[0]["out_dram"]
```

```python
from contextlib import ExitStack

import numpy as np

import concourse.bass as bass
from concourse import mybir

F32 = mybir.dt.float32
BF16 = mybir.dt.bfloat16
I32 = mybir.dt.int32
ALU = mybir.AluOpType
ACT = mybir.ActivationFunctionType
AX = mybir.AxisListType

P = 128
B, T = 4, 512
N = B * T
NT = N // P
QT = T // P
EPS = 1e-5
BIG = 1.0e30


def bc(ap, shape):
    return ap.broadcast_to(shape)


class Phase:

    counted = []

    def __init__(self, nc, ctx, tag):
        self.nc, self.ctx, self.tag = nc, ctx, tag

    def sem(self, name):
        s = self.nc.alloc_semaphore(f"{self.tag}_{name}")
        self.counted.append(s)
        return s

    @classmethod
    def retire(cls, nc):
        nc.clear_and_free_semaphores(cls.counted)
        cls.counted = []
        nc.all_engine_barrier()

    def sb(self, name, shape, dtype=F32):
        return self.ctx.enter_context(self.nc.sbuf_tensor(f"{self.tag}_{name}", shape, dtype))

    def banks(self, name, n):
        return [self.ctx.enter_context(self.nc.psum_tensor(f"{self.tag}_{name}{i}", [P, 512], F32)) for i in range(n)]


def layer_norm(nc, k, tag):
    with ExitStack() as ctx:
        ph = Phase(nc, ctx, tag)
        stats = ph.sb("stats", [P, NT, 6])
        mv = ph.sb("mv", [P, NT, 2])
        ve = ph.sb("ve", [P, NT])
        std = ph.sb("std", [P, NT])
        y = ph.sb("y", [P, NT])
        t = ph.sb("t", [P, NT])
        tps = ph.banks("tps", 4)
        chain, var_ready, std_ready, xn_ready, turned = (ph.sem(s) for s in (
            "chain", "var_ready", "std_ready", "xn_ready", "turned"))
        copied = ph.sem("copied")
        block = ctx.enter_context(nc.Block())

        @block.vector
        def _(v):
            done = [0]

            def link(ins):
                done[0] += 1
                ins.then_inc(chain, 1)

            def settle():
                v.wait_ge(chain, done[0])

            for i in range(NT):
                link(v.bn_stats(stats[:, i, :], k.x[:, i, :]))
            settle()
            for i in range(NT):
                link(v.bn_aggr(mv[:, i, :], stats[:, i, :]))
            settle()
            v.tensor_scalar(ve[:, :], mv[:, :, 1], EPS, None, ALU.add).then_inc(var_ready, 1)
            v.wait_ge(std_ready, 1)
            link(v.reciprocal(y[:, :], std[:, :]))
            settle()
            for _ in range(2):
                link(v.tensor_tensor(t[:, :], y[:, :], y[:, :], ALU.mult))
                settle()
                link(v.tensor_tensor(t[:, :], t[:, :], ve[:, :], ALU.mult))
                settle()
                link(v.tensor_scalar(t[:, :], t[:, :], -0.5, 1.5, ALU.mult, ALU.add))
                settle()
                link(v.tensor_tensor(y[:, :], y[:, :], t[:, :], ALU.mult))
                settle()
            for i in range(NT):
                v.tensor_scalar(k.xn[:, i, :], k.x[:, i, :], mv[:, i, 0:1], y[:, i:i + 1],
                                ALU.subtract, ALU.mult).then_inc(xn_ready, 1)

        @block.tensor
        def _(pe):
            for i in range(NT):
                pe.wait_ge(xn_ready, i + 1)
                pe.transpose(tps[i // 4][:, (i % 4) * P:(i % 4 + 1) * P], k.xn[:, i, :],
                             k.ident[:, :]).then_inc(turned, 1)

        @block.scalar
        def _(act):
            act.wait_ge(var_ready, 1)
            act.activation(std[:, :], ve[:, :], ACT.Sqrt).then_inc(std_ready, 1)
            for j in range(4):
                act.wait_ge(turned, 4 * j + 4)
                act.copy(k.xnT[:, j * 512:(j + 1) * 512], tps[j][:, :]).then_inc(copied, 1)
            act.wait_ge(copied, 4)


PAIRS = ((0, 0), (0, 1), (1, 0), (1, 1), (0, 2), (2, 0))
MR = 96


def head_tiles(nc, ctx, k, tag):
    k.qp = ctx.enter_context(nc.sbuf_tensor(f"{tag}_qp", [P, 16, T], BF16))
    k.kp = ctx.enter_context(nc.sbuf_tensor(f"{tag}_kp", [P, 16, T], BF16))
    k.vp = ctx.enter_context(nc.sbuf_tensor(f"{tag}_vp", [P, 4, QT, 4, 32], F32))
        


def split_heads(nc, k, tag, w_q, w_k, w_v, q_bias, k_bias, v_bias, scale, parts, fourier):
    with ExitStack() as ctx:
        ph = Phase(nc, ctx, tag)
        wq, wk, wv = (ph.sb(s, [P, P]) for s in ("wq", "wk", "wv"))
        qb, kb = ph.sb("qb", [P, 1]), ph.sb("kb", [P, 1])
        vb = ph.sb("vb", [1, P])
        whole = ph.sb("whole", [P, 2, N])
        rest = ph.sb("rest", [P, 2, N])
        part = ph.sb("part", [P, 2, 3, N], BF16)
        q_ps, k_ps = ph.banks("q", 2), ph.banks("k", 2)
        v_ps = ph.banks("v", 3 if fourier else 4)
        NV = len(v_ps)
        loaded, full_q, full_k, full_v, read_q, read_k, read_v, c1, c2, c3, c4, stored = (ph.sem(s) for s in (
            "loaded", "full_q", "full_k", "full_v", "read_q", "read_k", "read_v", "first", "rest1", "second",
            "third", "stored"))
        filled = ph.sem("filled")
        n_loads = 6
        if fourier:
            fa, trig = ph.sb("fa", [12, P]), ph.sb("trig", [12, T])
            f_whole, f_rest = ph.sb("f_whole", [P, T]), ph.sb("f_rest", [P, 2, T])
            f_part = ph.sb("f_part", [P, 2, 3, T], BF16)
            f_ps = ph.banks("f", 1)[0]
            full_f, f_chain = ph.sem("full_f"), ph.sem("f_chain")
            n_loads += 2
        block = ctx.enter_context(nc.Block())

        @block.gpsimd
        def _(pool):
            pool.memset(k.qp[:, :, :], 0.0).then_inc(filled, 1)
            pool.memset(k.kp[:, :, :], 0.0).then_inc(filled, 1)
            pool.memset(k.vp[:, :, :, :, :], 0.0).then_inc(filled, 1)
            pool.wait_ge(filled, 3)
            pool.memset(k.kp[MR:MR + 3, :, :], 1.0).then_inc(filled, 1)
            pool.wait_ge(filled, 4)
            pool.memset(k.vp[:, :, :, :, 8:9], 1.0).then_inc(filled, 1)
            pool.wait_ge(filled, 5)

        @block.sync
        def _(sp):
            pairs = [(wq[:, :], w_q), (wk[:, :], w_k), (wv[:, :], w_v), (qb[:, :], q_bias), (kb[:, :], k_bias),
                     (vb[:, :], v_bias)]
            if fourier:
                pairs += [(fa[:, :], fourier[0]), (trig[:, :], fourier[1])]
            for dst, src in pairs:
                sp.dma_start(dst, src).then_inc(loaded, 16)
            for i, sem in ((0, c1), (1, c3), (2, c4)):
                for s in range(2):
                    sp.wait_ge(sem, 2)
                    sp.dma_start(parts[s, i], part[:, s, i, :]).then_inc(stored, 16)
            n = 6
            if fourier:
                sp.wait_ge(f_chain, 9)
                sp.dma_start(fourier[2][0].rearrange("i h t -> h i t"), f_part[:, 0, :, :]).then_inc(stored, 16)
                sp.dma_start(fourier[2][1, :, 0:8].rearrange("i h t -> h i t"), f_part[0:8, 1, :, :]).then_inc(stored, 16)
                n = 8
            sp.wait_ge(stored, 16 * n)

        @block.tensor
        def _(pe):
            pe.wait_ge(loaded, 16 * n_loads)
            if fourier:
                pe.matmul(f_ps[:, :], fa[:, :], trig[:, :], start=True, stop=True).then_inc(full_f, 1)
            for c in range(B):
                for w, ps, full, read in ((wq, q_ps, full_q, read_q), (wk, k_ps, full_k, read_k)):
                    if c >= 2:
                        pe.wait_ge(read, c - 1)
                    pe.matmul(ps[c % 2][:, :], w[:, :], k.xnT[:, c * T:(c + 1) * T], start=True, stop=True)\
                        .then_inc(full, 1)
            for c in range(B):
                if c >= NV:
                    pe.wait_ge(read_v, c - NV + 1)
                for i in range(QT):
                    out = v_ps[c % NV][:, i * P:(i + 1) * P]
                    pe.matmul(out, k.xnT[:, (c * QT + i) * P:(c * QT + i + 1) * P], wv[:, :], start=True, stop=False)
                    last = pe.matmul(out, k.ones[0:1, :], vb[:, :], start=False, stop=True)
                last.then_inc(full_v, 1)

        @block.scalar
        def _(act):
            act.wait_ge(loaded, 16 * n_loads)
            for c in range(B):
                act.wait_ge(full_k, c + 1)
                act.activation(whole[:, 1, c * T:(c + 1) * T], k_ps[c % 2][:, :], ACT.Identity, bias=kb[:, 0:1])\
                    .then_inc(read_k, 1)
            act.wait_ge(read_k, B)
            act.copy(part[:, 1, 0, :], whole[:, 1, :]).then_inc(c1, 1)
            for c in range(B):
                act.wait_ge(full_v, c + 1)
                act.copy(k.v[:, c * QT:(c + 1) * QT, :].rearrange("p i d -> p (i d)"), v_ps[c % NV][:, :])\
                    .then_inc(read_v, 1)
            for s, sem in ((1, c2), (0, c2)):
                act.wait_ge(sem, 2 - s)
                act.copy(part[:, s, 1, :], rest[:, s, :]).then_inc(c3, 1)
            act.wait_ge(read_v, B)

        @block.vector
        def _(v):
            v.wait_ge(loaded, 16 * n_loads)
            for c in range(B):
                v.wait_ge(full_q, c + 1)
                v.tensor_scalar(whole[:, 0, c * T:(c + 1) * T], q_ps[c % 2][:, :], qb[:, 0:1], scale, ALU.add, ALU.mult)\
                    .then_inc(read_q, 1)
            v.wait_ge(read_q, B)
            v.tensor_copy(part[:, 0, 0, :], whole[:, 0, :]).then_inc(c1, 1)
            v.wait_ge(c1, 2)
            for s in (1, 0):
                v.tensor_tensor(rest[:, s, :], whole[:, s, :], part[:, s, 0, :], ALU.subtract).then_inc(c2, 1)
            if fourier:
                v.wait_ge(full_f, 1)
                n = [0]

                def link(ins):
                    n[0] += 1
                    ins.then_inc(f_chain, 1)
                    v.wait_ge(f_chain, n[0])

                link(v.tensor_copy(f_whole[:, :], f_ps[:, :]))
                for s, rows, src in ((0, P, f_whole), (1, 8, trig)):
                    link(v.tensor_copy(f_part[0:rows, s, 0, :], src[0:rows, :]))
                    link(v.tensor_tensor(f_rest[0:rows, s, :], src[0:rows, :], f_part[0:rows, s, 0, :], ALU.subtract))
                    link(v.tensor_copy(f_part[0:rows, s, 1, :], f_rest[0:rows, s, :]))
                    link(v.tensor_tensor(f_part[0:rows, s, 2, :], f_rest[0:rows, s, :], f_part[0:rows, s, 1, :],
                                         ALU.subtract))
            v.wait_ge(c3, 2)
            for s in (1, 0):
                v.tensor_tensor(part[:, s, 2, :], rest[:, s, :], part[:, s, 1, :], ALU.subtract).then_inc(c4, 1)


def small_heads(nc, k, tag, parts, w_out, out_bias, f_parts, causal):
    H, G, DH = 16, 4, 8
    ROWS = 16 if f_parts is not None else 8
    KS = len(PAIRS) * ROWS
    KT = MR + 3
    with ExitStack() as ctx:
        ph = Phase(nc, ctx, tag)
        wo = ph.sb("wo", [P, P])
        ob = ph.sb("ob", [1, P])
        qp, kp, vp = k.qp, k.kp, k.vp
        nmax = ph.sb("nmax", [P, 4, QT])
        zero = ph.sb("zero", [P, QT])
        mrest = ph.sb("mrest", [P, 2, QT])
        m3 = ph.sb("m3", [P, 2, QT, 3], BF16)
        pT = ph.sb("pT", [P, 2, 4, QT, T])
        rinv = ph.sb("rinv", [P, QT, 4])
        og = ph.sb("og", [P, T])
        o = ph.sb("o", [P, QT, P])
        oT = ph.sb("oT", [P, T])
        s_ps = ph.banks("s", 2)
        st_ps = [ctx.enter_context(nc.psum_tensor(f"{tag}_st{i}", [P, 2, 512], F32)) for i in range(2)]
        o_ps, m_ps = ph.banks("o", 1)[0], ph.banks("m", 1)[0]
        loaded, fixed_in, filled = (ph.sem(s) for s in ("loaded", "fixed_in", "filled"))
        heads_in = [ph.sem(f"heads_in{c}") for c in range(4)]
        s_done, max_done, split_done, mchain, mt_full, mt_read, st_done, exp_done, pv_done, v_in, og_read = (
            ph.sem(s) for s in ("s_done", "max_done", "split_done", "mchain", "mt_full", "mt_read", "st_done",
                                "exp_done", "pv_done", "v_in", "og_read"))
        og_full, to_full, to_read, rinv_ready, ot_full, ot_read, y_full, y_read = (ph.sem(s) for s in (
            "og_full", "to_full", "to_read", "rinv_ready", "ot_full", "ot_read", "y_full", "y_read"))
        block = ctx.enter_context(nc.Block())
        n_fixed = 2 * len(PAIRS) if f_parts is not None else 0
        LOADS = 2 * len(PAIRS) * 16

        def run(eng, step):
            for h in range(H):
                step(0, h, lambda i: i >= 0)
            with eng.Fori(1, B) as b:
                for h in range(H):
                    step(b, h, lambda i: True)
            for h in range(H):
                step(B, h, lambda i: i < 0)

        @block.sync
        def _(sp):
            sp.dma_start(wo[:, :], w_out).then_inc(loaded, 16)
            sp.dma_start(ob[:, :], out_bias).then_inc(loaded, 16)
            if f_parts is not None:
                for c, (i, j) in enumerate(PAIRS):
                    r = slice(ROWS * c + DH, ROWS * c + 2 * DH)
                    sp.dma_start(qp[r, :, :], f_parts[0, i].rearrange("(h r) t -> r h t", r=DH)).then_inc(fixed_in, 16)
                    sp.dma_start(kp[r, :, :], bc(f_parts[1, j, 0:DH].unsqueeze(1), [DH, H, T])).then_inc(fixed_in, 16)

            def load(b, g):
                for c, (i, j) in enumerate(PAIRS):
                    r = slice(ROWS * c, ROWS * c + DH)
                    for dst, s, part in ((qp, 0, i), (kp, 1, j)):
                        sp.dma_start(dst[r, 4 * g:4 * g + 4, :],
                                     parts[s, part, 32 * g:32 * g + 32, bass.ds(b * T, T)]
                                     .rearrange("(h r) t -> r h t", r=DH)).then_inc(heads_in[g], 16)

            for g in range(G):
                load(0, g)
            with sp.Fori(1, B) as b:
                for g in range(G):
                    sp.wait_ge(st_done, (b - 1) * 2 * H + 2 * (4 * g + 4))
                    load(b, g)

        @block.tensor
        def _(pe):
            pe.wait_ge(loaded, 32)
            if n_fixed:
                pe.wait_ge(fixed_in, 16 * n_fixed)

            def misc_free(b, h, after_mt):
                ended = isinstance(b, int) and b == B
                pe.wait_ge(mt_read, B * H + 1 if ended and h else b * H + h + (1 if after_mt else 0))
                pe.wait_ge(to_read, b * G + min((h - 13) // 4, -1 if ended else h) + 5)
                pe.wait_ge(ot_read, b + (1 if h > 10 else 0) + 1)
                pe.wait_ge(y_read, b + (1 if h > 13 else 0) + 1)

            def step(b, h, live):
                def scores(qt):
                    u = QT * h + qt
                    if qt == 0 and h % 4 == 0:
                        pe.wait_ge(heads_in[h // 4], (b + 1) * LOADS)
                    pe.wait_ge(max_done, b * H * QT + u + 1)
                    n = (qt + 1) * P if causal else T
                    last = pe.matmul(s_ps[u % 2][:, 0:n], qp[0:MR, h, qt * P:(qt + 1) * P], kp[0:MR, h, 0:n],
                                     start=True, stop=not causal)
                    if causal:
                        last = pe.matmul(s_ps[u % 2][:, n - P:n], k.ident_bf[:, :], k.later[:, :],
                                         start=False, stop=True)
                    last.then_inc(s_done, 1)

                def maxima(i):
                    pe.wait_ge(split_done, b * H + i + 1)
                    misc_free(b, h, False)
                    for qt in range(QT):
                        last = pe.matmul(m_ps[MR:MR + 3, qt * P:(qt + 1) * P], m3[:, i % 2, qt, :], k.ident_bf[:, :],
                                         start=True, stop=True)
                    last.then_inc(mt_full, 1)

                def turned_scores(i, pair):
                    if pair == 0:
                        pe.wait_ge(mt_read, b * H + i + 2)
                    pe.wait_ge(exp_done, b * 2 * H + 2 * i + pair + 1)
                    for kt in (2 * pair, 2 * pair + 1):
                        q0 = kt * P if causal else 0
                        out = st_ps[pair][:, kt % 2, :]
                        last = pe.matmul(out[:, q0:T], kp[:, i % H, kt * P:(kt + 1) * P], qp[:, i % H, q0:T],
                                         start=True, stop=not causal)
                        if causal:
                            last = pe.matmul(out[:, q0:q0 + P], k.later[:, :], k.ident_bf[:, :], start=False, stop=True)
                    last.then_inc(st_done, 1)

                def values(i):
                    g, kt = i // 4, i % 4
                    pe.wait_ge(exp_done, b * 2 * H + 2 * (4 * g + 3) + kt // 2 + 3)
                    if kt == 0:
                        pe.wait_ge(v_in, b * G + g + 1)
                        pe.wait_ge(og_read, b * G + g + 1)
                    q0 = kt * P if causal else 0
                    for j in range(4):
                        last = pe.matmul(o_ps[32 * j:32 * j + 32, q0:T], vp[:, g % 4, kt, j, :],
                                         pT[:, g % 2, j, kt, q0:T], start=(kt == 0), stop=(kt == QT - 1),
                                         skip_group_check=True)
                    if kt == QT - 1:
                        last.then_inc(pv_done, 1)

                def turn_o(g):
                    pe.wait_ge(og_read, b * G + g + 2)
                    misc_free(b, h, True)
                    for qt in range(QT):
                        last = pe.transpose(m_ps[:, qt * P:(qt + 1) * P], og[:, qt * P:(qt + 1) * P], k.ident[:, :])
                    last.then_inc(to_full, 1)

                new = live(0)
                if new:
                    scores(0)
                    scores(1)
                if live(h - 3):
                    turned_scores(h - 3, 0)
                if new:
                    scores(2)
                if live(h - 7):
                    values(h - 7)
                if new:
                    scores(3)
                if live(h - 1):
                    maxima(h - 1)
                if live(h - 3):
                    turned_scores(h - 3, 1)
                if h % 4 == 0 and live(h - 12):
                    turn_o((h - 12) // 4)
                if h == 10 and live(-1):
                    pe.wait_ge(to_read, b * G + 4)
                    misc_free(b, h, True)
                    for qt in range(QT):
                        last = pe.transpose(m_ps[:, qt * P:(qt + 1) * P], o[:, qt, :], k.ident[:, :])
                    last.then_inc(ot_full, 1)
                if h == 13 and live(-1):
                    pe.wait_ge(ot_read, b + 2)
                    misc_free(b, h, True)
                    for qt in range(QT):
                        out = m_ps[:, qt * P:(qt + 1) * P]
                        pe.matmul(out, oT[:, qt * P:(qt + 1) * P], wo[:, :], start=True, stop=False)
                        last = pe.matmul(out, k.ones[0:1, :], ob[:, :], start=False, stop=True)
                    last.then_inc(y_full, 1)

            run(pe, step)

        @block.scalar
        def _(act):
            act.sem_inc(exp_done, 2)
            act.sem_inc(mt_read, 1)

            def step(b, h, live):
                def exponentials(i, pair):
                    g = i // 4
                    act.wait_ge(st_done, b * 2 * H + 2 * i + pair + 1)
                    if pair == 0 and i % 4 == 0:
                        act.wait_ge(pv_done, b * G + g + 1)
                    if causal:
                        for kt in (2 * pair, 2 * pair + 1):
                            last = act.activation(pT[:, g % 2, i % 4, kt, kt * P:T], st_ps[pair][:, kt % 2, kt * P:T],
                                                  ACT.Exp)
                    else:
                        last = act.activation(pT[:, g % 2, i % 4, 2 * pair:2 * pair + 2, :], st_ps[pair][:, :, :],
                                              ACT.Exp)
                    last.then_inc(exp_done, 1)

                if live(h - 3):
                    exponentials(h - 3, 0)
                if live(h - 1):
                    i = h - 1
                    act.wait_ge(mt_full, b * H + i + 1)
                    act.copy(qp[MR:MR + 3, i % H, :], m_ps[MR:MR + 3, :]).then_inc(mt_read, 1)
                if live(h - 3):
                    exponentials(h - 3, 1)
                if h == 10 and live(-1):
                    act.wait_ge(ot_full, b)
                    act.copy(oT[:, :], m_ps[:, :]).then_inc(ot_read, 1)

            run(act, step)

        @block.gpsimd
        def _(pool):
            pool.memset(zero[:, :], 0.0).then_inc(filled, 1)
            pool.wait_ge(filled, 1)

            def step(b, h, live):
                if live(0):
                    pool.wait_ge(max_done, b * H * QT + QT * (h + 1) + 2)
                    if not (isinstance(b, int) and b == 0 and h < 2):
                        pool.wait_ge(mt_full, b * H + h - 1)
                    nm, rest, m = nmax[:, h % 4, :], mrest[:, h % 2, :], m3[:, h % 2, :, :]
                    c = b * 3 * H + 3 * h
                    pool.tensor_tensor(m[:, :, 0], nm, zero[:, :], ALU.add).then_inc(mchain, 1)
                    pool.wait_ge(mchain, c + 1)
                    pool.tensor_tensor(rest, nm, m[:, :, 0], ALU.subtract).then_inc(mchain, 1)
                    pool.wait_ge(mchain, c + 2)
                    pool.tensor_tensor(m[:, :, 1], rest, zero[:, :], ALU.add).then_inc(mchain, 1)
                    pool.wait_ge(mchain, c + 3)
                    pool.tensor_tensor(m[:, :, 2], rest, m[:, :, 1], ALU.subtract).then_inc(split_done, 1)

            run(pool, step)

        @block.vector
        def _(v):
            v.sem_inc(max_done, 2)
            v.sem_inc(pv_done, 2)
            v.sem_inc(og_read, 1)
            v.sem_inc(to_read, 4)
            v.sem_inc(ot_read, 2)
            v.sem_inc(y_read, 2)

            def step(b, h, live):
                def row_max(qt):
                    u = QT * h + qt
                    n = (qt + 1) * P if causal else T
                    v.wait_ge(s_done, b * H * QT + u + 1)
                    if qt == 0:
                        if not (isinstance(b, int) and b == 0 and h < 4):
                            v.wait_ge(split_done, b * H + h - 3)
                    v.tensor_reduce(nmax[:, h % 4, qt:qt + 1], s_ps[u % 2][:, 0:n], AX.X, ALU.max, negate=True)\
                        .then_inc(max_done, 1)

                if live(0):
                    row_max(0)
                    row_max(1)
                if h % 4 == 3 and live(h - 11):
                    g = (h - 11) // 4
                    v.wait_ge(pv_done, b * G + g + 3)
                    v.tensor_copy(og[:, :], o_ps[:, :]).then_inc(og_read, 1)
                if h % 4 == 1 and live(0):
                    g = h // 4
                    if not (isinstance(b, int) and b == 0):
                        v.wait_ge(pv_done, b * G + g - G + 3)
                    v.tensor_scalar(vp[:, g, :, :, 0:DH], k.v[:, bass.ds(b * QT, QT), 32 * g:32 * g + 32]
                                    .rearrange("p t (j d) -> p t j d", j=4), 1.0, None, ALU.mult).then_inc(v_in, 1)
                if h % 4 == 1 and live(h - 13):
                    g = (h - 13) // 4
                    v.wait_ge(to_full, b * G + g + 1)
                    w = m_ps[:, :].rearrange("p (t h d) -> p t h d", t=QT, h=4)
                    v.reciprocal(rinv[:, :, :], w[:, :, :, DH]).then_inc(rinv_ready, 1)
                    v.wait_ge(rinv_ready, b * G + g + 1)
                    for qt in range(QT):
                        c = 32 * (g % 4)
                        ins = v.tensor_tensor(o[:, qt, c:c + 32].rearrange("p (h d) -> p h d", h=4),
                                              w[:, qt, :, 0:DH], bc(rinv[:, qt, :].unsqueeze(2), [P, 4, DH]), ALU.mult)
                    ins.then_inc(to_read, 1)
                if h == 14 and live(-1):
                    v.wait_ge(y_full, b)
                    xs = k.x[:, bass.ds((b - 1) * QT, QT), :]
                    v.tensor_tensor(xs, m_ps[:, :].rearrange("p (t d) -> p t d", t=QT), xs, ALU.add).then_inc(y_read, 1)
                if live(0):
                    row_max(2)
                    row_max(3)

            run(v, step)


def token_logits(nc, k, tag, w_dram, width, bias_dram=None):
    per_bank = min(512 // width, NT)
    n_banks = NT // per_bank
    with ExitStack() as ctx:
        ph = Phase(nc, ctx, tag)
        w = ph.sb("w", [P, width])
        bias = ph.sb("bias", [1, width])
        ps = ph.banks("ps", n_banks)
        loaded, filled, copied = (ph.sem(s) for s in ("loaded", "filled", "copied"))
        block = ctx.enter_context(nc.Block())
        n_loads = 2 if bias_dram is not None else 1

        @block.sync
        def _(sp):
            sp.dma_start(w[:, :], w_dram).then_inc(loaded, 16)
            if bias_dram is not None:
                sp.dma_start(bias[:, :], bias_dram).then_inc(loaded, 16)

        @block.tensor
        def _(pe):
            pe.wait_ge(loaded, 16 * n_loads)
            for i in range(NT):
                c = (i % per_bank) * width
                out = ps[i // per_bank][:, c:c + width]
                last = pe.matmul(out, k.xnT[:, i * P:(i + 1) * P], w[:, :], start=True, stop=bias_dram is None)
                if bias_dram is not None:
                    last = pe.matmul(out, k.ones[0:1, :], bias[:, :], start=False, stop=True)
                if i % per_bank == per_bank - 1:
                    last.then_inc(filled, 1)

        @block.scalar
        def _(act):
            for j in range(n_banks):
                act.wait_ge(filled, j + 1)
                act.copy(k.logits[:, j * per_bank * width:(j + 1) * per_bank * width],
                         ps[j][:, 0:per_bank * width]).then_inc(copied, 1)
            act.wait_ge(copied, n_banks)


def top8_slots(nc, k, tag, gate_up, down):
    E = 64
    M = NT * E
    with ExitStack() as ctx:
        ph = Phase(nc, ctx, tag)
        best = ph.sb("best", [P, NT, 8])
        rest = ph.sb("rest", [P, NT, E])
        chosen = ph.sb("chosen", [P, NT, E])
        chosen_bf = ph.sb("chosen_bf", [P, NT, E], BF16)
        before = ph.sb("before", [P, NT, E], BF16)
        ex = ph.sb("ex", [P, NT, E])
        tot = ph.sb("tot", [P, NT])
        rtot = ph.sb("rtot", [P, NT])
        ps = ph.banks("ps", 2)
        chain, shifted, exp_done, before_ready, counted = (ph.sem(s) for s in (
            "chain", "shifted", "exp_done", "before_ready", "counted"))
        lg = k.logits[:, 0:M].rearrange("p (t e) -> p t e", e=E)
        block = ctx.enter_context(nc.Block())

        @block.sync
        def _(sp):
            with sp.Fori(0, 4) as i:
                sp.dma_start(k.w_gate_up[:, bass.ds(4 * i, 4), :, :],
                             gate_up[bass.ds(4 * i, 4)].rearrange("g p e f -> p g e f")).then_inc(k.weights_in, 16)
                sp.dma_start(k.w_down[:, bass.ds(4 * i, 4), :, :],
                             down[bass.ds(4 * i, 4)].rearrange("g p e f -> p g e f")).then_inc(k.weights_in, 16)

        @block.vector
        def _(v):
            done = [0]

            def link(ins):
                done[0] += 1
                ins.then_inc(chain, 1)

            def settle():
                v.wait_ge(chain, done[0])

            for i in range(NT):
                link(v.max(best[:, i, :], lg[:, i, :]))
            settle()
            v.tensor_tensor(ex[:, :, :], lg, bc(best[:, :, 0:1], [P, NT, E]), ALU.subtract).then_inc(shifted, 1)
            for i in range(NT):
                link(v.match_replace(rest[:, i, :], best[:, i, :], lg[:, i, :], -BIG))
            settle()
            link(v.tensor_tensor(chosen[:, :, :], rest[:, :, :], lg, ALU.not_equal))
            settle()
            link(v.tensor_copy(chosen_bf[:, :, :], chosen[:, :, :]))
            link(v.memset(before[:, 0, :], 0.0))
            settle()
            for i in range(1, NT):
                link(v.tensor_tensor(before[:, i, :], before[:, i - 1, :], chosen_bf[:, i - 1, :], ALU.add))
                settle()
            v.sem_inc(before_ready, 1)
            v.wait_ge(exp_done, 1)
            link(v.tensor_tensor(ex[:, :, :], ex[:, :, :], chosen[:, :, :], ALU.mult))
            settle()
            link(v.tensor_reduce(tot[:, :], ex[:, :, :], AX.X, ALU.add))
            settle()
            link(v.reciprocal(rtot[:, :], tot[:, :]))
            settle()
            link(v.tensor_tensor(k.weight[:, :, :], ex[:, :, :], bc(rtot[:, :].unsqueeze(2), [P, NT, E]), ALU.mult))
            link(v.tensor_scalar(chosen[:, :, :], chosen[:, :, :], -4096.0, 4096.0, ALU.mult, ALU.add))
            settle()
            for j in range(2):
                v.wait_ge(counted, j + 1)
                link(v.tensor_tensor(k.place[:, 8 * j:8 * j + 8, :], ps[j][:, :].rearrange("p (t e) -> p t e", e=E),
                                     chosen[:, 8 * j:8 * j + 8, :], ALU.add))
            settle()

        @block.scalar
        def _(act):
            act.wait_ge(shifted, 1)
            act.activation(ex[:, :, :], ex[:, :, :], ACT.Exp).then_inc(exp_done, 1)

        @block.tensor
        def _(pe):
            pe.wait_ge(before_ready, 1)
            for i in range(NT):
                out = ps[i // 8][:, (i % 8) * E:(i % 8 + 1) * E]
                pe.matmul(out, k.earlier[:, :], chosen_bf[:, i, :], start=True, stop=False)
                last = pe.matmul(out, k.ones_bf[:, :], before[:, i, :], start=False, stop=True)
                if i % 8 == 7:
                    last.then_inc(counted, 1)


def slot_dispatch(nc, k, tag):
    E, C = 64, 32
    with ExitStack() as ctx:
        ph = Phase(nc, ctx, tag)
        xs = ph.sb("xs", [P, 2, P])
        hot = ph.sb("hot", [P, 2, E, C])
        zeros = ph.sb("zeros", [P, 512], BF16)
        ps = ph.banks("ps", 4)
        zeroed, ready, used, copied = (ph.sem(s) for s in ("zeroed", "ready", "used", "copied"))
        filled = ph.sem("filled")
        block = ctx.enter_context(nc.Block())

        @block.vector
        def _(v):
            v.memset(zeros[:, :], 0.0).then_inc(zeroed, 1)
            v.sem_inc(used, 2)
            with v.Fori(0, NT // 2) as i:
                for s in range(2):
                    v.wait_ge(used, 2 * i + s + 1)
                    v.tensor_copy(xs[:, s, :], k.xn[:, bass.ds(2 * i + s, 1), :].rearrange("p a d -> p (a d)"))
                    v.tensor_tensor(hot[:, s, :, :],
                                    bc(k.place[:, bass.ds(2 * i + s, 1), :].rearrange("p a e -> p (a e)").unsqueeze(2), [P, E, C]),
                                    bc(k.iota[:, 0:C].unsqueeze(1), [P, E, C]), ALU.is_equal).then_inc(ready, 1)

        @block.tensor
        def _(pe):
            pe.wait_ge(zeroed, 1)
            for c in range(4):
                pe.matmul(ps[c][:, :], zeros[:, 0:P], zeros[:, :], start=True, stop=False, skip_group_check=True)
            with pe.Fori(0, NT // 2) as i:
                for s in range(2):
                    pe.wait_ge(ready, 2 * i + s + 1)
                    for c in range(4):
                        last = pe.matmul(ps[c][:, :], xs[:, s, :],
                                         hot[:, s, 16 * c:16 * c + 16, :].rearrange("p e c -> p (e c)"),
                                         start=False, stop=False, skip_group_check=True)
                    last.then_inc(used, 1)
            for c in range(4):
                pe.matmul(ps[c][:, :], zeros[:, 0:P], zeros[:, :], start=False, stop=True,
                          skip_group_check=True).then_inc(filled, 1)

        @block.scalar
        def _(act):
            for c in range(4):
                act.wait_ge(filled, c + 1)
                act.copy(k.slots_x[:, c * 512:(c + 1) * 512], ps[c][:, :]).then_inc(copied, 1)
            act.wait_ge(copied, 4)


def slot_experts(nc, k, tag):
    F, GROUPS, S = 96, 16, 4
    with ExitStack() as ctx:
        ph = Phase(nc, ctx, tag)
        sg = ph.sb("sg", [F, S, P])
        h = ph.sb("h", [F, S, P])
        gu_ps, y_ps = ph.banks("gu", S), ph.banks("y", S)
        gu_done, silu_done, h_done, y_done, stored = (ph.sem(s) for s in (
            "gu_done", "silu_done", "h_done", "y_done", "stored"))
        block = ctx.enter_context(nc.Block())

        @block.tensor
        def _(pe):
            pe.wait_ge(k.weights_in, 16 * 8)
            for i in range(GROUPS // S + 1):
                for s in range(S):
                    g = S * i + s
                    if g < GROUPS:
                        if i:
                            pe.wait_ge(h_done, g - S + 1)
                        for f in range(2):
                            for e in range(4):
                                last = pe.matmul(gu_ps[s][0:F, f * P + 32 * e:f * P + 32 * e + 32],
                                                 k.w_gate_up[:, g, e, f * F:(f + 1) * F],
                                                 k.slots_x[:, g * P + 32 * e:g * P + 32 * e + 32], start=True, stop=True)
                        last.then_inc(gu_done, 1)
                    g -= S
                    if g >= 0:
                        pe.wait_ge(h_done, g + 1)
                        if g >= S:
                            pe.wait_ge(stored, g - S + 1)
                        for e in range(4):
                            last = pe.matmul(y_ps[s][32 * e:32 * e + 32, 0:P], h[:, s, 32 * e:32 * e + 32],
                                             k.w_down[:, g, e, :], start=True, stop=True)
                        last.then_inc(y_done, 1)

        @block.scalar
        def _(act):
            for g in range(GROUPS + S):
                if g < GROUPS:
                    act.wait_ge(gu_done, g + 1)
                    if g >= S:
                        act.wait_ge(h_done, g - S + 1)
                    act.activation(sg[:, g % S, :], gu_ps[g % S][0:F, 0:P], ACT.Silu).then_inc(silu_done, 1)
                if g >= S:
                    act.wait_ge(y_done, g - S + 1)
                    act.copy(k.slots_y[:, g - S, :], y_ps[g % S][:, 0:P]).then_inc(stored, 1)
            act.wait_ge(stored, GROUPS)

        @block.vector
        def _(v):
            for g in range(GROUPS):
                v.wait_ge(silu_done, g + 1)
                if g >= S:
                    v.wait_ge(y_done, g - S + 1)
                v.tensor_tensor(h[:, g % S, :], sg[:, g % S, :], gu_ps[g % S][0:F, P:2 * P], ALU.mult).then_inc(h_done, 1)


def slot_combine(nc, k, tag):
    E, C, GROUPS = 64, 32, 16
    with ExitStack() as ctx:
        ph = Phase(nc, ctx, tag)
        hot = ph.sb("hot", [P, 2, E, C])
        share = ph.sb("share", [P, 2, E, C])
        shareT = ph.sb("shareT", [P, 2, GROUPS, P])
        t_ps = ph.banks("t", 4)
        y_ps = ph.banks("y", 2)
        hot_ready, share_ready, turned, copied, summed, added = (
            ph.sem(s) for s in ("hot_ready", "share_ready", "turned", "copied", "summed", "added"))
        block = ctx.enter_context(nc.Block())

        @block.vector
        def _(v):
            v.sem_inc(turned, 8)
            v.sem_inc(summed, 2)
            v.sem_inc(added, 2)

            def shares(t, s):
                v.wait_ge(turned, 4 * t + 4)
                v.tensor_tensor(hot[:, s, :, :],
                                bc(k.place[:, bass.ds(t, 1), :].rearrange("p a e -> p (a e)").unsqueeze(2), [P, E, C]),
                                bc(k.iota[:, 0:C].unsqueeze(1), [P, E, C]), ALU.is_equal).then_inc(hot_ready, 1)
                v.wait_ge(hot_ready, t + 1)
                v.tensor_tensor(share[:, s, :, :], hot[:, s, :, :],
                                bc(k.weight[:, bass.ds(t, 1), :].rearrange("p a e -> p (a e)").unsqueeze(2), [P, E, C]),
                                ALU.mult).then_inc(share_ready, 1)

            def add(t, s):
                v.wait_ge(summed, t + 3)
                xs = k.x[:, bass.ds(t, 1), :].rearrange("p a d -> p (a d)")
                v.tensor_tensor(xs, y_ps[s][:, 0:P], xs, ALU.add).then_inc(added, 1)

            for s in range(2):
                shares(s, s)
            with v.Fori(1, NT // 2) as i:
                for s in range(2):
                    shares(2 * i + s, s)
                    add(2 * i + s - 2, s)
            for s in range(2):
                add(NT - 2 + s, s)

        @block.tensor
        def _(pe):
            def turn(t, s, c):
                if c == 0:
                    pe.wait_ge(share_ready, t + 1)
                sh = share[:, s, :, :].rearrange("p e c -> p (e c)")
                pe.wait_ge(copied, 4 * t + c + 1)
                for g in range(4):
                    last = pe.transpose(t_ps[c][:, g * P:(g + 1) * P], sh[:, (4 * c + g) * P:(4 * c + g + 1) * P],
                                        k.ident[:, :])
                last.then_inc(turned, 1)

            def sums(t, s, c):
                pe.wait_ge(copied, 4 * t + c + 5)
                if c == 0:
                    pe.wait_ge(added, t + 1)
                for g in range(4 * c, 4 * c + 4):
                    last = pe.matmul(y_ps[s][:, 0:P], shareT[:, s, g, :], k.slots_y[:, g, :],
                                     start=(g == 0), stop=(g == GROUPS - 1))
                if c == 3:
                    last.then_inc(summed, 1)

            for c in range(4):
                turn(0, 0, c)
            with pe.Fori(0, NT // 2 - 1) as i:
                for s in range(2):
                    for c in range(4):
                        turn(2 * i + s + 1, 1 - s, c)
                        sums(2 * i + s, s, c)
            for c in range(4):
                turn(NT - 1, 1, c)
                sums(NT - 2, 0, c)
            for c in range(4):
                sums(NT - 1, 1, c)

        @block.scalar
        def _(act):
            act.sem_inc(copied, 4)
            with act.Fori(0, NT // 2) as i:
                for s in range(2):
                    act.wait_ge(summed, 2 * i + s + 1)
                    for c in range(4):
                        act.wait_ge(turned, 8 * i + 4 * s + c + 1 + 8)
                        act.copy(shareT[:, s, 4 * c:4 * c + 4, :].rearrange("p g t -> p (g t)"), t_ps[c][:, :])\
                            .then_inc(copied, 1)


def top2_gates(nc, k, tag, groups, rule, scale_dram=None, capacity=None):
    M = NT * groups
    with ExitStack() as ctx:
        ph = Phase(nc, ctx, tag)
        below = ph.sb("below", [P, M, 8])
        first = ph.sb("first", [P, M, 8])
        second = ph.sb("second", [P, M, 8])
        left = ph.sb("left", [P, M, 8])
        m = ph.sb("m", [P, 2, M])
        e = ph.sb("e", [P, 2, M])
        where = ph.sb("where", [P, M])
        tot = ph.sb("tot", [P, M])
        chain, best_ready, exp_done, scale_in, both_ready, counted = (
            ph.sem(s) for s in ("chain", "best_ready", "exp_done", "scale_in", "both_ready", "counted"))
        if rule == "capacity":
            both = ph.sb("both", [P, NT, 8], BF16)
            before = ph.sb("before", [P, NT, 8], BF16)
            ex = ph.sb("ex", [P, M, 8])
            ps = ph.banks("ps", 1)
        if rule == "sigmoid":
            rscale = ph.sb("rscale", [P, 1])
        lg = k.logits[:, 0:M * 8].rearrange("p (m e) -> p m e", e=8)
        gate = k.gate[:, 0:M * 8].rearrange("p (m e) -> p m e", e=8)
        wide = [P, M, 8]
        iota8 = bc(k.iota[:, 0:8].unsqueeze(1), wide)
        block = ctx.enter_context(nc.Block())

        @block.sync
        def _(sp):
            if rule == "sigmoid":
                sp.dma_start(rscale[:, :], scale_dram).then_inc(scale_in, 16)

        @block.vector
        def _(v):
            done = [0]

            def link(ins):
                done[0] += 1
                ins.then_inc(chain, 1)
                v.wait_ge(chain, done[0])

            def over8(ap):
                return bc(ap.unsqueeze(2), wide)

            def best(src, i, hot):
                link(v.tensor_reduce(m[:, i, :], src, AX.X, ALU.max))
                link(v.tensor_tensor(below[:, :, :], src, over8(m[:, i, :]), ALU.is_lt))
                link(v.scalar_tensor_tensor(below[:, :, :], below[:, :, :], 1024.0, iota8, ALU.mult, ALU.add))
                link(v.tensor_reduce(where[:, :], below[:, :, :], AX.X, ALU.min))
                link(v.tensor_tensor(hot[:, :, :], iota8, over8(where[:, :]), ALU.is_equal))

            best(lg, 0, first)
            link(v.scalar_tensor_tensor(left[:, :, :], first[:, :, :], -BIG, lg, ALU.mult, ALU.add))
            best(left[:, :, :], 1, second)
            if rule == "sigmoid":
                v.sem_inc(best_ready, 1)
                v.wait_ge(exp_done, 1)
                link(v.tensor_scalar(e[:, :, :], e[:, :, :], 1.0, None, ALU.add))
                link(v.reciprocal(e[:, :, :], e[:, :, :]))
                link(v.tensor_tensor(tot[:, :], e[:, 0, :], e[:, 1, :], ALU.add))
                link(v.tensor_scalar(tot[:, :], tot[:, :], 1e-9, None, ALU.max))
                link(v.reciprocal(tot[:, :], tot[:, :]))
                v.wait_ge(scale_in, 16)
                link(v.tensor_scalar(tot[:, :], tot[:, :], rscale[:, 0:1], None, ALU.mult))
                for i in range(2):
                    link(v.tensor_tensor(e[:, i, :], e[:, i, :], tot[:, :], ALU.mult))
            else:
                link(v.tensor_tensor(e[:, 1, :], m[:, 1, :], m[:, 0, :], ALU.subtract))
                if rule == "capacity":
                    link(v.tensor_tensor(ex[:, :, :], lg, over8(m[:, 0, :]), ALU.subtract))
                v.sem_inc(best_ready, 1)
                v.wait_ge(exp_done, 1)
                if rule == "softmax2":
                    link(v.tensor_scalar(tot[:, :], e[:, 1, :], 1.0, None, ALU.add))
                else:
                    link(v.tensor_reduce(tot[:, :], ex[:, :, :], AX.X, ALU.add))
                link(v.reciprocal(e[:, 0, :], tot[:, :]))
                link(v.tensor_tensor(e[:, 1, :], e[:, 1, :], e[:, 0, :], ALU.mult))
            if rule == "capacity":
                link(v.tensor_tensor(both[:, :, :], first[:, :, :], second[:, :, :], ALU.add))
                link(v.memset(before[:, 0, :], 0.0))
                for i in range(1, NT):
                    link(v.tensor_tensor(before[:, i, :], before[:, i - 1, :], both[:, i - 1, :], ALU.add))
                v.sem_inc(both_ready, 1)
            link(v.tensor_tensor(first[:, :, :], first[:, :, :], over8(e[:, 0, :]), ALU.mult))
            link(v.tensor_tensor(second[:, :, :], second[:, :, :], over8(e[:, 1, :]), ALU.mult))
            link(v.tensor_tensor(gate, first[:, :, :], second[:, :, :], ALU.add))
            if rule == "capacity":
                v.wait_ge(counted, 1)
                link(v.tensor_scalar(left[:, :, :], ps[0][:, 0:M * 8].rearrange("p (m e) -> p m e", e=8),
                                     float(capacity), None, ALU.is_lt))
                link(v.tensor_tensor(gate, gate, left[:, :, :], ALU.mult))
                link(v.tensor_reduce(tot[:, :], gate, AX.X, ALU.add))
                link(v.tensor_scalar(tot[:, :], tot[:, :], 1e-6, None, ALU.add))
                link(v.reciprocal(tot[:, :], tot[:, :]))
                link(v.tensor_tensor(gate, gate, over8(tot[:, :]), ALU.mult))

        @block.scalar
        def _(act):
            act.wait_ge(best_ready, 1)
            if rule == "sigmoid":
                act.activation(e[:, :, :], m[:, :, :], ACT.Exp, scale=-1.0).then_inc(exp_done, 1)
            elif rule == "softmax2":
                act.activation(e[:, 1, :], e[:, 1, :], ACT.Exp).then_inc(exp_done, 1)
            else:
                act.activation(ex[:, :, :], ex[:, :, :], ACT.Exp)
                act.activation(e[:, 1, :], e[:, 1, :], ACT.Exp).then_inc(exp_done, 1)

        if rule == "capacity":
            @block.tensor
            def _(pe):
                pe.wait_ge(both_ready, 1)
                for i in range(NT):
                    out = ps[0][:, i * 8:(i + 1) * 8]
                    pe.matmul(out, k.earlier[:, :], both[:, i, :], start=True, stop=False)
                    last = pe.matmul(out, k.ones_bf[:, :], before[:, i, :], start=False, stop=True)
                last.then_inc(counted, 1)


def gated_ffn(nc, k, tag, w0d, w1d, w2d, b0d, b1d, b2d):
    E, C = 8, 4
    STEPS = E * C
    with ExitStack() as ctx:
        ph = Phase(nc, ctx, tag)
        w0 = ph.sb("w0", [P, E, C, P])
        w1 = ph.sb("w1", [P, E, C, P])
        w2 = ph.sb("w2", [P, E, C, P])
        b0 = ph.sb("b0", [P, E * C])
        b1 = ph.sb("b1", [P, E * C])
        b2 = ph.sb("b2", [8, P])
        sg = ph.sb("sg", [P, 2, T])
        hg = ph.sb("hg", [P, 2, T])
        gs = ph.sb("gs", [P, QT, 8])
        gT = ph.sb("gT", [8, T])
        h_ps, g_ps, y_ps, m_ps = (ph.banks(s, 2) for s in ("h", "g", "y", "m"))
        loaded, h_full, g_full, silu_done, hg_done, hg_used, y_full, y_free, gs_ready, gT_full, gT_ready, b_full = (
            ph.sem(s) for s in ("loaded", "h_full", "g_full", "silu_done", "hg_done", "hg_used", "y_full",
                                "y_free", "gs_ready", "gT_full", "gT_ready", "b_full"))
        acc_chain = ph.sem("acc_chain")
        expert_in = [ph.sem(f"expert_in{e}") for e in range(E)]
        block = ctx.enter_context(nc.Block())

        @block.sync
        def _(sp):
            for dst, src in ((b0[:, :], b0d), (b1[:, :], b1d), (b2[:, :], b2d)):
                sp.dma_start(dst, src).then_inc(loaded, 16)
            for e in range(E):
                for w, src in ((w1, w1d), (w0, w0d), (w2, w2d)):
                    sp.dma_start(w[:, e, :, :], src[:, e]).then_inc(expert_in[e], 16)

        @block.tensor
        def _(pe):
            pe.wait_ge(loaded, 16 * 3)
            with pe.Fori(0, B) as t:
                xs = k.xnT[:, bass.ds(t * T, T)]

                def up(n):
                    pe.wait_ge(hg_done, t * STEPS + n + 1)
                    if n % C == 0:
                        pe.wait_ge(expert_in[n // C], 48)
                    pe.matmul(g_ps[n % 2][:, :], w1[:, n // C, n % C, :], xs, start=True, stop=True).then_inc(g_full, 1)
                    pe.matmul(h_ps[n % 2][:, :], w0[:, n // C, n % C, :], xs, start=True, stop=True).then_inc(h_full, 1)

                def down(n):
                    e, c = n // C, n % C
                    pe.wait_ge(hg_done, t * STEPS + n + 3)
                    if c == 0:
                        pe.wait_ge(y_free, t * E + e + 1)
                    for i in range(QT):
                        last = pe.matmul(y_ps[e % 2][:, i * P:(i + 1) * P], hg[:, n % 2, i * P:(i + 1) * P],
                                         w2[:, e, c, :], start=(c == 0 and i == 0), stop=(c == C - 1),
                                         skip_group_check=True)
                    last.then_inc(hg_used, 1)

                for n in range(STEPS + 1):
                    if n < STEPS:
                        up(n)
                    if n >= 1:
                        down(n - 1)
                pe.wait_ge(gs_ready, t + 1)
                for i in range(QT):
                    last = pe.transpose(m_ps[0][0:8, i * P:(i + 1) * P], gs[:, i, :], k.ident[:, :])
                last.then_inc(gT_full, 1)
                pe.wait_ge(gT_ready, t + 1)
                for i in range(QT):
                    last = pe.matmul(m_ps[1][:, i * P:(i + 1) * P], gT[:, i * P:(i + 1) * P], b2[:, :],
                                     start=True, stop=True)
                last.then_inc(b_full, 1)

        @block.scalar
        def _(act):
            act.wait_ge(loaded, 16 * 3)
            with act.Fori(0, B) as t:
                for n in range(STEPS):
                    act.wait_ge(g_full, t * STEPS + n + 1)
                    act.wait_ge(hg_done, t * STEPS + n + 1)
                    act.activation(sg[:, n % 2, :], g_ps[n % 2][:, :], ACT.Silu, bias=b1[:, n:n + 1]).then_inc(silu_done, 1)

        @block.vector
        def _(v):
            v.sem_inc(hg_done, 2)
            v.sem_inc(hg_used, 2)
            v.sem_inc(y_free, 2)
            v.wait_ge(loaded, 16 * 3)
            with v.Fori(0, B) as t:
                v.tensor_copy(gs[:, :, :], k.gate[:, bass.ds(t * QT * 8, QT * 8)].rearrange("p (i e) -> p i e", e=8))\
                    .then_inc(gs_ready, 1)
                v.wait_ge(gs_ready, t + 1)
                xs = k.x[:, bass.ds(t * QT, QT), :]

                def gated(e):
                    v.wait_ge(hg_used, t * STEPS + (e + 1) * C + 2)
                    if e > 0:
                        v.wait_ge(y_free, t * E + e + 2)
                    for i in range(QT):
                        last = v.scalar_tensor_tensor(xs[:, i, :], y_ps[e % 2][:, i * P:(i + 1) * P],
                                                      gs[:, i, e:e + 1], xs[:, i, :], ALU.mult, ALU.add)
                    last.then_inc(y_free, 1)

                for n in range(STEPS + 2):
                    if n < STEPS:
                        v.wait_ge(silu_done, t * STEPS + n + 1)
                        v.wait_ge(h_full, t * STEPS + n + 1)
                        v.wait_ge(hg_used, t * STEPS + n + 1)
                        v.scalar_tensor_tensor(hg[:, n % 2, :], h_ps[n % 2][:, :], b0[:, n:n + 1], sg[:, n % 2, :],
                                               ALU.add, ALU.mult).then_inc(hg_done, 1)
                    if n >= 5 and n % C == 1:
                        gated(n // C - 1)
                v.wait_ge(gT_full, t + 1)
                v.tensor_copy(gT[:, :], m_ps[0][0:8, :]).then_inc(gT_ready, 1)
                v.wait_ge(b_full, t + 1)
                v.wait_ge(y_free, t * E + E + 2)
                v.tensor_tensor(xs, m_ps[1][:, :].rearrange("p (i d) -> p i d", d=P), xs, ALU.add).then_inc(acc_chain, 1)
                v.wait_ge(acc_chain, t + 1)


def selective_scan(nc, k, tag, d):
    S = 16
    NEAR = 99.0
    with ExitStack() as ctx:
        ph = Phase(nc, ctx, tag)
        w_in = ph.sb("w_in", [P, 2 * P])
        w_x = ph.sb("w_x", [P, S + 2 * P])
        w_dt = ph.sb("w_dt", [S, P])
        w_o = ph.sb("w_o", [P, P])
        b_o = ph.sb("b_o", [1, P])
        b_in = ph.sb("b_in", [P, 2])
        b_bc = ph.sb("b_bc", [P, 2])
        b_dl = ph.sb("b_dl", [S, 1])
        b_dt = ph.sb("b_dt", [P, 1])
        dpar = ph.sb("dpar", [P, 1])
        a_log = ph.sb("a_log", [P, S])
        a = ph.sb("a", [P, S])
        a_slow = ph.sb("a_slow", [P, 1])
        xi = ph.sb("xi", [P, T])
        res = ph.sb("res", [P, T])
        dl = ph.sb("dl", [S, T])
        cm = ph.sb("cm", [P, T])
        z = ph.sb("z", [P, T])
        s1 = ph.sb("s1", [P, T])
        s2 = ph.sb("s2", [P, T])
        delta = ph.sb("delta", [P, T])
        u = ph.sb("u", [P, T])
        da = ph.sb("da", [P, S, T])
        da_slow = ph.sb("da_slow", [P, T])
        h = ph.sb("h", [P, S, T])
        y = ph.sb("y", [P, T])
        peak = ph.sb("peak", [P, 1])
        top = ph.sb("top", [1, 1])
        flag = ph.sb("flag", [1, 1], I32)
        state = ph.sb("state", [P, S])
        ps = ph.banks("ps", 8)
        chain, loaded, a_raw, a_ready, in_full, in_read, dl_full, dl_ready, bc_full, dt_full, z_ready, e_ready = (
            ph.sem(s) for s in ("chain", "loaded", "a_raw", "a_ready", "in_full", "in_read", "dl_full", "dl_ready",
                                "bc_full", "dt_full", "z_ready", "e_ready"))
        delta_ready, da_ready, peak_ready, peak_full, y_ready, y_full, x_added, checked, mixed, state_set = (
            ph.sem(s) for s in ("delta_ready", "da_ready", "peak_ready", "peak_full", "y_ready", "y_full", "x_added",
                                "checked", "mixed", "state_set"))
        block = ctx.enter_context(nc.Block())
        loads = [(w_in[:, :], d["w_in"]), (w_x[:, :], d["w_x"]), (w_dt[:, :], d["w_dt"]), (w_o[:, :], d["w_o"]),
                 (b_o[:, :], d["b_o"]), (b_in[:, :], d["b_in"]), (b_bc[:, :], d["b_bc"]), (b_dl[:, :], d["b_dl"]),
                 (b_dt[:, :], d["b_dt"]), (dpar[:, :], d["dpar"]), (a_log[:, :], d["a_log"])]

        @block.sync
        def _(sp):
            for dst, src in loads:
                sp.dma_start(dst, src).then_inc(loaded, 16)

        @block.tensor
        def _(pe):
            pe.wait_ge(loaded, 16 * len(loads))
            with pe.Fori(0, B) as b:
                xs = k.xnT[:, bass.ds(b * T, T)]
                for i in range(2):
                    pe.matmul(ps[i][:, :], w_in[:, i * P:(i + 1) * P], xs, start=True, stop=True).then_inc(in_full, 1)
                pe.wait_ge(in_read, 2 * b + 2)
                pe.matmul(ps[2][0:S, :], w_x[:, 0:S], xi[:, :], start=True, stop=True).then_inc(dl_full, 1)
                for i in range(2):
                    last = pe.matmul(ps[3 + i][:, :], w_x[:, S + i * P:S + (i + 1) * P], xi[:, :], start=True, stop=True)
                last.then_inc(bc_full, 1)
                pe.wait_ge(dl_ready, b + 1)
                pe.matmul(ps[5][:, :], w_dt[:, :], dl[:, :], start=True, stop=True).then_inc(dt_full, 1)
                pe.wait_ge(peak_ready, b + 1)
                pe.transpose(ps[6][0:1, 0:P], peak[:, :], k.ident[:, :]).then_inc(peak_full, 1)
                pe.wait_ge(y_ready, b + 1)
                for i in range(QT):
                    out = ps[7][:, i * P:(i + 1) * P]
                    pe.matmul(out, y[:, i * P:(i + 1) * P], w_o[:, :], start=True, stop=False)
                    last = pe.matmul(out, k.ones[0:1, :], b_o[:, :], start=False, stop=True)
                last.then_inc(y_full, 1)
                pe.wait_ge(x_added, b + 1)

        @block.scalar
        def _(act):
            act.wait_ge(a_raw, 1)
            act.activation(a[:, :], a_log[:, :], ACT.Exp).then_inc(a_ready, 1)
            with act.Fori(0, B) as b:
                act.wait_ge(in_full, 2 * b + 1)
                act.activation(xi[:, :], ps[0][:, :], ACT.Silu, bias=b_in[:, 0:1]).then_inc(in_read, 1)
                act.wait_ge(in_full, 2 * b + 2)
                act.activation(res[:, :], ps[1][:, :], ACT.Silu, bias=b_in[:, 1:2]).then_inc(in_read, 1)
                act.wait_ge(z_ready, b + 1)
                act.activation(z[:, :], z[:, :], ACT.Exp).then_inc(e_ready, 1)
                act.wait_ge(delta_ready, b + 1)
                act.activation(da_slow[:, :], delta[:, :], ACT.Exp, scale=a_slow[:, 0:1]).then_inc(da_ready, 1)
                for n in range(S):
                    act.activation(da[:, n, :], delta[:, :], ACT.Exp, scale=a[:, n:n + 1]).then_inc(da_ready, 1)
                act.wait_ge(x_added, b + 1)

        @block.vector
        def _(v):
            v.wait_ge(loaded, 16 * len(loads))
            v.tensor_scalar(a_log[:, :], a_log[:, :], 2.0, -5.0, ALU.min, ALU.max).then_inc(a_raw, 1)
            v.wait_ge(a_ready, 1)
            v.tensor_scalar(a[:, :], a[:, :], -1.0, -5.0, ALU.mult, ALU.max).then_inc(a_raw, 1)
            v.wait_ge(a_raw, 2)
            v.tensor_scalar(a[:, :], a[:, :], -0.01, None, ALU.min).then_inc(a_raw, 1)
            v.wait_ge(a_raw, 3)
            v.tensor_reduce(a_slow[:, :], a[:, :], AX.X, ALU.max).then_inc(a_raw, 1)
            v.wait_ge(a_raw, 4)
            LINKS = 21
            with v.Fori(0, B) as b:
                done = [0]

                def link(ins):
                    done[0] += 1
                    ins.then_inc(chain, 1)
                    v.wait_ge(chain, b * LINKS + done[0])

                v.wait_ge(dl_full, b + 1)
                v.tensor_scalar(dl[:, :], ps[2][0:S, :], b_dl[:, 0:1], None, ALU.add).then_inc(dl_ready, 1)
                v.wait_ge(bc_full, b + 1)
                link(v.tensor_scalar(cm[:, :], ps[4][:, :], b_bc[:, 1:2], None, ALU.add))
                v.wait_ge(dt_full, b + 1)
                v.tensor_scalar(z[:, :], ps[5][:, :], b_dt[:, 0:1], 0.0, ALU.add, ALU.min).then_inc(z_ready, 1)
                v.wait_ge(e_ready, b + 1)
                link(v.tensor_scalar(z[:, :], z[:, :], 0.2, None, ALU.min))
                link(v.tensor_scalar(s1[:, :], z[:, :], 2.0, None, ALU.add))
                link(v.reciprocal(s1[:, :], s1[:, :]))
                link(v.tensor_tensor(s1[:, :], z[:, :], s1[:, :], ALU.mult))
                link(v.tensor_tensor(s2[:, :], s1[:, :], s1[:, :], ALU.mult))
                link(v.tensor_scalar(z[:, :], s2[:, :], 2.0 / 9, 2.0 / 7, ALU.mult, ALU.add))
                for c in (2.0 / 5, 2.0 / 3, 2.0):
                    link(v.tensor_tensor(z[:, :], z[:, :], s2[:, :], ALU.mult))
                    link(v.tensor_scalar(z[:, :], z[:, :], c, None, ALU.add))
                link(v.tensor_tensor(z[:, :], z[:, :], s1[:, :], ALU.mult))
                v.tensor_scalar(delta[:, :], z[:, :], 1e-5, 0.1, ALU.max, ALU.min).then_inc(delta_ready, 1)
                v.wait_ge(delta_ready, b + 1)
                link(v.scalar_tensor_tensor(u[:, :], ps[3][:, :], b_bc[:, 0:1], delta[:, :], ALU.add, ALU.mult))
                link(v.tensor_tensor(u[:, :], u[:, :], xi[:, :], ALU.mult))
                link(v.scalar_tensor_tensor(s1[:, :], u[:, :], -1.0, u[:, :], ALU.mult, ALU.max))
                v.wait_ge(da_ready, b * (S + 1) + 1)
                link(v.tensor_tensor_scan(s2[:, :], da_slow[:, :], s1[:, :], 0.0, ALU.mult, ALU.add))
                v.tensor_reduce(peak[:, :], s2[:, :], AX.X, ALU.max).then_inc(peak_ready, 1)
                for n in range(S):
                    v.wait_ge(da_ready, b * (S + 1) + n + 2)
                    last = v.tensor_tensor_scan(h[:, n, :], da[:, n, :], u[:, :], 0.0, ALU.mult, ALU.add)
                link(last)
                v.wait_ge(peak_full, b + 1)
                link(v.tensor_reduce(top[:, :], ps[6][0:1, 0:P], AX.X, ALU.max))
                v.tensor_scalar(flag[:, :], top[:, :], NEAR, None, ALU.is_lt).then_inc(checked, 1)
                v.wait_ge(checked, b + 1)
                v.memset(state[:, :], 0.0).then_inc(state_set, 1)
                small = v.value_load(flag[0:1, 0:1], min_val=0, max_val=1)
                with v.If(small < 1):
                    v.drain()
                    with v.Fori(0, T) as t:
                        v.tensor_tensor(state[:, :], state[:, :], da[:, :, bass.ds(t, 1)].rearrange("p n a -> p (n a)"),
                                        ALU.mult)
                        v.drain()
                        v.tensor_scalar(state[:, :], state[:, :], u[:, bass.ds(t, 1)], -100.0, ALU.add, ALU.max)
                        v.drain()
                        v.tensor_scalar(state[:, :], state[:, :], 100.0, None, ALU.min)
                        v.drain()
                        v.tensor_copy(h[:, :, bass.ds(t, 1)].rearrange("p n a -> p (n a)"), state[:, :])
                        v.drain()
                link(v.tensor_reduce(s1[:, :], h[:, :, :].rearrange("p n t -> p t n"), AX.X, ALU.add))
                assert done[0] == LINKS
                v.tensor_tensor(s1[:, :], s1[:, :], cm[:, :], ALU.mult).then_inc(mixed, 1)
                v.wait_ge(mixed, 3 * b + 1)
                v.scalar_tensor_tensor(s1[:, :], xi[:, :], dpar[:, 0:1], s1[:, :], ALU.mult, ALU.add).then_inc(mixed, 1)
                v.wait_ge(mixed, 3 * b + 2)
                v.wait_ge(in_read, 2 * b + 2)
                v.tensor_tensor(y[:, :], s1[:, :], res[:, :], ALU.mult).then_inc(y_ready, 1)
                v.wait_ge(y_full, b + 1)
                xs = k.x[:, bass.ds(b * QT, QT), :]
                v.tensor_tensor(xs, ps[7][:, :].rearrange("p (i d) -> p i d", d=P), xs, ALU.add).then_inc(x_added, 1)
                v.sem_inc(mixed, 1)


def shared_ffn(nc, k, tag, wg_d, wd_d):
    E = 8
    with ExitStack() as ctx:
        ph = Phase(nc, ctx, tag)
        wg = ph.sb("wg", [P, 2, P])
        wd = ph.sb("wd", [P, 2, E, P])
        hid = ph.sb("hid", [P, 2, T])
        gs = ph.sb("gs", [P, QT, 8])
        h_ps = ph.banks("h", 2)
        y_ps = ph.banks("y", 4)
        loaded, h_full, h_ready, y_full, y_free, gs_ready, chain = (ph.sem(s) for s in (
            "loaded", "h_full", "h_ready", "y_full", "y_free", "gs_ready", "chain"))
        block = ctx.enter_context(nc.Block())
        Y = 2 * QT

        @block.sync
        def _(sp):
            sp.dma_start(wg[:, :, :], wg_d).then_inc(loaded, 16)
            sp.dma_start(wd[:, :, :, :], wd_d).then_inc(loaded, 16)

        @block.tensor
        def _(pe):
            pe.wait_ge(loaded, 32)
            with pe.Fori(0, B) as t:
                xs = k.xnT[:, bass.ds(t * T, T)]
                for c in range(2):
                    pe.matmul(h_ps[c][:, :], wg[:, c, :], xs, start=True, stop=True).then_inc(h_full, 1)
                pe.wait_ge(h_ready, 2 * t + 2)
                for n in range(Y):
                    i, half = n // 2, n % 2
                    pe.wait_ge(y_free, t * Y + n + 1)
                    for c in range(2):
                        last = pe.matmul(y_ps[n % 4][:, :], hid[:, c, i * P:(i + 1) * P],
                                         wd[:, c, 4 * half:4 * half + 4, :].rearrange("p e d -> p (e d)"),
                                         start=(c == 0), stop=(c == 1))
                    last.then_inc(y_full, 1)

        @block.scalar
        def _(act):
            with act.Fori(0, B) as t:
                for c in range(2):
                    act.wait_ge(h_full, 2 * t + c + 1)
                    act.activation(hid[:, c, :], h_ps[c][:, :], ACT.Silu).then_inc(h_ready, 1)

        @block.vector
        def _(v):
            v.sem_inc(y_free, 4)
            with v.Fori(0, B) as t:
                v.tensor_copy(gs[:, :, :], k.gate[:, bass.ds(t * QT * 8, QT * 8)].rearrange("p (i e) -> p i e", e=8))\
                    .then_inc(gs_ready, 1)
                v.wait_ge(gs_ready, t + 1)
                xs = k.x[:, bass.ds(t * QT, QT), :]
                for n in range(Y):
                    i, half = n // 2, n % 2
                    v.wait_ge(y_full, t * Y + n + 1)
                    for e in range(4):
                        ins = v.scalar_tensor_tensor(xs[:, i, :], y_ps[n % 4][:, e * P:(e + 1) * P],
                                                     gs[:, i, 4 * half + e:4 * half + e + 1], xs[:, i, :],
                                                     ALU.mult, ALU.add)
                        if e < 3:
                            ins.then_inc(chain, 1)
                            v.wait_ge(chain, (t * Y + n) * 3 + e + 1)
                        else:
                            ins.then_inc(y_free, 1)
                            v.wait_ge(y_free, t * Y + n + 5)


def relative_heads(nc, k, tag, d, band):
    H, DH, C, W = 16, 64, 8, 257
    STEPS, TAIL = 2 * H, 8
    fills = {0: [("q", 0), ("k", 0)] + [("v", i) for i in range(0, 2 * QT, 2)]}
    for c in range(1, C):
        fills.setdefault(4 * c - 4, []).append(("q", c))
        fills[4 * c - 3] = [("k", c)]
    for i in range(QT):
        fills[4 * i + 6] = [("v", 2 * i + 1)]
    order = [f for s in range(STEPS) for f in fills.get(s, [])]
    place = {f: n for n, f in enumerate(order)}
    PER = len(order) // 2
    SPANS = (((0, P), (P, 2 * P)), ((0, 2 * P), (2 * P, 2 * P)))
    with ExitStack() as ctx:
        ph = Phase(nc, ctx, tag)
        wq = ph.sb("wq", [P, C, P])
        wk = ph.sb("wk", [P, C, P])
        wv = ph.sb("wv", [P, 2, 512])
        wo = ph.sb("wo", [P, C, P])
        bq = ph.sb("bq", [P, C])
        bo = ph.sb("bo", [1, P])
        xb = ph.sb("xb", [P, T])
        qT = ph.sb("qT", [P, 2, T])
        kT = ph.sb("kT", [P, 2, T])
        val = ph.sb("val", [P, QT, H * DH])
        rel = ph.sb("rel", [P, 4, QT, 2 * P])
        lg = ph.sb("lg", [P, 4, 512])
        mx = ph.sb("mx", [P, 4, 2])
        nmax = ph.sb("nmax", [P, 4, 2])
        spare = ph.sb("spare", [P, 1])
        pT = ph.sb("pT", [P, 2, 2, 512])
        rsum = ph.sb("rsum", [P, 4, QT])
        rinv = ph.sb("rinv", [P, 2, QT])
        o = ph.sb("o", [P, 2, QT, P])
        oT = ph.sb("oT", [P, 2, T])
        s_ps, t_ps, m_ps = (ph.banks(s, 2) for s in ("s", "t", "m"))
        o_ps, y_ps = ph.banks("o", 1)[0], ph.banks("y", 1)[0]
        loaded, xb_ready, m_full0, m_full1, m_free0, m_free1 = (ph.sem(s) for s in (
            "loaded", "xb_ready", "m_full0", "m_full1", "m_free0", "m_free1"))
        rel_in = [ph.sem(f"rel_in{i}") for i in range(4)]
        s_done, mx_done, max_done, exp_done, t_done, pt_copied, pv_done, o_ready, rinv_ready = (
            ph.sem(s) for s in ("s_done", "mx_done", "max_done", "exp_done", "t_done", "pt_copied", "pv_done",
                                "o_ready", "rinv_ready"))
        to_full, to_read, y_full, y_read, spare_set = (ph.sem(s) for s in (
            "to_full", "to_read", "y_full", "y_read", "spare_set"))
        m_full, m_free = (m_full0, m_full1), (m_free0, m_free1)
        skewed = band[P - 1:P - 1 + B * H * T * W].rearrange("(h q r) -> h q r", q=QT, r=P * W)
        block = ctx.enter_context(nc.Block())

        def run(eng, step):
            for s in range(STEPS):
                step(0, s, lambda i: i >= 0)
            with eng.Fori(1, B) as b:
                for s in range(STEPS):
                    step(b, s, lambda i: True)
            for s in range(TAIL):
                step(B, s, lambda i: i < 0)

        @block.sync
        def _(sp):
            for dst, src in ((wq[:, :, :], d["a3_wq"]), (wk[:, :, :], d["a3_wk"]), (wv[:, :, :], d["a3_wv"]),
                             (bq[:, :], d["a3_bq"]), (wo[:, :, :], d["a3_wo"]), (bo[:, :], d["a3_bo"])):
                sp.dma_start(dst, src).then_inc(loaded, 16)
            with sp.Fori(0, B) as b:
                for h in range(H):
                    sp.wait_ge(mx_done, b * STEPS + 2 * h + 2)
                    sp.dma_start(rel[:, h % 4, :, :], skewed[bass.ds(b * H + h, 1), :, 0:2 * P * P]
                                 .rearrange("h q (t p) -> (h t) q p", p=2 * P)).then_inc(rel_in[h % 4], 16)

        @block.tensor
        def _(pe):
            pe.wait_ge(loaded, 16 * 6)

            def step(b, s, live):
                def fill(kind, i):
                    n = place[(kind, i)]
                    pe.wait_ge(m_free[n % 2], b * PER + n // 2 + 1)
                    pe.wait_ge(to_read, b * C + (s - 1) // 4 + 2)
                    if kind == "v":
                        left, right = xb[:, (i // 2) * P:(i // 2 + 1) * P], wv[:, i % 2, :]
                    else:
                        left, right = (wq if kind == "q" else wk)[:, i, :], xb[:, :]
                    pe.matmul(m_ps[n % 2][:, :], left, right, start=True, stop=True).then_inc(m_full[n % 2], 1)

                def evicted(kind, i):
                    n = place[(kind, i)]
                    pe.wait_ge(m_free[n % 2], b * PER + n // 2 + 2)

                def scores():
                    h = s // 2
                    if s % 4 == 0:
                        evicted("q", h // 2)
                        evicted("k", h // 2)
                    r = slice(64 * (h % 2), 64 * (h % 2) + 64)
                    pe.wait_ge(mx_done, b * STEPS + s + 7)
                    for i, (c0, n) in enumerate(SPANS[s % 2]):
                        q1 = (2 * (s % 2) + i + 1) * P
                        last = pe.matmul(s_ps[s % 2][:, c0:c0 + n], qT[r, h // 2 % 2, q1 - P:q1],
                                         kT[r, h // 2 % 2, q1 - n:q1], start=True, stop=True)
                    last.then_inc(s_done, 1)

                def turn(i):
                    pe.wait_ge(exp_done, b * STEPS + i + 1)
                    pe.wait_ge(pt_copied, b * STEPS + i + 1)
                    for c in range(3 + i % 2):
                        last = pe.transpose(t_ps[i % 2][:, c * P:(c + 1) * P], lg[:, i % 4, c * P:(c + 1) * P],
                                            k.ident[:, :])
                    last.then_inc(t_done, 1)

                def filled_0(s):
                    return sum(place[f] % 2 == 0 for i in range(s + 1) for f in fills.get(i, []))

                def values(h):
                    pe.wait_ge(pt_copied, b * STEPS + 2 * h + 4)
                    pe.wait_ge(o_ready, b * H + h + 1)
                    if h in (0, H // 2):
                        evicted("v", 2 * QT - 2 if h == 0 else 2 * QT - 1)
                    h_ = h % H
                    for qt in range(QT):
                        c0, n = SPANS[qt // 2][qt % 2]
                        for c in range(n // P):
                            last = pe.matmul(o_ps[:, qt * DH:(qt + 1) * DH], pT[:, h % 2, qt // 2, c0 + c * P:c0 + (c + 1) * P],
                                             val[:, qt + 1 - n // P + c, h_ * DH:(h_ + 1) * DH], start=(c == 0),
                                             stop=(c == n // P - 1))
                    last.then_inc(pv_done, 1)

                def turn_out(c):
                    pe.wait_ge(o_ready, b * H + 2 * c + 3)
                    pe.wait_ge(m_free[0], b * PER + 1 + (filled_0(s) if live(0) else 0))
                    for qt in range(QT):
                        last = pe.transpose(m_ps[0][:, qt * P:(qt + 1) * P], o[:, c % 2, qt, :], k.ident[:, :])
                    last.then_inc(to_full, 1)

                def out_products(c):
                    pe.wait_ge(to_read, b * C + c + 4)
                    if c == 0:
                        pe.wait_ge(y_read, b + 1)
                    for qt in range(QT):
                        out = y_ps[:, qt * P:(qt + 1) * P]
                        last = pe.matmul(out, oT[:, c % 2, qt * P:(qt + 1) * P], wo[:, c % C, :], start=(c == 0 and qt == 0),
                                         stop=False, skip_group_check=True)
                    if c % C == C - 1:
                        for qt in range(QT):
                            last = pe.matmul(y_ps[:, qt * P:(qt + 1) * P], k.ones[0:1, :], bo[:, :], start=False,
                                             stop=True, skip_group_check=True)
                        last.then_inc(y_full, 1)

                if live(0):
                    if s == 0:
                        pe.wait_ge(xb_ready, b + 1)
                        for f in fills[0][:-1]:
                            fill(*f)
                    scores()
                if live(s - 2):
                    turn(s - 2)
                if live(0):
                    for f in (fills[0][-1:] if s == 0 else fills.get(s, [])):
                        fill(*f)
                if s % 2 == 0 and live(s - 4):
                    values((s - 4) // 2)
                if s % 4 == 0 and live(s - 8):
                    turn_out((s - 8) // 4)
                if s % 4 == 2 and live(s - 10):
                    out_products((s - 10) // 4)

            run(pe, step)

        @block.scalar
        def _(act):
            act.sem_inc(pt_copied, 2)
            act.sem_inc(to_read, 3)

            def step(b, s, live):
                def keys(c):
                    n = place[("k", c)]
                    act.wait_ge(m_full[n % 2], b * PER + n // 2 + 1)
                    act.copy(kT[:, c % 2, :], m_ps[n % 2][:, :]).then_inc(m_free[n % 2], 1)

                if s == 0 and live(0):
                    keys(0)
                if live(s - 2):
                    i = s - 2
                    n = (3 + i % 2) * P
                    act.wait_ge(t_done, b * STEPS + i + 5)
                    act.copy(pT[:, i // 2 % 2, i % 2, 0:n], t_ps[i % 2][:, 0:n]).then_inc(pt_copied, 1)
                if live(0):
                    act.wait_ge(max_done, b * STEPS + s + 1)
                    for i, (c0, n) in enumerate(SPANS[s % 2]):
                        qt = 2 * (s % 2) + i
                        last = act.activation(lg[:, s % 4, c0:c0 + n], lg[:, s % 4, c0:c0 + n], ACT.Exp,
                                              bias=nmax[:, s % 4, i:i + 1], accum_out=rsum[:, s // 2 % 4, qt:qt + 1])
                    last.then_inc(exp_done, 1)
                    for f in fills.get(s, []):
                        if f[0] == "k" and s > 0:
                            keys(f[1])
                if s % 4 == 0 and live(s - 8):
                    c = (s - 8) // 4
                    act.wait_ge(to_full, b * C + c + 1)
                    act.copy(oT[:, c % 2, :], m_ps[0][:, :]).then_inc(to_read, 1)

            run(act, step)

        @block.vector
        def _(v):
            v.sem_inc(t_done, 4)
            v.sem_inc(mx_done, 8)
            v.sem_inc(m_free0, 1)
            v.sem_inc(m_free1, 1)
            v.sem_inc(o_ready, 1)
            v.sem_inc(y_read, 1)
            v.wait_ge(loaded, 16 * 6)

            def step(b, s, live):
                def evict(kind, i):
                    if kind == "k":
                        return
                    n = place[(kind, i)]
                    v.wait_ge(m_full[n % 2], b * PER + n // 2 + 1)
                    if kind == "q":
                        ins = v.tensor_scalar(qT[:, i % 2, :], m_ps[n % 2][:, :], bq[:, i:i + 1], DH ** -0.5, ALU.add,
                                              ALU.mult)
                    else:
                        ins = v.tensor_copy(val[:, i // 2, (i % 2) * 512:(i % 2 + 1) * 512], m_ps[n % 2][:, :])
                    ins.then_inc(m_free[n % 2], 1)

                if s == 0 and live(0):
                    v.tensor_copy(xb[:, :], k.xnT[:, bass.ds(b * T, T)]).then_inc(xb_ready, 1)
                    for f in fills[0][:-1]:
                        evict(*f)
                if live(0):
                    h = s // 2
                    v.wait_ge(s_done, b * STEPS + s + 1)
                    v.wait_ge(rel_in[h % 4], 16 * (b * (H // 4) + h // 4 + 1))
                    v.wait_ge(t_done, b * STEPS + s + 1)
                    v.memset(spare[:, :], 0.0).then_inc(spare_set, 1)
                    for i, (c0, n) in enumerate(SPANS[s % 2]):
                        last = v.tensor_tensor_reduce(lg[:, s % 4, c0:c0 + n], s_ps[s % 2][:, c0:c0 + n],
                                                      rel[:, h % 4, 2 * (s % 2) + i, 2 * P - n:2 * P], 1.0, -3.0e38,
                                                      ALU.add, ALU.max, mx[:, s % 4, i:i + 1])
                    last.then_inc(mx_done, 1)
                    for f in (fills[0][-1:] if s == 0 else fills.get(s, [])):
                        evict(*f)
                    v.wait_ge(mx_done, b * STEPS + s + 9)
                    v.tensor_scalar(nmax[:, s % 4, :], mx[:, s % 4, :], -1.0, None, ALU.mult).then_inc(max_done, 1)
                if s % 2 == 1 and live(s - 5):
                    h = (s - 5) // 2
                    v.wait_ge(exp_done, b * STEPS + 2 * h + 2)
                    v.reciprocal(rinv[:, h % 2, :], rsum[:, h % 4, :]).then_inc(rinv_ready, 1)
                    v.wait_ge(rinv_ready, b * H + h + 1)
                    v.wait_ge(pv_done, b * H + h + 1)
                    v.tensor_tensor(o[:, h // 2 % 2, :, (h % 2) * DH:(h % 2 + 1) * DH],
                                    o_ps[:, 0:QT * DH].rearrange("p (t e) -> p t e", t=QT),
                                    bc(rinv[:, h % 2, :].unsqueeze(2), [P, QT, DH]), ALU.mult).then_inc(o_ready, 1)
                if s == 7 and live(-1):
                    v.wait_ge(y_full, b)
                    xs = k.x[:, bass.ds((b - 1) * QT, QT), :]
                    v.tensor_tensor(xs, y_ps[:, :].rearrange("p (t d) -> p t d", t=QT), xs, ALU.add).then_inc(y_read, 1)

            run(v, step)


def switch_heads(nc, k, tag, d, band):
    H, E = 8, 8
    RH, RG, NB, W, HOLE = 16, 4, 10, 257, 129
    UNITS = H * QT
    pairs = {-1: [[("v", 0, i), ("v", 0, i + 2)] for i in (0, 1, 4, 5)]}
    for u in range(UNITS + 3):
        h, r = u // QT, u % QT
        hv, hy, y0 = h + 1, (h - 1 if r == 3 else h - 2), (0 if r == 3 else 2 * r + 2)
        pairs[u] = [[f for f in (("v", hv, 2 * r + i), ("y", hy, y0 + i)) if 0 <= f[1] < (H if f[0] == "v" else H - 1)]
                    for i in range(2)]
    pairs[UNITS + 3] = [[("y", H - 1, i), ("y", H - 1, i + 2)] for i in (0, 1, 4, 5)]
    LAST = UNITS + 3

    def is_turned(u):
        return u // QT - 1 if u % QT == 2 and u >= QT else None

    relative = {}
    for g in range(RG):
        relative[8 * g] = ("r", g)
        for j in range(4):
            relative[8 * g + 2 + j] = ("e", 4 * g + j)

    order = []
    for u in range(-1, LAST + 1):
        if u == -1 or u % QT == 0 and u // QT + 1 < H:
            order += [("q", (u + QT) // QT if u >= 0 else 0), ("k", (u + QT) // QT if u >= 0 else 0)]
        order += pairs[u][0]
        if is_turned(u) is not None:
            order += [("t", is_turned(u))]
        for pair in pairs[u][1:]:
            order += pair
        if u in relative:
            order += [relative[u]]
    transfers = sorted([(4 * h - 9, "wv", h) for h in range(H)] + [(4 * h + 2, "wo", h) for h in range(H)] +
                       [(u + 1, "rows", i) for u, (kind, i) in relative.items() if kind == "e"])
    place = {name: n for n, name in enumerate(order)}
    PER = len(order) // 4
    LINKS = 3 * 2 * H * 2 * QT
    with ExitStack() as ctx:
        ph = Phase(nc, ctx, tag)
        wq = ph.sb("wq", [P, H, P])
        wk = ph.sb("wk", [P, H, P])
        wv = ph.sb("wv", [P, 2, 2, 512])
        wo = ph.sb("wo", [P, 2, 2, 512])
        xb = ph.sb("xb", [P, T])
        gs = ph.sb("gs", [P, QT, 2, H, E])
        acc = ph.sb("acc", [P, QT, P])
        qT = ph.sb("qT", [P, 2, T])
        kT = ph.sb("kT", [P, 2, T])
        val = ph.sb("val", [P, 3, QT, P])
        nmax = ph.sb("nmax", [P, 4])
        prob = ph.sb("prob", [P, 2, T])
        pT = ph.sb("pT", [P, 2, QT, T])
        rsum = ph.sb("rsum", [P, 2, QT])
        rinv = ph.sb("rinv", [P, 2, QT])
        o = ph.sb("o", [P, 2, QT, P])
        oT = ph.sb("oT", [P, 2, T])
        wr = ph.sb("wr", [P, RG, P])
        br = ph.sb("br", [P, RG])
        rel = ph.sb("rel", [P, P])
        rT = ph.sb("rT", [P, 2, T])
        rows = ph.sb("rows", [P, 4, QT, P])
        hole = ph.sb("hole", [P, 4, QT, HOLE])
        s_ps = ph.banks("s", 2)
        t_ps, o_ps = ph.banks("t", 1), ph.banks("o", 1)
        m_ps = ph.banks("m", 4)
        m_full = [ph.sem(f"m_full{i}") for i in range(4)]
        m_free = [ph.sem(f"m_free{i}") for i in range(4)]
        loaded, wv_in0, wv_in1, wo_in0, wo_in1, xb_ready, gs_ready, link, v_ready, y_ready = (ph.sem(s) for s in (
            "loaded", "wv_in0", "wv_in1", "wo_in0", "wo_in1", "xb_ready", "gs_ready", "link", "v_ready", "y_ready"))
        s_done, max_done, exp_done, t_done, pt_copied, pv_done, o_ready, rinv_ready, added = (
            ph.sem(s) for s in ("s_done", "max_done", "exp_done", "t_done", "pt_copied", "pv_done", "o_ready",
                                "rinv_ready", "added"))
        wv_in, wo_in = (wv_in0, wv_in1), (wo_in0, wo_in1)
        hole_set, filled = ph.sem("hole_set"), ph.sem("filled")
        written = [ph.sem(f"written{i}") for i in range(4)]
        lead = band[0:P].rearrange("(a w) -> a w", a=1)
        main = band[P:P + B * RH * T * W].rearrange("(h t w) -> h t w", t=T, w=W)
        block = ctx.enter_context(nc.Block())

        @block.sync
        def _(sp):
            for dst, src in ((wq[:, :, :], d["f3_wq"]), (wk[:, :, :], d["f3_wk"]), (wr[:, :, :], d["a3_wr"]),
                             (br[:, :], d["a3_br"]), (rel[:, :], d["a3_rel"])):
                sp.dma_start(dst, src).then_inc(loaded, 16)
            with sp.Fori(0, B) as b:
                for _, kind, i in transfers:
                    if kind == "wv":
                        sp.wait_ge(v_ready, b * H + i + 1)
                        sp.dma_start(wv[:, i % 2, :, :], d["f3_wv"][i]).then_inc(wv_in[i % 2], 16)
                    elif kind == "wo":
                        sp.wait_ge(y_ready, b * H + i + 1)
                        sp.dma_start(wo[:, i % 2, :, :], d["f3_wo"][i]).then_inc(wo_in[i % 2], 16)
                    else:
                        n = place[("e", i)]
                        sp.wait_ge(m_free[n % 4], b * PER + n // 4 + 2)
                        sp.dma_start(main[bass.ds(b * RH + i, 1), :, 0:P].rearrange("h (i p) w -> (h p) i w", p=P),
                                     rows[:, i % 4, :, :]).then_inc(written[i % 4], 16)
            for s in written:
                sp.wait_ge(s, 16 * B * RG + 16)

        @block.gpsimd
        def _(pool):
            pool.memset(hole[:, :, :, :], -1e9).then_inc(hole_set, 1)
            pool.wait_ge(hole_set, 1)
            pool.dma_start(lead, hole[0:1, 0, 0, 0:P]).then_inc(filled, 16)
            for i in range(B * RH // 4):
                pool.wait_ge(v_ready, i + 4)
                pool.dma_start(main[4 * i:4 * i + 4, :, P:W].rearrange("h (i p) w -> p h i w", p=P), hole[:, :, :, :])\
                    .then_inc(filled, 16)
            pool.wait_ge(filled, 16 * (1 + B * RH // 4))

        @block.tensor
        def _(pe):
            pe.wait_ge(loaded, 16 * 5)
            with pe.Fori(0, B) as b:
                def m_open(*name):
                    n = place[name]
                    pe.wait_ge(m_free[n % 4], b * PER + n // 4 + 1)
                    return m_ps[n % 4], m_full[n % 4]

                def m_read(*name):
                    n = place[name]
                    pe.wait_ge(m_free[n % 4], b * PER + n // 4 + 2)

                def queries_keys(h):
                    for kind, w in (("q", wq), ("k", wk)):
                        ps, full = m_open(kind, h)
                        pe.matmul(ps[:, :], w[:, h, :], xb[:, :], start=True, stop=True).then_inc(full, 1)

                def fill(pair):
                    for kind, h, i in pair:
                        ps, full = m_open(kind, h, i)
                        if kind == "v":
                            left, w, w_in = xb[:, (i // 2) * P:(i // 2 + 1) * P], wv, wv_in
                        else:
                            left, w, w_in = oT[:, h % 2, (i // 2) * P:(i // 2 + 1) * P], wo, wo_in
                        if i == 0:
                            pe.wait_ge(w_in[h % 2], 16 * (b * (H // 2) + h // 2 + 1))
                        pe.matmul(ps[:, :], left, w[:, h % 2, i % 2, :], start=True, stop=True).then_inc(full, 1)

                def scores(u):
                    h, qt = u // QT, u % QT
                    if qt == 0:
                        m_read("q", h)
                        m_read("k", h)
                    pe.wait_ge(exp_done, b * UNITS + u + 1)
                    pe.matmul(s_ps[u % 2][:, :], qT[:, h % 2, qt * P:(qt + 1) * P], kT[:, h % 2, :],
                              start=True, stop=True).then_inc(s_done, 1)

                def turn(u):
                    pe.wait_ge(exp_done, b * UNITS + u + 3)
                    pe.wait_ge(pt_copied, b * UNITS + u + 1)
                    for kt in range(QT):
                        last = pe.transpose(t_ps[0][:, kt * P:(kt + 1) * P], prob[:, u % 2, kt * P:(kt + 1) * P],
                                            k.ident[:, :])
                    last.then_inc(t_done, 1)

                def values(h):
                    pe.wait_ge(pt_copied, b * UNITS + QT * (h + 1) + 1)
                    m_read("v", h, 2 * QT - 1)
                    pe.wait_ge(o_ready, b * H + h + 1)
                    for qt in range(QT):
                        for kt in range(QT):
                            last = pe.matmul(o_ps[0][:, qt * P:(qt + 1) * P], pT[:, h % 2, kt, qt * P:(qt + 1) * P],
                                             val[:, h % 3, kt, :], start=(kt == 0), stop=(kt == QT - 1))
                    last.then_inc(pv_done, 1)

                def turn_out(h):
                    pe.wait_ge(o_ready, b * H + h + 2)
                    ps, full = m_open("t", h)
                    for qt in range(QT):
                        last = pe.transpose(ps[:, qt * P:(qt + 1) * P], o[:, h % 2, qt, :], k.ident[:, :])
                    last.then_inc(full, 1)

                def relative_fill(kind, i):
                    if kind == "r":
                        ps, full = m_open("r", i)
                        pe.matmul(ps[:, :], wr[:, i, :], xb[:, :], start=True, stop=True).then_inc(full, 1)
                        return
                    g, r = i // 4, slice(32 * (i % 4), 32 * (i % 4) + NB)
                    if i % 4 == 0:
                        m_read("r", g)
                    ps, full = m_open("e", i)
                    for qt in range(QT):
                        last = pe.matmul(ps[:, qt * P:(qt + 1) * P], rT[r, g % 2, qt * P:(qt + 1) * P], rel[r, :],
                                         start=True, stop=True)
                    last.then_inc(full, 1)

                pe.wait_ge(xb_ready, b + 1)
                queries_keys(0)
                for pair in pairs[-1]:
                    fill(pair)
                for u in range(LAST + 1):
                    if u < UNITS:
                        scores(u)
                    if u % QT == 0 and u // QT + 1 < H:
                        queries_keys(u // QT + 1)
                    if u == LAST or u % QT == 3 and u > QT:
                        m_read("t", u // QT - 1)
                    fill(pairs[u][0])
                    if 1 <= u <= UNITS:
                        turn(u - 1)
                    if u % QT == 1 and u > QT:
                        values(u // QT - 1)
                    if is_turned(u) is not None:
                        turn_out(is_turned(u))
                    for pair in pairs[u][1:]:
                        fill(pair)
                    if u in relative:
                        relative_fill(*relative[u])

        @block.scalar
        def _(act):
            act.sem_inc(exp_done, 2)
            act.sem_inc(pt_copied, 1)
            for s in written:
                act.sem_inc(s, 16)
            act.wait_ge(loaded, 16 * 5)
            with act.Fori(0, B) as b:
                def m_wait(*name):
                    n = place[name]
                    act.wait_ge(m_full[n % 4], b * PER + n // 4 + 1)
                    return m_ps[n % 4], m_free[n % 4]

                def queries_keys(h):
                    ps, free = m_wait("q", h)
                    act.mul(qT[:, h % 2, :], ps[:, :], float(P) ** -0.5).then_inc(free, 1)
                    ps, free = m_wait("k", h)
                    act.copy(kT[:, h % 2, :], ps[:, :]).then_inc(free, 1)

                queries_keys(0)
                for u in range(LAST):
                    if u % QT == 0 and u // QT + 1 < H:
                        queries_keys(u // QT + 1)
                    if 1 <= u <= UNITS:
                        h, qt = (u - 1) // QT, (u - 1) % QT
                        act.wait_ge(t_done, b * UNITS + u + 2)
                        act.copy(pT[:, h % 2, :, qt * P:(qt + 1) * P],
                                 t_ps[0][:, :].rearrange("p (a q) -> p a q", q=P)).then_inc(pt_copied, 1)
                    if u < UNITS:
                        h, qt = u // QT, u % QT
                        act.wait_ge(max_done, b * UNITS + u + 1)
                        act.wait_ge(t_done, b * UNITS + u + 1)
                        act.activation(prob[:, u % 2, :], s_ps[u % 2][:, :], ACT.Exp, bias=nmax[:, u % 4:u % 4 + 1],
                                       accum_out=rsum[:, h % 2, qt:qt + 1]).then_inc(exp_done, 1)
                    if is_turned(u) is not None:
                        h = is_turned(u)
                        ps, free = m_wait("t", h)
                        act.copy(oT[:, h % 2, :], ps[:, :]).then_inc(free, 1)
                    if u in relative:
                        kind, i = relative[u]
                        ps, free = m_wait(kind, i)
                        if kind == "r":
                            act.activation(rT[:, i % 2, :], ps[:, :], ACT.Identity, bias=br[:, i:i + 1]).then_inc(free, 1)
                        else:
                            act.wait_ge(written[i % 4], 16 * (b * RG + i // 4 + 1))
                            act.copy(rows[:, i % 4, :, :].rearrange("p j e -> p (j e)"), ps[:, :]).then_inc(free, 1)

        @block.vector
        def _(v):
            v.sem_inc(t_done, 2)
            v.sem_inc(v_ready, 2)
            v.sem_inc(y_ready, 2)
            v.sem_inc(o_ready, 1)
            for s in m_free:
                v.sem_inc(s, 1)
            with v.Fori(0, B) as b:
                links = [0]

                v.tensor_copy(xb[:, :], k.xnT[:, bass.ds(b * T, T)]).then_inc(xb_ready, 1)
                v.tensor_copy(gs[:, :, :, :, :].rearrange("p i s h e -> p (i s h e)"),
                              k.gate[:, bass.ds(b * QT * 2 * H * E, QT * 2 * H * E)]).then_inc(gs_ready, 1)
                v.wait_ge(gs_ready, 2 * b + 1)
                v.tensor_copy(acc[:, :, :], k.x[:, bass.ds(b * QT, QT), :]).then_inc(gs_ready, 1)
                v.wait_ge(gs_ready, 2 * b + 2)

                def summed(*name):
                    n = place[name]
                    v.wait_ge(m_free[n % 4], b * PER + n // 4 + 2)

                def gather(pair):
                    count = [0] * len(pair)
                    for e in range(4):
                        for j, (kind, h, i) in enumerate(pair):
                            n = place[(kind, h, i)]
                            ps, free = m_ps[n % 4], m_free[n % 4]
                            if kind == "v":
                                out, s = val[:, h % 3, i // 2, :], 0
                            else:
                                out, s = acc[:, i // 2, :], 1
                            g = gs[:, i // 2, s, h, 4 * (i % 2) + e:4 * (i % 2) + e + 1]
                            if e == 0:
                                if i % 2 == 1:
                                    summed(kind, h, i - 1)
                                elif kind == "y" and h >= 1:
                                    summed(kind, h - 1, i + 1)
                                v.wait_ge(m_full[n % 4], b * PER + n // 4 + 1)
                            else:
                                v.wait_ge(link, b * LINKS + count[j])
                            if kind == "v" and i % 2 == 0 and e == 0:
                                ins = v.tensor_scalar(out, ps[:, 0:P], g, None, ALU.mult)
                            else:
                                ins = v.scalar_tensor_tensor(out, ps[:, e * P:(e + 1) * P], g, out, ALU.mult, ALU.add)
                            if e == 3:
                                ins.then_inc(free, 1)
                            else:
                                ins.then_inc(link, 1)
                                links[0] += 1
                                count[j] = links[0]
                    for kind, h, i in pair:
                        if i == 2 * QT - 1:
                            summed(kind, h, i)
                            v.sem_inc(v_ready if kind == "v" else y_ready, 1)

                def normalised(h):
                    v.wait_ge(exp_done, b * UNITS + QT * (h + 1) + 2)
                    v.reciprocal(rinv[:, h % 2, :], rsum[:, h % 2, :]).then_inc(rinv_ready, 1)
                    v.wait_ge(rinv_ready, b * H + h + 1)
                    v.wait_ge(pv_done, b * H + h + 1)
                    v.tensor_tensor(o[:, h % 2, :, :], o_ps[0][:, :].rearrange("p (t e) -> p t e", t=QT),
                                    bc(rinv[:, h % 2, :].unsqueeze(2), [P, QT, P]), ALU.mult).then_inc(o_ready, 1)

                for pair in pairs[-1]:
                    gather(pair)
                for u in range(LAST + 1):
                    if u < UNITS:
                        v.wait_ge(s_done, b * UNITS + u + 1)
                        v.tensor_reduce(nmax[:, u % 4:u % 4 + 1], s_ps[u % 2][:, :], AX.X, ALU.max, negate=True)\
                            .then_inc(max_done, 1)
                    gather(pairs[u][0])
                    if u % QT == 1 and u > QT:
                        normalised(u // QT - 1)
                    for pair in pairs[u][1:]:
                        gather(pair)
                v.tensor_copy(k.x[:, bass.ds(b * QT, QT), :], acc[:, :, :]).then_inc(added, 1)
                v.wait_ge(added, b + 1)


def layer3(nc, k, d):
    token_logits(nc, k, "r3", d["f3_wr"], P)
    top2_gates(nc, k, "g3", 16, "sigmoid", scale_dram=d["f3_scale"])
    band = nc.dram_tensor("band", (P + B * 16 * T * 257,), F32, kind="Internal").ap()
    switch_heads(nc, k, "f3", d, band)
    relative_heads(nc, k, "a3", d, band)


def layer3_layout(a, d):
    f = np.float32
    z = np.zeros((P, 4, 4, 32), f)
    z[..., 0:10] = a["L3_attn_Wr"].reshape(P, 4, 4, 10)
    d["a3_wr"] = z.reshape(P, 4, P)
    z = np.zeros((4, 4, 32), f)
    z[..., 0:10] = a["L3_attn_br"].reshape(4, 4, 10)
    d["a3_br"] = z.reshape(4, P).T
    z = np.zeros((4, 32, P), f)
    z[:, 0:10, :] = a["L3_attn_b_nd"][None, :, ::-1]
    d["a3_rel"] = z.reshape(P, P)
    d["a3_wq"], d["a3_wk"] = (a["L3_attn_" + n].reshape(P, 8, P) for n in ("Wq", "Wk"))
    d["a3_wv"] = a["L3_attn_Wv"].reshape(P, 2, 512)
    d["a3_bq"] = a["L3_attn_bq"].reshape(8, P).T
    d["a3_wo"] = a["L3_attn_Wproj"].reshape(8, P, P).transpose(1, 0, 2)
    d["a3_bo"] = a["L3_attn_bproj"][None]
    d["f3_wr"] = np.concatenate([a["L3_ffn_sel_v_w"], a["L3_ffn_sel_o_w"]]).T
    d["f3_scale"] = np.tile(a["L3_ffn_route_scale"], (P, 1))
    d["f3_wq"], d["f3_wk"] = (a["L3_ffn_" + n].reshape(8, P, P).transpose(2, 0, 1) for n in ("q_w", "k_w"))
    for n, s in (("f3_wv", "v_w"), ("f3_wo", "o_w")):
        d[n] = a["L3_ffn_" + s].reshape(8, 2, 4, P, P).transpose(0, 3, 1, 2, 4).reshape(8, P, 2, 512)




class State:
    pass


def program(nc, d, out):
    with ExitStack() as ctx:
        def sb(name, shape, dtype=F32):
            return ctx.enter_context(nc.sbuf_tensor(name, shape, dtype))

        k = State()
        Phase.counted = []
        k.x = sb("x", [P, NT, P])
        k.xn = sb("xn", [P, NT, P])
        k.xnT = sb("xnT", [P, N])
        k.ident = sb("ident", [P, P])
        k.ident_bf = sb("ident_bf", [P, P], BF16)
        k.ones = sb("ones", [1, P])
        k.ones_bf = sb("ones_bf", [P, P], BF16)
        k.earlier = sb("earlier", [P, P], BF16)
        k.later = sb("later", [P, P], BF16)
        k.iota = sb("iota", [P, 64])
        k.logits = sb("logits", [P, NT * P])

        with ExitStack() as c1:
            ph = Phase(nc, c1, "setup")
            tmp = ph.sb("tmp", [P, 2, P])
            loaded, made = ph.sem("loaded"), ph.sem("made")
            block = c1.enter_context(nc.Block())

            @block.sync
            def _(sp):
                for dst, src in ((k.x[:, :, :], d["x"].rearrange("(t p) d -> p t d", p=P)), (k.ident[:, :], d["ident"]),
                                 (tmp[:, 0, :], d["earlier"]), (tmp[:, 1, :], d["later"]), (k.iota[:, :], d["iota"])):
                    sp.dma_start(dst, src).then_inc(loaded, 16)

            @block.vector
            def _(v):
                v.memset(k.ones[:, :], 1.0).then_inc(made, 1)
                v.memset(k.ones_bf[:, :], 1.0).then_inc(made, 1)
                v.wait_ge(loaded, 80)
                v.tensor_copy(k.ident_bf[:, :], k.ident[:, :]).then_inc(made, 1)
                v.tensor_copy(k.earlier[:, :], tmp[:, 0, :]).then_inc(made, 1)
                v.tensor_copy(k.later[:, :], tmp[:, 1, :]).then_inc(made, 1)
                v.wait_ge(made, 5)

        layer_norm(nc, k, "n0")
        with ExitStack() as c2:
            k.v = c2.enter_context(nc.sbuf_tensor("v0", [P, NT, P], F32))
            head_tiles(nc, c2, k, "t0")
            parts = nc.dram_tensor("parts0", (2, 3, P, N), BF16, kind="Internal").ap()
            split_heads(nc, k, "q0", d["a0_wq"], d["a0_wk"], d["a0_wv"], d["a0_bq"], d["a0_bk"], d["a0_bv"],
                        8 ** -0.5, parts, None)
            small_heads(nc, k, "a0", parts, d["a0_wo"], d["a0_bo"], None, False)
        token_logits(nc, k, "r0", d["f0_wr"], 64)
        with ExitStack() as c2:
            k.weight = c2.enter_context(nc.sbuf_tensor("weight", [P, NT, 64], F32))
            k.place = c2.enter_context(nc.sbuf_tensor("place", [P, NT, 64], F32))
            k.slots_x = c2.enter_context(nc.sbuf_tensor("slots_x", [P, 64 * 32], F32))
            k.slots_y = c2.enter_context(nc.sbuf_tensor("slots_y", [P, 16, P], F32))
            with ExitStack() as c3:
                k.w_gate_up = c3.enter_context(nc.sbuf_tensor("w_gate_up", [P, 16, 4, 192], F32))
                k.w_down = c3.enter_context(nc.sbuf_tensor("w_down", [96, 16, 4, P], F32))
                k.weights_in = Phase(nc, c3, "w0").sem("weights_in")
                top8_slots(nc, k, "p0", d["f0_wgu"], d["f0_wd"])
                slot_dispatch(nc, k, "d0")
                slot_experts(nc, k, "e0")
            slot_combine(nc, k, "c0")
        Phase.retire(nc)
        layer_norm(nc, k, "n1")
        with ExitStack() as c2:
            k.v = c2.enter_context(nc.sbuf_tensor("v1", [P, NT, P], F32))
            head_tiles(nc, c2, k, "t1")
            parts = nc.dram_tensor("parts1", (2, 3, P, N), BF16, kind="Internal").ap()
            f_parts = nc.dram_tensor("f_parts", (2, 3, P, T), BF16, kind="Internal").ap()
            split_heads(nc, k, "q1", d["a1_wq"], d["a1_wk"], d["a1_wv"], d["a1_bz"], d["a1_bz"], d["a1_br"],
                        8 ** -0.5, parts, (d["a1_fa"], d["a1_trig"], f_parts))
            small_heads(nc, k, "a1", parts, d["a1_wo"], d["a1_br"], f_parts, True)
        with ExitStack() as c2:
            k.gate = c2.enter_context(nc.sbuf_tensor("gate1", [P, NT * 8], F32))
            token_logits(nc, k, "r1", d["f1_wr"], 8, d["f1_br"])
            top2_gates(nc, k, "g1", 1, "softmax2")
            gated_ffn(nc, k, "f1", d["f1_w0"], d["f1_w1"], d["f1_w2"], d["f1_b0"], d["f1_b1"], d["f1_b2"])
        Phase.retire(nc)
        layer_norm(nc, k, "n2")
        selective_scan(nc, k, "s2", {n[3:]: a for n, a in d.items() if n.startswith("s2_")})
        with ExitStack() as c2:
            k.gate = c2.enter_context(nc.sbuf_tensor("gate2", [P, NT * 8], F32))
            token_logits(nc, k, "r2", d["f2_wr"], 8)
            top2_gates(nc, k, "g2", 1, "capacity", capacity=N * 5 // 32)
            shared_ffn(nc, k, "f2", d["f2_wg"], d["f2_wd"])
        Phase.retire(nc)
        layer_norm(nc, k, "n3")
        with ExitStack() as c2:
            k.gate = c2.enter_context(nc.sbuf_tensor("gate3", [P, NT * P], F32))
            layer3(nc, k, d)

        with ExitStack() as c1:
            ph = Phase(nc, c1, "store")
            stored = ph.sem("stored")
            block = c1.enter_context(nc.Block())

            @block.sync
            def _(sp):
                sp.dma_start(out.rearrange("b (t p) d -> p (b t) d", p=P), k.x[:, :, :]).then_inc(stored, 16)
                sp.wait_ge(stored, 16)


def laid_out(a):
    def col(v, n):
        return np.ascontiguousarray(v.reshape(n, 128).T)

    d = {}
    f = np.float32
    d["x"] = a["L0_attn_x"].reshape(N, P)
    d["ident"] = np.eye(P, dtype=f)
    d["earlier"] = np.triu(np.ones((P, P), f), 1)
    d["later"] = np.triu(np.full((P, P), -BIG, f), 1)
    d["iota"] = np.tile(np.arange(64, dtype=f), (P, 1))
    w, bias = a["L0_attn_qkv_w"], a["L0_attn_qkv_b"]
    d["a0_wq"], d["a0_wk"], d["a0_wv"] = w[:, 0:128], w[:, 128:256], w[:, 256:384]
    d["a0_bq"], d["a0_bk"] = bias[0:128, None], bias[128:256, None]
    d["a0_bv"], d["a0_bo"] = bias[None, 256:384], a["L0_attn_proj_b"][None]
    d["a0_wo"] = a["L0_attn_proj_w"]
    d["f0_wr"] = a["L0_ffn_gate_w"].T
    gu = np.concatenate([a["L0_ffn_w_gate"], a["L0_ffn_w_up"]], axis=1)
    d["f0_wgu"] = gu.reshape(16, 4, 192, P).transpose(0, 3, 1, 2)
    d["f0_wd"] = a["L0_ffn_w_down"].reshape(16, 4, P, 96).transpose(0, 3, 1, 2)
    w = a["L1_attn_Wqkv"].T
    d["a1_wq"], d["a1_wk"], d["a1_wv"] = w[:, 0:128], w[:, 128:256], w[:, 256:384]
    d["a1_bz"], d["a1_br"] = np.zeros((P, 1), f), np.zeros((1, P), f)
    d["a1_wo"] = a["L1_attn_Wout"].T
    fa = np.zeros((12, 16, 8), f)
    al, be = a["L1_attn_alpha"], a["L1_attn_beta"]
    for r in range(4):
        fa[r, :, r], fa[4 + r, :, r] = al[:, r], be[:, r]
        fa[4 + r, :, 4 + r], fa[8 + r, :, 4 + r] = al[:, r], be[:, r]
    d["a1_fa"] = fa.reshape(12, P)
    ang = (10000.0 ** (-2.0 * np.arange(4) / 8))[:, None] * np.arange(T)[None, :]
    d["a1_trig"] = np.concatenate([np.cos(ang), np.sin(ang), -np.cos(ang)]).astype(f)
    d["f1_wr"], d["f1_br"] = a["L1_ffn_Wg"], a["L1_ffn_bg"][None]
    for n, s in (("f1_w0", "W0"), ("f1_w1", "W1")):
        d[n] = a["L1_ffn_" + s].reshape(8, P, 4, P).transpose(1, 0, 2, 3)
    d["f1_w2"] = a["L1_ffn_W2"].reshape(8, 4, P, P).transpose(2, 0, 1, 3)
    d["f1_b0"], d["f1_b1"] = col(a["L1_ffn_b0"], 32), col(a["L1_ffn_b1"], 32)
    d["f1_b2"] = a["L1_ffn_b2"]
    d["s2_w_in"], d["s2_w_x"] = a["L2_attn_in_proj_w"].T, a["L2_attn_x_proj_w"].T
    d["s2_w_dt"], d["s2_w_o"] = a["L2_attn_dt_proj_w"].T, a["L2_attn_out_proj_w"].T
    d["s2_b_o"], d["s2_b_in"] = a["L2_attn_out_proj_b"][None], col(a["L2_attn_in_proj_b"], 2)
    xb = a["L2_attn_x_proj_b"]
    d["s2_b_dl"], d["s2_b_bc"] = xb[0:16, None], col(xb[16:], 2)
    d["s2_b_dt"], d["s2_dpar"], d["s2_a_log"] = a["L2_attn_dt_proj_b"][:, None], a["L2_attn_D_param"][:, None], a["L2_attn_A_log"]
    d["f2_wr"] = a["L2_ffn_w_router"].T
    d["f2_wg"] = a["L2_ffn_w_gate"].T.reshape(P, 2, P)
    d["f2_wd"] = a["L2_ffn_w_down"].transpose(2, 0, 1).reshape(2, P, 8, P).transpose(1, 0, 2, 3)
    layer3_layout(a, d)
    return {n: np.ascontiguousarray(v) for n, v in d.items()}


def kernel(**inputs):
    import concourse.bacc as bacc
    from concourse.bass_utils import run_bass_kernel_spmd

    nc = bacc.Bacc("TRN2", target_bir_lowering=False, num_devices=1)
    nc.disable_value_cache = True
    arrays = laid_out({n: np.asarray(v) for n, v in inputs.items()})
    aps = {n: nc.dram_tensor(f"{n}_in", v.shape, F32, kind="ExternalInput").ap() for n, v in arrays.items()}
    out = nc.dram_tensor("out_dram", (B, T, P), F32, kind="ExternalOutput").ap()
    program(nc, aps, out)
    r = run_bass_kernel_spmd(nc, [{f"{n}_in": v for n, v in arrays.items()}], core_ids=[0])
    return r.results[0]["out_dram"]
```
